# Optimizing a Trainium2 kernel written in Bass

```python
import numpy as np
import jax
import jax.numpy as jnp

def _softmax(x, axis=-1):
    return jax.nn.softmax(x, axis=axis)

def _gelu(x):
    return jax.nn.gelu(x, approximate=True)

def _silu(x):
    return jax.nn.silu(x)

def _sigmoid(x):
    return jax.nn.sigmoid(x)

def _layernorm(x, axis=-1, eps=1e-05):
    m = jnp.mean(x, axis=axis, keepdims=True)
    v = jnp.var(x, axis=axis, keepdims=True)
    return (x - m) / jnp.sqrt(v + eps)

def _scatter_add(tgt, idx, src, axis=0):
    return tgt.at[idx].add(src)

def _segment_sum(src, seg, n):
    return jax.ops.segment_sum(src, seg, n)
kernel_name = 'mk_sandwich_d1_jaxref_r8_086bde'

def setup_inputs(seed: int=0):
    np.random.seed(seed)
    _w = jnp.asarray

    def _L0_attn_setup():
        import jax, jax.numpy as jnp
        import numpy as np
        D_MODEL = 128
        D_STATE = 64
        EXPAND = 2
        N_HEADS = 32
        NGROUPS = 1
        CHUNK = 128
        R = 2
        D_INNER = EXPAND * D_MODEL
        HEAD_DIM = D_INNER // N_HEADS
        BC = NGROUPS * D_STATE
        D_PROJ = D_INNER + D_INNER * R + BC * R + BC + 2 * N_HEADS + D_STATE // 2
        SCALE = (D_STATE * R) ** (-0.5)
        EPS = 1e-06
        NEG = -1e+30

        def _rms(x):
            return x * jax.lax.rsqrt(jnp.mean(x * x, axis=-1, keepdims=True) + EPS)

        def _rope(x, cos, sin):
            h = x.shape[-1] // 2
            x1, x2 = (x[..., :h], x[..., h:])
            return jnp.concatenate([x1 * cos - x2 * sin, x1 * sin + x2 * cos], axis=-1)
        key = jax.random.key(seed)
        ks = jax.random.split(key, 7)
        B, T = (2, 256)
        return {'x': jax.random.normal(ks[0], (B, T, D_MODEL), jnp.float32), 'W_in': jax.random.normal(ks[1], (D_MODEL, D_PROJ), jnp.float32) * 0.02, 'A_log': jax.random.normal(ks[2], (N_HEADS,), jnp.float32) * 0.5, 'dt_bias': jax.random.normal(ks[3], (N_HEADS,), jnp.float32) * 0.5, 'B_norm_bias': 1.0 + 0.1 * jax.random.normal(ks[4], (NGROUPS, D_STATE), jnp.float32), 'C_norm_bias': 1.0 + 0.1 * jax.random.normal(ks[5], (NGROUPS, D_STATE), jnp.float32), 'W_out': jax.random.normal(ks[6], (D_INNER, D_MODEL), jnp.float32) * 0.02}
    _L0_attn_in = _L0_attn_setup()

    def _L0_ffn_setup():
        import jax, jax.numpy as jnp
        import numpy as np
        DIM = 128

        def _reference_tuple_inner(x, W_r, W_k, W_v, mu_r, mu_k):
            B, T, C = x.shape
            x_prev = jnp.concatenate([jnp.zeros((B, 1, C), x.dtype), x[:, :-1, :]], axis=1)
            xr = mu_r * x + (1.0 - mu_r) * x_prev
            xk = mu_k * x + (1.0 - mu_k) * x_prev
            r = jax.nn.sigmoid(jnp.einsum('btc,dc->btd', xr, W_r))
            k = jnp.einsum('btc,dc->btd', xk, W_k)
            k_act = jnp.square(jax.nn.relu(k))
            out = r * jnp.einsum('btc,dc->btd', k_act, W_v)
            new_state = x[:, -1, :]
            return (out, new_state)
        key = jax.random.key(seed)
        ks = jax.random.split(key, 6)
        B, T, C = (8, 256, DIM)
        x = jax.random.normal(ks[0], (B, T, C), dtype=jnp.float32)
        s = 1.0 / np.sqrt(C)
        W_r = jax.random.uniform(ks[1], (C, C), jnp.float32, -s, s)
        W_k = jax.random.uniform(ks[2], (C, C), jnp.float32, -s, s)
        W_v = jax.random.uniform(ks[3], (C, C), jnp.float32, -s, s)
        mu_r = jax.random.uniform(ks[4], (C,), jnp.float32)
        mu_k = jax.random.uniform(ks[5], (C,), jnp.float32)
        return {'x': x, 'W_r': W_r, 'W_k': W_k, 'W_v': W_v, 'mu_r': mu_r, 'mu_k': mu_k}
    _L0_ffn_in = _L0_ffn_setup()
    _d = {'L0_attn_x': _L0_attn_in['x'], 'L0_attn_W_in': _L0_attn_in['W_in'], 'L0_attn_A_log': _L0_attn_in['A_log'], 'L0_attn_dt_bias': _L0_attn_in['dt_bias'], 'L0_attn_B_norm_bias': _L0_attn_in['B_norm_bias'], 'L0_attn_C_norm_bias': _L0_attn_in['C_norm_bias'], 'L0_attn_W_out': _L0_attn_in['W_out'], 'L0_ffn_W_r': _L0_ffn_in['W_r'], 'L0_ffn_W_k': _L0_ffn_in['W_k'], 'L0_ffn_W_v': _L0_ffn_in['W_v'], 'L0_ffn_mu_r': _L0_ffn_in['mu_r'], 'L0_ffn_mu_k': _L0_ffn_in['mu_k']}
    _x0 = _d['L0_attn_x']
    _d['L0_attn_x'] = jax.random.normal(jax.random.fold_in(jax.random.key(seed), 1), (8, 512, 128), dtype=_x0.dtype)
    del _x0
    return _d

def reference(L0_attn_x, L0_attn_W_in, L0_attn_A_log, L0_attn_dt_bias, L0_attn_B_norm_bias, L0_attn_C_norm_bias, L0_attn_W_out, L0_ffn_W_r, L0_ffn_W_k, L0_ffn_W_v, L0_ffn_mu_r, L0_ffn_mu_k):

    def _L0_attn_ref(x, W_in, A_log, dt_bias, B_norm_bias, C_norm_bias, W_out):
        import jax, jax.numpy as jnp
        import numpy as np
        D_MODEL = 128
        D_STATE = 64
        EXPAND = 2
        N_HEADS = 32
        NGROUPS = 1
        CHUNK = 128
        R = 2
        D_INNER = EXPAND * D_MODEL
        HEAD_DIM = D_INNER // N_HEADS
        BC = NGROUPS * D_STATE
        D_PROJ = D_INNER + D_INNER * R + BC * R + BC + 2 * N_HEADS + D_STATE // 2
        SCALE = (D_STATE * R) ** (-0.5)
        EPS = 1e-06
        NEG = -1e+30

        def _rms(x):
            return x * jax.lax.rsqrt(jnp.mean(x * x, axis=-1, keepdims=True) + EPS)

        def _rope(x, cos, sin):
            h = x.shape[-1] // 2
            x1, x2 = (x[..., :h], x[..., h:])
            return jnp.concatenate([x1 * cos - x2 * sin, x1 * sin + x2 * cos], axis=-1)
        B, T, _ = x.shape
        L = CHUNK
        NC = T // L
        G, H, N, P = (NGROUPS, N_HEADS, D_STATE, HEAD_DIM)
        E = H // G
        proj = x @ W_in
        o = 0
        z = proj[..., :D_INNER]
        o = D_INNER
        x_raw = proj[..., o:o + D_INNER * R]
        o += D_INNER * R
        Bm = proj[..., o:o + BC * R]
        o += BC * R
        Cm = proj[..., o:o + BC]
        o += BC
        dt_raw = proj[..., o:o + H]
        o += H
        lam_raw = proj[..., o:o + H]
        o += H
        theta = proj[..., o:]
        x_raw = jax.nn.silu(x_raw)
        Bm = _rms(Bm.reshape(B, T, G, R, N)) * B_norm_bias[:, None, :]
        Cm = _rms(Cm.reshape(B, T, G, N)) * C_norm_bias
        A = -jnp.exp(A_log)
        dt = jnp.clip(jax.nn.softplus(dt_raw + dt_bias), 0.0001, 0.5)
        ang = -jnp.cumsum(jnp.mean(dt, axis=-1, keepdims=True) * theta, axis=1)
        cos, sin = (jnp.cos(ang), jnp.sin(ang))
        Cr = _rope(Cm, cos[:, :, None, :], sin[:, :, None, :])
        Br = _rope(Bm, cos[:, :, None, None, :], sin[:, :, None, None, :])
        xh = x_raw.reshape(B, T, H, R, P)
        log_dA = dt * A
        alpha = jnp.exp(log_dA)
        lam = jax.nn.sigmoid(lam_raw)
        xg = (lam * dt)[..., None, None] * xh
        x_prev = jnp.pad(xh, ((0, 0), (1, 0), (0, 0), (0, 0), (0, 0)))[:, :T]
        xb = ((1.0 - lam) * dt * alpha)[..., None, None] * x_prev
        Bb = jnp.pad(Br, ((0, 0), (1, 0), (0, 0), (0, 0), (0, 0)))[:, :T]

        def ch(a):
            return a.reshape(B, NC, L, *a.shape[2:])
        cum = jnp.cumsum(ch(log_dA), axis=2)
        mask = jnp.tril(jnp.ones((L, L), bool))
        diff = cum[:, :, :, None, :] - cum[:, :, None, :, :]
        dmat = jnp.exp(jnp.where(mask[None, None, :, :, None], diff, NEG))
        Cc = ch(Cr)
        Bgc, Bbc = (ch(Br), ch(Bb))
        xgc = ch(xg).reshape(B, NC, L, G, E, R, P)
        xbc = ch(xb).reshape(B, NC, L, G, E, R, P)
        sg = jnp.einsum('bclgn,bcmgrn->bclmgr', Cc, Bgc) * SCALE
        sb = jnp.einsum('bclgn,bcmgrn->bclmgr', Cc, Bbc) * SCALE
        dg = dmat.reshape(B, NC, L, L, G, E)
        y_intra = jnp.einsum('bclmgr,bclmge,bcmgerp->bclgep', sg, dg, xgc) + jnp.einsum('bclmgr,bclmge,bcmgerp->bclgep', sb, dg, xbc)
        dec_end = jnp.exp(cum[:, :, -1:, :] - cum).reshape(B, NC, L, G, E)
        st = (jnp.einsum('bclge,bclgrn,bclgerp->bcgenp', dec_end, Bgc, xgc) + jnp.einsum('bclge,bclgrn,bclgerp->bcgenp', dec_end, Bbc, xbc)).reshape(B, NC, H, N, P)
        cdec = jnp.exp(cum[:, :, -1, :])

        def step(S, inp):
            cd, s = inp
            return (cd[..., None, None] * S + s, S)
        _, Sprev = jax.lax.scan(step, jnp.zeros((B, H, N, P), x.dtype), (jnp.moveaxis(cdec, 1, 0), jnp.moveaxis(st, 1, 0)))
        Sprev = jnp.moveaxis(Sprev, 0, 1).reshape(B, NC, G, E, N, P)
        dec_in = jnp.exp(cum).reshape(B, NC, L, G, E)
        y_inter = SCALE * jnp.einsum('bclgn,bclge,bcgenp->bclgep', Cc, dec_in, Sprev)
        y = (y_intra + y_inter).reshape(B, T, D_INNER)
        y = _rms(y * jax.nn.silu(z))
        return y @ W_out

    def _L0_ffn_ref(x, W_r, W_k, W_v, mu_r, mu_k):
        import jax, jax.numpy as jnp
        import numpy as np
        DIM = 128

        def _reference_tuple_inner(x, W_r, W_k, W_v, mu_r, mu_k):
            B, T, C = x.shape
            x_prev = jnp.concatenate([jnp.zeros((B, 1, C), x.dtype), x[:, :-1, :]], axis=1)
            xr = mu_r * x + (1.0 - mu_r) * x_prev
            xk = mu_k * x + (1.0 - mu_k) * x_prev
            r = jax.nn.sigmoid(jnp.einsum('btc,dc->btd', xr, W_r))
            k = jnp.einsum('btc,dc->btd', xk, W_k)
            k_act = jnp.square(jax.nn.relu(k))
            out = r * jnp.einsum('btc,dc->btd', k_act, W_v)
            new_state = x[:, -1, :]
            return (out, new_state)
        return _reference_tuple_inner(x, W_r, W_k, W_v, mu_r, mu_k)[0]
    x = L0_attn_x
    x = x + _layernorm(_L0_attn_ref(_layernorm(x, axis=-1), L0_attn_W_in, L0_attn_A_log, L0_attn_dt_bias, L0_attn_B_norm_bias, L0_attn_C_norm_bias, L0_attn_W_out), axis=-1)
    x = x + _layernorm(_L0_ffn_ref(_layernorm(x, axis=-1), L0_ffn_W_r, L0_ffn_W_k, L0_ffn_W_v, L0_ffn_mu_r, L0_ffn_mu_k), axis=-1)
    return x

_drawn_inputs = setup_inputs


def setup_inputs(seed=0):
    import zlib

    import numpy as np

    out = dict(_drawn_inputs(seed))
    spreads = {}
    factors = {}
    for name, (base, spread) in spreads.items():
        noise = np.random.default_rng([zlib.crc32(name.encode()), seed]).standard_normal(out[name].shape)
        drawn = base * np.exp(spread * noise) if base else spread * noise
        out[name] = jnp.asarray(drawn.astype(out[name].dtype))
    for name, factor in factors.items():
        out[name] = (out[name] * factor).astype(out[name].dtype)
    return out
```

```python
from contextlib import ExitStack

import numpy as np

import concourse.bass as bass
from concourse import mybir

F32 = mybir.dt.float32
I32 = mybir.dt.int32
ALU = mybir.AluOpType
ACT = mybir.ActivationFunctionType
AX_X = mybir.AxisListType.X

B, T, D = 8, 512, 128
L = 64
NC_ = T // L
NQ = B // 2
NT = NC_ * NQ
H, P, R, N = 32, 8, 2, 64
DI = H * P
G3 = R + 1
O_BC, O_Z, O_X, O_S = 0, G3 * N, G3 * N + DI, G3 * N + DI + DI * R
NS = 3 * H
WCOLS = O_S + NS
AK = 8
MAX_A = 68.0 / (0.5 * L / 2)
EPS_LN, EPS_RMS = 1e-5, 1e-6
SCALE2_INV = float(N * R)
MAGIC = 1.5 * 2.0 ** 23
TWO_PI_HI = 6.28125
TWO_PI_LO = float(2 * np.pi - 6.28125)
PI_IN = 3.1415925

MOM = 6
FLAG_AT = 6
LA_AT, B_AT, PRE_AT, EG_AT, ANG_AT = 5, 8, 17, 20, 28
F_AT, TABLES_AT = 10, 15
P_B, P_CUM, P_F, P_S = 2, 4, 6, 8
FAC_POW = MOM + 3

CONSTS = ["ident", "strict", "tri", "ones", "centre", "late", "early", "shift", "edge", "hot"]


def constants():
    k, m = np.arange(128)[:, None], np.arange(128)[None, :]
    same, kl, ml = k // L == m // L, k % L, m % L
    mid = L // 2 - 1
    mats = {
        "ident": k == m,
        "strict": same & (kl < ml),
        "tri": same & (kl <= ml),
        "ones": same,
        "late": same & (kl > mid),
        "early": same & (kl <= mid),
        "shift": same & (kl == ml + 1),
        "edge": same & (kl == 0) & (ml == L - 1),
        "hot": (kl == m) & (m < L),
    }
    mats = {n: v.astype(np.float32) for n, v in mats.items()}
    mats["centre"] = mats["tri"] - mats["early"]
    return np.concatenate([mats[n] for n in CONSTS], axis=1).astype(np.float32)


def build(nc, x, w_in, a_log, dt_bias, bc_bias, w_out, w_r, w_k, w_v, mu, consts, out, force_general=False):
    ctx = ExitStack()
    with ctx:
        def sb(name, *shape, dt=F32):
            return ctx.enter_context(nc.sbuf_tensor(name, list(shape), dt))

        def sem(name):
            return ctx.enter_context(nc.semaphore(name))

        def at(buf, i):
            if isinstance(i, int):
                return buf[:, i, :]
            return buf[:, bass.ds(i, 1), :].rearrange("p a n -> p (a n)")

        def wait_past(eng, semaphore, value):
            if not isinstance(value, int) or value > 0:
                eng.wait_ge(semaphore, value)

        def steps(eng, n, body, first=1):
            for k in range(first):
                body(k)
            with eng.Fori(first, n) as k:
                body(k)

        x_all = sb("x_all", 128, NT, D)
        xnT_all = sb("xnT_all", 128, NT, 128)
        o_all = sb("o_all", 128, NT, D)
        w_sb = sb("w_sb", 128, WCOLS)
        cm = sb("cm", 128, len(CONSTS), 128)
        wo_sb = sb("wo_sb", 128, 2, D)
        wr_sb = sb("wr_sb", 128, D)
        wk_sb = sb("wk_sb", 128, D)
        wv_sb = sb("wv_sb", 128, D)
        mu_sb = sb("mu_sb", 128, 2)
        dtb_sb = sb("dtb_sb", 128, H)
        negA = sb("negA", 128, H)
        bcb_sb = sb("bcb_sb", 128, G3 * N)
        flag = sb("flag", 128, 4)
        flag_i = sb("flag_i", 128, 1, dt=I32)
        small = sb("small", 128, NT, NS)
        dt_all = sb("dt_all", 128, NT, H)
        g_all = sb("g_all", 128, NT, H)
        b_all = sb("b_all", 128, NT, H)
        la_all = sb("la_all", 128, NT, H)
        ec_all = sb("ec_all", 128, NT, H)
        eg_all = sb("eg_all", 128, NT, H)
        f_all = sb("f_all", 128, NT, H)
        cs_all = sb("cs_all", 128, NT, 4 * H)
        ost_all = sb("ost_all", 128, NT, 6)
        ysq_all = sb("ysq_all", 128, NT, 1)
        csq_all = sb("csq_all", 128, NT, 1)
        tokc = sb("tokc", 128, 8, NT)
        halfn = sb("halfn", 128, 8)
        epst = sb("epst", 128, 4)

        bank = [ctx.enter_context(nc.psum_tensor(f"bank{n}", [128, 512], F32)) for n in range(8)]

        def c_(name):
            return cm[:, CONSTS.index(name), :]

        s_x = [sem(f"x_loaded{k}") for k in range(4)]
        s_w = sem("w_in_loaded")
        s_w2 = sem("other_weights_loaded")
        s_a = sem("decay_inputs_loaded")
        s_c = sem("consts_loaded")
        s_ones = sem("fills_done")
        prep = sem("prep_vector")

        bn8 = sb("bn8", 128, AK, 6)
        mo8 = sb("mo8", 128, 6, AK)
        rs8 = sb("rs8", 128, AK)
        xn8 = sb("xn8", 128, AK, D)
        xt8 = sb("xt8", 128, AK, 128)
        a_st, a_mo, a_rs, a_xn, a_tr, a_ev, a_mm, a_sm = (sem(n) for n in (
            "a_stats", "a_moments", "a_rstd", "a_normed", "a_transposed", "a_evacuated", "a_projected", "a_small"))
        v2, s2, p2 = sem("tables_vector"), sem("tables_scalar"), sem("tables_tensor")

        mean8 = sem("a_means")
        halfpi = sb("halfpi", 128, 1)
        mdt = sb("mdt", 128, NT)

        def scratch(n):
            return o_all[:].rearrange("p t d -> p (t d)")[:, n * NT * H:(n + 1) * NT * H]\
                .rearrange("p (t h) -> p t h", h=H)

        pre3 = scratch(0)
        turns = scratch(1)
        ang = scratch(2)
        ang_in = scratch(3)

        def flat(buf):
            return buf[:].rearrange("p t h -> p (t h)")

        xt = sb("xt", 128, 2, 128)
        bc = sb("bc", 128, 2, G3 * N)
        rot = sb("rot", 128, G3, 2, 2, H)
        dup = sb("dup", 128, 2, G3, 2, N)
        xs = sb("xs", 128, 2, DI * R)
        zs = sb("zs", 128, 2, DI)
        junk = sb("junk", 128, G3 * N)
        junk_y = sb("junk_y", 128, DI)
        msb = sb("msb", 128, 2, R)
        mse = sb("mse", 128, R)
        rb = sb("rb", 128, 2, R)
        wx = sb("wx", 128, 2, H, R)
        x1 = sb("x1", 128, 2, DI * R)
        prod = sb("prod", 128, R, N)
        cb = sb("cb", 128, R)
        cbr = sb("cbr", 128, 2, R)
        d0 = sb("d0", 128, DI)
        d1 = sb("d1", 128, DI)
        dg = sb("dg", 128, 2, DI)
        bt = sb("bt", 128, G3, 128)
        sg = sb("sg", 128, R, 128)
        st = sb("st", 128, NQ, DI)
        sp = sb("sp", 128, DI)
        ya = sb("ya", 128, DI)
        ys = sb("ys", 128, DI)
        y = sb("y", 128, 2, DI)
        yt = sb("yt", 128, 2, 128)
        oh = sb("oh", 128, 2, 128)
        xk = sb("xk", 128, 2, DI * R)
        fk = sb("fk", 128, H)
        sk = sb("sk", 128, DI)
        yk = sb("yk", 128, DI)

        names = ("xt_copied zbc_ps x_ps bc_ready rotated dup0 dup1 x_silu z_silu sq_done mse_ready rb_ready w_ready "
                 "x1_ready prod_ready cb_ready cbr_ready d0_ready d1_ready dg_ready t_ps t_sb sg_ps sg_ready p_ps "
                 "p_added st_ready y_ps ya_ready ys_ready y_ready ysq_done yt_ps yt_sb o_ps o_sb ost_done st_zero").split()
        S = {n: sem(n) for n in names}
        G = {n: sem("g_" + n) for n in ("oh x1k fk_ps fk_sb s1 y_ps yk p_ps st zero done".split())}

        fst = sb("fst", 128, NQ, 6)
        fmo = sb("fmo", 128, 6, NQ)
        frs = sb("frs", 128, 2, NQ)
        fnb = sb("fnb", 128, NQ)
        xn2 = sb("xn2", 128, NQ, D)
        x2T = sb("x2T", 128, 2, B, L + 1)
        dl = sb("dl", 128, B * L)
        xkm = sb("xkm", 128, B * L)
        xrm = sb("xrm", 128, B * L)
        kr = sb("kr", 128, B * L)
        ka = sb("ka", 128, B * L)
        th = sb("th", 128, NQ, D)
        ff = sb("ff", 128, NQ, D)
        f2 = sb("f2", 128, NQ, D)
        xr = sb("xr", 128, 2, NQ, D)
        oc = sb("oc", 128, 2, NQ, D)
        cnames = ("x1 stats mom pow norm_bias normed tr_ps tr_sb carried delta mix_k mix_r k_ps k_relu k_act r_ps th v_ps "
                  "f stats3 mom3 pow3 res bias3 outv").split()
        C = {n: sem("c_" + n) for n in cnames}
        C3 = sem("c_mean3")
        fnb3 = sb("fnb3", 128, NQ)
        frs3 = sb("frs3", 128, NQ)
        stored = [sem(f"stored{n}") for n in range(2)]
        fac_v, fac_p = sem("factors_vector"), sem("factors_pool")

        def moments(dve, stats, mo, n, chain, base, scale):
            even, odd = stats[:, 0:n, 1], stats[:, 0:n, 4]
            nc.vector.tensor_tensor(mo[:, 0, 0:n], even, odd, ALU.add).then_inc(chain, 1)
            nc.vector.tensor_tensor(mo[:, 1, 0:n], even, odd, ALU.subtract).then_inc(chain, 1)
            nc.vector.tensor_tensor(mo[:, 2, 0:n], stats[:, 0:n, 2], stats[:, 0:n, 5], ALU.add).then_inc(chain, 1)
            dve.wait_ge(chain, base + 2)
            nc.vector.tensor_tensor(mo[:, 3, 0:n], mo[:, 1, 0:n], mo[:, 1, 0:n], ALU.mult).then_inc(chain, 1)
            dve.wait_ge(chain, base + 4)
            nc.vector.scalar_tensor_tensor(out=mo[:, 4, 0:n], in0=mo[:, 3, 0:n], scalar=float(D // 4),
                                           in1=mo[:, 2, 0:n], op0=ALU.mult, op1=ALU.add).then_inc(chain, 1)
            dve.wait_ge(chain, base + 5)
            nc.vector.tensor_scalar(mo[:, 5, 0:n], mo[:, 4, 0:n], 1.0 / D, float(scale), ALU.mult, ALU.add).then_inc(chain, 1)

        block = ctx.enter_context(nc.Block())

        @block.sync
        def _(sp_):
            for k in range(NC_ // 2):
                for h in range(2):
                    for q in range(0, NQ, 1):
                        (sp_ if q % 2 else sp_).dma_start(
                            x_all[64 * h:64 * h + 64, 8 * k + q:8 * k + q + 5:4, :],
                            x[2 * q + h, 2 * k * L:2 * (k + 1) * L, :].rearrange("(c l) d -> l c d", l=L),
                        ).then_inc(s_x[k], 16)
            with sp_.Fori(0, NC_ // 2) as cc:
                for par in range(2):
                    c = cc * 2 + par
                    sp_.wait_ge(C["outv"], (c + 1) * NQ)
                    for h in range(2):
                        sp_.dma_start(
                            out.rearrange("(q h) (c l) d -> h c l q d", h=2, l=L)[h, bass.ds(c, 1)]
                            .rearrange("a l q d -> (a l) q d"),
                            oc[64 * h:64 * h + 64, par]).then_inc(stored[par], 16)
            for par in range(2):
                sp_.wait_ge(stored[par], 16 * NC_)

        @block.gpsimd
        def _(pool):
            for dst, src in ((wo_sb[:], w_out.rearrange("(k p) n -> p k n", p=128)), (wr_sb[:], w_r), (wk_sb[:], w_k),
                             (wv_sb[:], w_v), (mu_sb[:], mu), (bcb_sb[:], bc_bias.partition_broadcast(128))):
                pool.dma_start(dst, src).then_inc(s_w2, 16)
            nc.gpsimd.memset(halfn[:], -0.5).then_inc(s_ones, 1)
            nc.gpsimd.memset(epst[:], EPS_RMS).then_inc(s_ones, 1)
            nc.gpsimd.memset(st[:], 0.0).then_inc(S["st_zero"], 1)
            nc.gpsimd.memset(dup[:], 0.0).then_inc(S["st_zero"], 1)
            nc.gpsimd.memset(x2T[:, 1, :, L:L + 1], 0.0).then_inc(S["st_zero"], 1)
            pool.wait_ge(s_ones, 2)
            with pool.Fori(0, NT // AK) as k:
                pool.wait_ge(a_mo, (k + 1) * MOM)
                nc.gpsimd.tensor_tensor(rs8[:], mo8[:, 5, :], halfn[:, 0:AK], ALU.pow).then_inc(a_rs, 1)

            def early(n, par):
                pool.wait_ge(S["bc_ready"], n + 1)
                pool.wait_ge(S["cb_ready"], n)
                nc.gpsimd.tensor_tensor(prod[:], bc[:, par, 0:R * N].rearrange("p (r n) -> p r n", r=R),
                                        bc[:, par, R * N:].unsqueeze(1).broadcast_to([128, R, N]),
                                        ALU.mult).then_inc(S["prod_ready"], 1)
                pool.wait_ge(S["sq_done"], n + 1)
                nc.gpsimd.tensor_tensor(mse[:], msb[:, par], epst[:, 0:R], ALU.add).then_inc(S["mse_ready"], 1)
                pool.wait_ge(S["mse_ready"], n + 1)
                nc.gpsimd.tensor_tensor(rb[:, par], mse[:], halfn[:, 0:R], ALU.pow).then_inc(S["rb_ready"], 1)
                pool.wait_ge(S["rb_ready"], n + 1)
                if not isinstance(n, int) or n >= 2:
                    pool.wait_ge(S["x1_ready"], n - 1)
                nc.gpsimd.tensor_tensor(wx[:, par], at(eg_all, n).unsqueeze(2).broadcast_to([128, H, R]),
                                        rb[:, par].unsqueeze(1).broadcast_to([128, H, R]),
                                        ALU.mult).then_inc(S["w_ready"], 1)
                pool.wait_ge(S["cb_ready"], n + 1)
                if not isinstance(n, int) or n >= 2:
                    pool.wait_ge(S["d1_ready"], n - 1)
                nc.gpsimd.tensor_tensor(cbr[:, par], cb[:], rb[:, par], ALU.mult).then_inc(S["cbr_ready"], 1)
                pool.wait_ge(S["d1_ready"], n + 1)
                if not isinstance(n, int) or n >= 2:
                    pool.wait_ge(S["ys_ready"], n - 1)
                nc.gpsimd.tensor_tensor(dg[:, par].rearrange("p (h e) -> p h e", e=P),
                                        d1[:].rearrange("p (h e) -> p h e", e=P),
                                        at(g_all, n).unsqueeze(2).broadcast_to([128, H, P]),
                                        ALU.mult).then_inc(S["dg_ready"], 1)

            def late(i, q, par, general):
                if not general:
                    pool.wait_ge(S["p_added"], i + 1)
                    pool.wait_ge(S["y_ps"], i + 1)
                    nc.gpsimd.tensor_tensor(st[:, q].rearrange("p (h e) -> p h e", e=P),
                                            sp[:].rearrange("p (h e) -> p h e", e=P),
                                            at(f_all, i).unsqueeze(2).broadcast_to([128, H, P]),
                                            ALU.mult).then_inc(S["st_ready"], 1)
                pool.wait_ge(S["ys_ready"], i + 1)
                pool.wait_ge(S["z_silu"], i + 1)
                if not isinstance(i, int) or i >= 2:
                    pool.wait_ge(S["yt_ps"], i - 1)
                    pool.wait_ge(S["ysq_done"], i - 1)
                nc.gpsimd.tensor_tensor(y[:, par], ys[:], zs[:, par], ALU.mult).then_inc(S["y_ready"], 1)

            def tiles(general):
                early(0, 0)
                for q in range(NQ):
                    early(q + 1, (q + 1) % 2)
                    late(q, q, q % 2, general)
                with pool.Fori(1, NC_ - 1) as c:
                    for q in range(NQ):
                        early(c * NQ + q + 1, (q + 1) % 2)
                        late(c * NQ + q, q, q % 2, general)
                for q in range(NQ):
                    if q < NQ - 1:
                        early((NC_ - 1) * NQ + q + 1, (q + 1) % 2)
                    late((NC_ - 1) * NQ + q, q, q % 2, general)

            pool.wait_ge(prep, FLAG_AT)
            pool.wait_ge(v2, EG_AT)
            pool.wait_ge(s2, F_AT)
            fl = pool.value_load(flag_i[0:1, 0:1], min_val=0, max_val=1)
            with pool.If(fl > 0):
                tiles(False)
            with pool.Else():
                tiles(True)

            for half in range(0, NT, 8):
                pool.wait_ge(fac_v, FAC_POW)
                nc.gpsimd.tensor_tensor(tokc[:, 7, half:half + 8], tokc[:, 6, half:half + 8], halfn[:],
                                        ALU.pow).then_inc(fac_p, 1)
            def chunk(cc):
                for par in range(2):
                    c = cc * 2 + par
                    pool.wait_ge(C["mom"], (c + 1) * MOM)
                    nc.gpsimd.tensor_tensor(frs[:, 0], fmo[:, 5], halfn[:, 0:NQ], ALU.pow).then_inc(C["pow"], 1)
                    pool.wait_ge(C["tr_sb"], c + 1)
                    pool.wait_ge(C["carried"], c + 1)
                    wait_past(pool, C["mix_r"], c)
                    nc.gpsimd.tensor_tensor(dl[:].rearrange("p (b l) -> p b l", b=B), x2T[:, par, :, 1:],
                                            x2T[:, par, :, 0:L], ALU.subtract).then_inc(C["delta"], 1)
                    pool.wait_ge(C["mom3"], (c + 1) * MOM)
                    nc.gpsimd.tensor_tensor(frs[:, 1], fmo[:, 5], halfn[:, 0:NQ], ALU.pow).then_inc(C["pow3"], 1)

            steps(pool, NC_ // 2, chunk)

        @block.scalar
        def _(act):
            act.dma_start(negA[:], a_log.partition_broadcast(128)).then_inc(s_a, 16)
            act.dma_start(dtb_sb[:], dt_bias.partition_broadcast(128)).then_inc(s_a, 16)
            act.dma_start(cm[:], consts.rearrange("p (n m) -> p n m", m=128)).then_inc(s_c, 16)
            act.dma_start(w_sb[:, O_S:], w_in[:, O_S:]).then_inc(s_w, 16)
            act.dma_start(w_sb[:, 0:O_S], w_in[:, 0:O_S]).then_inc(s_w, 16)
            act.wait_ge(s_a, 32)
            nc.scalar.activation(negA[:], negA[:], ACT.Exp).then_inc(s2, 1)
            def first_phase(k):
                for j in range(2):
                    act.wait_ge(a_tr, k * 2 + j + 1)
                    wait_past(act, a_mm, k * 2 + j)
                    nc.scalar.activation(xt8[:, 4 * j:4 * j + 4], bank[j][:], ACT.Copy).then_inc(a_ev, 1)
                for j in range(2):
                    act.wait_ge(a_ev, k * 2 + j + 1)
                    nc.scalar.activation(xnT_all[:, bass.ds(k * AK + 4 * j, 4)], xt8[:, 4 * j:4 * j + 4],
                                         ACT.Copy).then_inc(a_sm, 1)
                    act.wait_ge(a_mm, k * 2 + j + 1)
                    nc.scalar.activation(small[:, bass.ds(k * AK + 4 * j, 4)],
                                         bank[2 + j][:, 0:4 * NS].rearrange("p (t s) -> p t s", t=4),
                                         ACT.Copy).then_inc(a_sm, 1)

            steps(act, NT // AK, first_phase)
            act.wait_ge(v2, 1)
            nc.scalar.activation(dt_all[:], dt_all[:], ACT.Exp).then_inc(s2, 1)
            act.wait_ge(a_sm, 4 * NT // AK)
            nc.scalar.activation(b_all[:], small[:, :, H:2 * H], ACT.Tanh, scale=0.5).then_inc(s2, 1)
            act.wait_ge(v2, 2)
            nc.scalar.activation(dt_all[:], dt_all[:], ACT.Ln).then_inc(s2, 1)
            act.wait_ge(prep, FLAG_AT)
            for j in range(2):
                act.wait_ge(p2, P_CUM)
                nc.scalar.activation(ec_all[:, 16 * j:16 * j + 16].rearrange("p t h -> p (t h)"), bank[j][:],
                                     ACT.Exp, scale=flag[:, 0:1]).then_inc(s2, 1)
                nc.scalar.activation(eg_all[:, 16 * j:16 * j + 16].rearrange("p t h -> p (t h)"), bank[j][:],
                                     ACT.Exp, scale=flag[:, 1:2]).then_inc(s2, 1)
            for j in range(2):
                act.wait_ge(p2, P_F)
                nc.scalar.activation(f_all[:, 16 * j:16 * j + 16].rearrange("p t h -> p (t h)"), bank[2 + j][:],
                                     ACT.Exp).then_inc(s2, 1)
            nc.scalar.activation(b_all[:], la_all[:], ACT.Exp).then_inc(s2, 1)
            act.wait_ge(v2, ANG_AT)
            for slot, src, scale, bias in ((0, turns, -1.0, halfpi[:, 0:1]), (3, turns, -1.0, halfpi[:, 0:1]),
                                           (2, ang_in, 1.0, 0.0), (1, ang_in, -1.0, 0.0)):
                nc.scalar.activation(cs_all[:, :, slot * H:slot * H + H], src[:], ACT.Sin, scale=scale,
                                     bias=bias).then_inc(s2, 1)

            def copy_in(n, par):
                if not isinstance(n, int) or n >= 2:
                    act.wait_ge(S["x_ps"], n - 1)
                nc.scalar.activation(xt[:, par], at(xnT_all, n), ACT.Copy).then_inc(S["xt_copied"], 1)

            def squares(n, par):
                act.wait_ge(S["bc_ready"], n + 1)
                if not isinstance(n, int) or n >= 2:
                    act.wait_ge(S["rb_ready"], n - 1)
                act.wait_ge(S["sq_done"], n)
                for r in range(R):
                    nc.scalar.activation(junk[:, r * N:r * N + N], bank[0][:, r * N:r * N + N], ACT.Square,
                                         scale=float(N) ** -0.5, accum_out=msb[:, par, r:r + 1])
                nc.scalar.activation(junk[:, R * N:], bank[0][:, R * N:G3 * N], ACT.Square, scale=float(N) ** -0.5,
                                     accum_out=at(csq_all, n)).then_inc(S["sq_done"], 1)

            def gates(n, par):
                act.wait_ge(S["x_ps"], n + 1)
                if not isinstance(n, int) or n >= 2:
                    act.wait_ge(S["x1_ready"], n - 1)
                    act.wait_ge(S["d1_ready"], n - 1)
                nc.scalar.activation(xs[:, par], bank[1][:], ACT.Silu).then_inc(S["x_silu"], 1)
                if not isinstance(n, int) or n >= 2:
                    act.wait_ge(S["y_ready"], n - 1)
                nc.scalar.activation(zs[:, par], bank[0][:, O_Z:O_Z + DI], ACT.Silu).then_inc(S["z_silu"], 1)

            def turned(n):
                act.wait_ge(S["t_ps"], n + 1)
                nc.scalar.activation(bt[:].rearrange("p g m -> p (g m)"), bank[2][:, 0:G3 * 128],
                                     ACT.Copy).then_inc(S["t_sb"], 1)

            def own_token(n, par):
                act.wait_ge(S["x_silu"], n + 1)
                act.wait_ge(S["cbr_ready"], n + 1)
                act.wait_ge(S["d1_ready"], n)
                nc.scalar.activation(d0[:].rearrange("p (h e) -> p h e", e=P),
                                     xs[:, par].rearrange("p (h r e) -> p r h e", r=R, e=P)[:, 0],
                                     ACT.Copy, scale=cbr[:, par, 0:1]).then_inc(S["d0_ready"], 1)

            def late_yt(i):
                act.wait_ge(S["yt_ps"], i + 1)
                act.wait_ge(S["o_ps"], i)
                nc.scalar.activation(yt[:].rearrange("p k m -> p (k m)"), bank[6][:, 0:DI], ACT.Copy).then_inc(S["yt_sb"], 1)

            def late_ysq(i, par):
                act.wait_ge(S["ysq_done"], i)
                act.wait_ge(S["y_ready"], i + 1)
                nc.scalar.activation(junk_y[:], y[:, par], ACT.Square, scale=float(DI) ** -0.5,
                                     accum_out=at(ysq_all, i)).then_inc(S["ysq_done"], 1)

            def late_o(i):
                act.wait_ge(S["o_ps"], i + 1)
                nc.scalar.activation(at(o_all, i), bank[7][:, 0:D], ACT.Copy).then_inc(S["o_sb"], 1)

            def step(i, q, ahead=2, behind=True):
                par, other = q % 2, (q + 1) % 2
                if ahead >= 1:
                    squares(i + 1, other)
                if behind:
                    late_yt(i - 1)
                if ahead >= 1:
                    gates(i + 1, other)
                    turned(i + 1)
                    own_token(i + 1, other)
                if behind:
                    late_ysq(i - 1, other)
                if ahead >= 2:
                    copy_in(i + 2, par)
                if behind:
                    late_o(i - 1)

            copy_in(0, 0)
            copy_in(1, 1)
            act.wait_ge(S["st_zero"], 3)
            squares(0, 0)
            gates(0, 0)
            turned(0)
            own_token(0, 0)
            for q in range(NQ):
                step(q, q, behind=q > 0)
            with act.Fori(1, NC_ - 1) as c:
                for q in range(NQ):
                    step(c * NQ + q, q)
            for q in range(NQ):
                step((NC_ - 1) * NQ + q, q, ahead=min(2, NQ - 1 - q))
            late_yt(NT - 1)
            late_ysq(NT - 1, (NT - 1) % 2)
            late_o(NT - 1)

            def chunk(cc):
                for par in range(2):
                    c = cc * 2 + par
                    act.wait_ge(C["norm_bias"], c + 1)
                    wait_past(act, C["tr_ps"], c)
                    for q in range(NQ):
                        nc.scalar.activation(xn2[:, q], xr[:, par, q], ACT.Identity, scale=frs[:, 0, q:q + 1],
                                             bias=fnb[:, q:q + 1]).then_inc(C["normed"], 1)
                    act.wait_ge(C["tr_ps"], c + 1)
                    wait_past(act, C["carried"], c)
                    nc.scalar.activation(x2T[:, par, :, 1:], bank[0][:].rearrange("p (b l) -> p b l", b=B),
                                         ACT.Copy).then_inc(C["tr_sb"], 1)
                    act.wait_ge(C["k_ps"], c + 1)
                    wait_past(act, C["k_act"], c)
                    nc.scalar.activation(kr[:], bank[1][:], ACT.Relu).then_inc(C["k_relu"], 1)
                    act.wait_ge(C["r_ps"], c + 1)
                    wait_past(act, C["f"], c * NQ)
                    nc.scalar.activation(th[:].rearrange("p q d -> p (q d)"), bank[2][:], ACT.Tanh,
                                         scale=0.5).then_inc(C["th"], 1)
                    act.wait_ge(C["bias3"], c + 1)
                    for q in range(NQ):
                        act.wait_ge(C["res"], c * NQ + q + 1)
                        if q == 0:
                            wait_past(act, stored[par], cc * 32)
                        nc.scalar.activation(oc[:, par, q], f2[:, q], ACT.Identity,
                                             bias=fnb3[:, q:q + 1]).then_inc(C["outv"], 1)

            steps(act, NC_ // 2, chunk)

        @block.tensor
        def _(pe):
            pe.wait_ge(s_c, 16)
            pe.wait_ge(s_w, 32)
            def first_phase(k):
                for j in range(2):
                    wait_past(pe, a_ev, k * 2 + j)
                    for t in range(4 * j, 4 * j + 4):
                        pe.wait_ge(a_xn, k * AK + t + 1)
                        mm = nc.tensor.transpose(bank[j][:, (t % 4) * 128:(t % 4) * 128 + 128], xn8[:, t], c_("ident"))
                    mm.then_inc(a_tr, 1)
                for j in range(2):
                    pe.wait_ge(a_ev, k * 2 + j + 1)
                    wait_past(pe, a_sm, (k * 2 + j) * 2)
                    for t in range(4 * j, 4 * j + 4):
                        mm = nc.tensor.matmul(bank[2 + j][:, (t % 4) * NS:(t % 4) * NS + NS], xt8[:, t], w_sb[:, O_S:],
                                              start=True, stop=True)
                    mm.then_inc(a_mm, 1)

            steps(pe, NT // AK, first_phase)
            pe.wait_ge(a_sm, 4 * NT // AK)
            pe.wait_ge(v2, B_AT)
            bf = b_all[:].rearrange("p t h -> p (t h)")
            lf = la_all[:].rearrange("p t h -> p (t h)")
            E = NQ * H
            for j in range(2):
                nc.tensor.matmul(bank[4 + j][:], c_("shift"), bf[:, 512 * j:512 * j + 512], start=True, stop=False,
                                 skip_group_check=True)
                w = 512 if j == 0 else 512 - E
                nc.tensor.matmul(bank[4 + j][:, 0:w], c_("edge"), bf[:, 512 * j + E:512 * j + E + w], start=False,
                                 stop=True, skip_group_check=True).then_inc(p2, 1)
            pe.wait_ge(v2, LA_AT)
            for j in range(2):
                nc.tensor.matmul(bank[j][:], c_("centre"), lf[:, 512 * j:512 * j + 512], start=True,
                                 stop=True).then_inc(p2, 1)
            for j in range(2):
                nc.tensor.matmul(bank[2 + j][:], c_("late"), lf[:, 512 * j:512 * j + 512], start=True, stop=False,
                                 skip_group_check=True)
                w = 512 if j == 0 else 512 - E
                nc.tensor.matmul(bank[2 + j][:, 0:w], c_("early"), lf[:, 512 * j + E:512 * j + E + w], start=False,
                                 stop=True, skip_group_check=True).then_inc(p2, 1)
            pe.wait_ge(v2, PRE_AT)
            mt, pre = flat(dt_all), flat(pre3)
            for j in range(2):
                nc.tensor.matmul(bank[6 + j][:], c_("tri"), mt[:, 512 * j:512 * j + 512], start=True, stop=False)
                nc.tensor.matmul(bank[6 + j][:], c_("ones"), pre[:, 512 * j:512 * j + 512], start=False,
                                 stop=True).then_inc(p2, 1)

            def project(n, par):
                pe.wait_ge(S["xt_copied"], n + 1)
                pe.wait_ge(S["z_silu"], n)
                nc.tensor.matmul(bank[0][:, 0:O_X], xt[:, par], w_sb[:, 0:O_X], start=True, stop=True)\
                    .then_inc(S["zbc_ps"], 1)
                pe.wait_ge(S["x_silu"], n)
                nc.tensor.matmul(bank[1][:], xt[:, par], w_sb[:, O_X:O_S], start=True, stop=True)\
                    .then_inc(S["x_ps"], 1)

            def turn(n, par):
                pe.wait_ge(S["dup1"], n + 1)
                pe.wait_ge(S["t_sb"], n)
                for g in range(G3):
                    mm = nc.tensor.transpose(bank[2][:, g * 128:g * 128 + 128],
                                             dup[:, par, g].rearrange("p a n -> p (a n)"), c_("ident"))
                mm.then_inc(S["t_ps"], 1)

            def score(n):
                pe.wait_ge(S["t_sb"], n + 1)
                pe.wait_ge(S["sg_ready"], n)
                for r in range(R):
                    mm = nc.tensor.matmul(bank[3][:, r * 128:r * 128 + 128], bt[:, r], bt[:, R], start=True, stop=True)
                mm.then_inc(S["sg_ps"], 1)

            def rx(buf, r):
                return buf.rearrange("p (h r e) -> p r h e", r=R, e=P)[:, r]

            def mix(i, q, par, between):
                pe.wait_ge(S["x1_ready"], i + 1)
                pe.wait_ge(S["p_added"], i)
                for r in range(R):
                    mm = nc.tensor.matmul(bank[5][:, 0:DI], dup[:, par, r].rearrange("p a n -> p (a n)"),
                                          rx(x1[:, par], r), start=(r == 0), stop=(r == R - 1))
                mm.then_inc(S["p_ps"], 1)
                if not isinstance(i, int) or i >= NQ:
                    pe.wait_ge(S["st_ready"], i - NQ + 1)
                else:
                    pe.wait_ge(S["st_zero"], 3)
                pe.wait_ge(S["ya_ready"], i)
                nc.tensor.matmul(bank[4][:, 0:DI], bt[:, R], st[:, q], start=True, stop=False)
                between()
                pe.wait_ge(S["sg_ready"], i + 1)
                for r in range(R):
                    mm = nc.tensor.matmul(bank[4][:, 0:DI], sg[:, r], rx(x1[:, par], r), start=False, stop=(r == R - 1))
                mm.then_inc(S["y_ps"], 1)

            def mix_general(i, q, par):
                def token(t):
                    n = i * L + t
                    pe.wait_ge(G["oh"], n + 1)
                    wait_past(pe, G["fk_sb"], n)
                    nc.tensor.matmul(bank[3][:, 0:H], oh[:, 0], at(b_all, i), start=True, stop=True).then_inc(G["fk_ps"], 1)
                    pe.wait_ge(S["t_sb"], i + 1)
                    pe.wait_ge(G["s1"], n + 1)
                    wait_past(pe, G["yk"], n)
                    nc.tensor.matmul(bank[4][:, 0:DI], bt[:, R], sk[:], start=True, stop=True).then_inc(G["y_ps"], 1)
                    pe.wait_ge(G["x1k"], n + 1)
                    wait_past(pe, G["st"], n)
                    for r in range(R):
                        mm = nc.tensor.matmul(bank[5][:, 0:DI], dup[:, par, r].rearrange("p a n -> p (a n)"),
                                              rx(xk[:, 0], r), start=(r == 0), stop=(r == R - 1))
                    mm.then_inc(G["p_ps"], 1)

                steps(pe, L, token, first=1 if isinstance(i, int) and i == 0 else 0)

            def y_turn(i, par):
                pe.wait_ge(S["y_ready"], i + 1)
                pe.wait_ge(S["yt_sb"], i)
                for k in range(2):
                    mm = nc.tensor.transpose(bank[6][:, k * 128:k * 128 + 128], y[:, par, k * 128:k * 128 + 128],
                                             c_("ident"))
                mm.then_inc(S["yt_ps"], 1)

            def y_out(i):
                pe.wait_ge(S["yt_sb"], i + 1)
                pe.wait_ge(S["o_sb"], i)
                for k in range(2):
                    mm = nc.tensor.matmul(bank[7][:, 0:D], yt[:, k], wo_sb[:, k], start=(k == 0), stop=(k == 1))
                mm.then_inc(S["o_ps"], 1)

            def step(i, q, general, first=False, last=False):
                par, other = q % 2, (q + 1) % 2
                if not last:
                    project(i + 1, other)
                if not first:
                    y_turn(i - 1, other)
                if general:
                    mix_general(i, q, par)
                    if not last:
                        turn(i + 1, other)
                else:
                    mix(i, q, par, lambda: None if last else turn(i + 1, other))
                if not first:
                    y_out(i - 1)
                if not last and not general:
                    score(i + 1)

            def tiles(general):
                project(0, 0)
                turn(0, 0)
                if not general:
                    score(0)
                for q in range(NQ):
                    step(q, q, general, first=(q == 0))
                with pe.Fori(1, NC_ - 1) as c:
                    for q in range(NQ):
                        step(c * NQ + q, q, general)
                for q in range(NQ):
                    step((NC_ - 1) * NQ + q, q, general, last=(q == NQ - 1))
                y_turn(NT - 1, (NT - 1) % 2)
                y_out(NT - 1)

            pe.wait_ge(s_w2, 16 * 6)
            pe.wait_ge(prep, FLAG_AT)
            pe.wait_ge(s2, F_AT)
            fl = pe.value_load(flag_i[0:1, 0:1], min_val=0, max_val=1)
            with pe.If(fl > 0):
                tiles(False)
            with pe.Else():
                tiles(True)

            pe.wait_ge(S["o_sb"], NT)
            def chunk(cc):
                for par in range(2):
                    c = cc * 2 + par
                    pe.wait_ge(C["normed"], (c + 1) * NQ)
                    wait_past(pe, C["tr_sb"], c)
                    for q in range(NQ):
                        mm = nc.tensor.transpose(bank[0][:, q * 128:q * 128 + 128], xn2[:, q], c_("ident"))
                    mm.then_inc(C["tr_ps"], 1)
                    pe.wait_ge(C["mix_k"], c + 1)
                    wait_past(pe, C["k_act"], c)
                    nc.tensor.matmul(bank[1][:], wk_sb[:], xkm[:], start=True, stop=True).then_inc(C["k_ps"], 1)
                    pe.wait_ge(C["mix_r"], c + 1)
                    wait_past(pe, C["th"], c)
                    for q in range(NQ):
                        mm = nc.tensor.matmul(bank[2][:, q * D:q * D + D], xrm[:, q * 128:q * 128 + 128], wr_sb[:],
                                              start=True, stop=True)
                    mm.then_inc(C["r_ps"], 1)
                    pe.wait_ge(C["k_act"], c + 1)
                    wait_past(pe, C["f"], c * NQ)
                    for q in range(NQ):
                        mm = nc.tensor.matmul(bank[3][:, q * D:q * D + D], ka[:, q * 128:q * 128 + 128], wv_sb[:],
                                              start=True, stop=True)
                    mm.then_inc(C["v_ps"], 1)

            steps(pe, NC_ // 2, chunk)

        @block.vector
        def _(dve):
            vec = nc.vector
            dve.wait_ge(s2, 1)
            vec.tensor_reduce(flag[:, 2:3], negA[:], AX_X, ALU.max).then_inc(prep, 1)
            dve.wait_ge(prep, 1)
            vec.tensor_scalar(flag[:, 0:1], flag[:, 2:3], -1.0 if force_general else MAX_A, None, ALU.is_le)\
                .then_inc(prep, 1)
            dve.wait_ge(prep, 2)
            vec.tensor_scalar(flag[:, 1:2], flag[:, 0:1], -1.0, None, ALU.mult).then_inc(prep, 1)
            vec.tensor_copy(flag_i[:], flag[:, 0:1]).then_inc(prep, 1)
            vec.tensor_scalar(negA[:], negA[:], -1.0, None, ALU.mult).then_inc(prep, 1)
            vec.memset(halfpi[:], float(np.pi / 2)).then_inc(prep, 1)

            for k4 in range(4):
                dve.wait_ge(s_x[k4], 16 * 8)
            def first_phase(k):
                for t in range(AK):
                    vec.bn_stats(bn8[:, t], at(x_all, k * AK + t)).then_inc(a_st, 1)
                dve.wait_ge(a_st, (k + 1) * AK)
                wait_past(dve, a_rs, k)
                moments(dve, bn8, mo8, AK, a_mo, k * MOM, EPS_LN)
                vec.tensor_scalar(mo8[:, 1, :], mo8[:, 0, :], 0.5, None, ALU.mult).then_inc(mean8, 1)
                dve.wait_ge(mean8, k + 1)
                dve.wait_ge(a_rs, k + 1)
                wait_past(dve, a_tr, k * 2)
                for t in range(AK):
                    vec.tensor_scalar(xn8[:, t], at(x_all, k * AK + t), mo8[:, 1, t:t + 1], rs8[:, t:t + 1],
                                      ALU.subtract, ALU.mult).then_inc(a_xn, 1)

            steps(dve, NT // AK, first_phase)

            chain = [0]

            def link(ins):
                chain[0] += 1
                ins.then_inc(v2, 1)
                return chain[0]

            dve.wait_ge(a_sm, 4 * NT // AK)
            dve.wait_ge(s_a, 32)
            dve.wait_ge(prep, FLAG_AT)
            link(vec.tensor_tensor(dt_all[:], small[:, :, 0:H], dtb_sb[:].unsqueeze(1).broadcast_to([128, NT, H]), ALU.add))
            dve.wait_ge(s2, 2)
            link(vec.tensor_scalar(dt_all[:], dt_all[:], 1e9, 1.0, ALU.min, ALU.add))
            dve.wait_ge(s2, 4)
            link(vec.tensor_scalar(dt_all[:], dt_all[:], 1e-4, 0.5, ALU.max, ALU.min))
            link(vec.tensor_scalar(b_all[:], b_all[:], 0.5, 0.5, ALU.mult, ALU.add))
            dve.wait_ge(v2, 3)
            la = link(vec.tensor_tensor(la_all[:], dt_all[:], negA[:].unsqueeze(1).broadcast_to([128, NT, H]), ALU.mult))
            assert la == LA_AT
            dve.wait_ge(v2, 4)
            link(vec.tensor_tensor(g_all[:], b_all[:], dt_all[:], ALU.mult))
            link(vec.tensor_reduce(mdt[:], dt_all[:], AX_X, ALU.add))
            dve.wait_ge(v2, 6)
            assert link(vec.tensor_tensor(b_all[:], dt_all[:], g_all[:], ALU.subtract)) == B_AT
            dve.wait_ge(v2, B_AT)
            mt3 = dt_all
            link(vec.scalar_tensor_tensor(out=mt3[:], in0=small[:, :, 2 * H:], scalar=1.0 / H,
                                          in1=mdt[:].unsqueeze(2).broadcast_to([128, NT, H]), op0=ALU.mult, op1=ALU.mult))
            link(vec.memset(pre3[:, 0:NQ], 0.0))
            for c in range(1, NC_):
                dve.wait_ge(v2, chain[0])
                n = link(vec.tensor_tensor(pre3[:, NQ * c:NQ * c + NQ], pre3[:, NQ * c - NQ:NQ * c],
                                           mt3[:, NQ * c - NQ:NQ * c], ALU.add))
            assert n == PRE_AT, n
            dve.wait_ge(s2, 10)
            dve.wait_ge(p2, P_B)
            for j in range(2):
                link(vec.tensor_tensor(flat(turns)[:, 512 * j:512 * j + 512], bank[4 + j][:],
                                       flat(g_all)[:, 512 * j:512 * j + 512], ALU.add))
            dve.wait_ge(v2, chain[0])
            assert link(vec.tensor_tensor(eg_all[:], turns[:], eg_all[:], ALU.mult)) == EG_AT
            dve.wait_ge(p2, P_S)
            dve.wait_ge(v2, EG_AT)
            for j in range(2):
                link(vec.tensor_scalar(flat(turns)[:, 512 * j:512 * j + 512], bank[6 + j][:], float(1 / (2 * np.pi)),
                                       MAGIC, ALU.mult, ALU.add))
            dve.wait_ge(v2, chain[0])
            link(vec.tensor_scalar(turns[:], turns[:], MAGIC, None, ALU.subtract))
            dve.wait_ge(v2, chain[0])
            for j in range(2):
                cols = slice(512 * j, 512 * j + 512)
                link(vec.scalar_tensor_tensor(out=flat(ang)[:, cols], in0=flat(turns)[:, cols], scalar=-TWO_PI_HI,
                                              in1=bank[6 + j][:], op0=ALU.mult, op1=ALU.add))
            dve.wait_ge(v2, chain[0])
            link(vec.scalar_tensor_tensor(out=ang[:], in0=turns[:], scalar=-TWO_PI_LO, in1=ang[:], op0=ALU.mult,
                                          op1=ALU.add))
            dve.wait_ge(v2, chain[0])
            link(vec.scalar_tensor_tensor(out=turns[:], in0=ang[:], scalar=-1.0, in1=ang[:], op0=ALU.mult, op1=ALU.max))
            n = link(vec.tensor_scalar(ang_in[:], ang[:], -PI_IN, PI_IN, ALU.max, ALU.min))
            assert n == ANG_AT, n

            def early(n, par, general):
                dve.wait_ge(S["zbc_ps"], n + 1)
                if not isinstance(n, int) or n >= 2:
                    dve.wait_ge(S["prod_ready"], n - 1)
                vec.tensor_tensor(bc[:, par], bank[0][:, 0:G3 * N], bcb_sb[:], ALU.mult).then_inc(S["bc_ready"], 1)
                dve.wait_ge(S["bc_ready"], n + 1)
                vec.tensor_tensor(rot[:], bc[:, par].rearrange("p (g a n) -> p g a n", g=G3, a=2).unsqueeze(3)
                                  .broadcast_to([128, G3, 2, 2, H]),
                                  at(cs_all, n).rearrange("p (a j n) -> p a j n", a=2, j=2).unsqueeze(1)
                                  .broadcast_to([128, G3, 2, 2, H]), ALU.mult).then_inc(S["rotated"], 1)
                dve.wait_ge(S["prod_ready"], n + 1)
                vec.tensor_reduce(cb[:], prod[:], AX_X, ALU.add).then_inc(S["cb_ready"], 1)
                dve.wait_ge(S["rotated"], n + 1)
                if not isinstance(n, int) or n >= 2:
                    if general:
                        dve.wait_ge(G["p_ps"], (n - 1) * L)
                    else:
                        dve.wait_ge(S["y_ps"], n - 1)
                for h in range(2):
                    rows = slice(64 * h, 64 * h + 64)
                    vec.tensor_tensor(dup[rows, par, :, h, :].rearrange("p g (j n) -> p g j n", j=2),
                                      rot[rows, :, 0], rot[rows, :, 1], ALU.add).then_inc(S[f"dup{h}"], 1)
                dve.wait_ge(S["x_silu"], n + 1)
                dve.wait_ge(S["w_ready"], n + 1)
                vec.tensor_tensor(x1[:, par].rearrange("p (a e) -> p a e", e=P),
                                  xs[:, par].rearrange("p (a e) -> p a e", e=P),
                                  wx[:, par].rearrange("p h r -> p (h r)").unsqueeze(2).broadcast_to([128, H * R, P]),
                                  ALU.mult).then_inc(S["x1_ready"], 1)
                dve.wait_ge(S["d0_ready"], n + 1)
                dve.wait_ge(S["dg_ready"], n)
                vec.scalar_tensor_tensor(out=d1[:].rearrange("p (h e) -> p h e", e=P),
                                         in0=xs[:, par].rearrange("p (h r e) -> p r h e", r=R, e=P)[:, 1],
                                         scalar=cbr[:, par, 1:2], in1=d0[:].rearrange("p (h e) -> p h e", e=P),
                                         op0=ALU.mult, op1=ALU.add).then_inc(S["d1_ready"], 1)

            def mask(n):
                dve.wait_ge(S["sg_ps"], n + 1)
                vec.tensor_tensor(sg[:], bank[3][:, 0:R * 128].rearrange("p (r m) -> p r m", r=R),
                                  c_("strict").unsqueeze(1).broadcast_to([128, R, 128]), ALU.mult)\
                    .then_inc(S["sg_ready"], 1)

            def state(i, q):
                dve.wait_ge(S["p_ps"], i + 1)
                dve.wait_ge(S["st_ready"], i)
                vec.tensor_tensor(sp[:], bank[5][:, 0:DI], st[:, q], ALU.add).then_inc(S["p_added"], 1)

            def outputs(i, par, general):
                by_head = lambda a: a.rearrange("p (h e) -> p h e", e=P)
                if not general:
                    dve.wait_ge(S["y_ps"], i + 1)
                    vec.tensor_tensor(by_head(ya[:]), by_head(bank[4][:, 0:DI]),
                                      at(ec_all, i).unsqueeze(2).broadcast_to([128, H, P]), ALU.mult)\
                        .then_inc(S["ya_ready"], 1)
                    dve.wait_ge(S["ya_ready"], i + 1)
                dve.wait_ge(S["dg_ready"], i + 1)
                dve.wait_ge(S["y_ready"], i)
                vec.tensor_tensor(ys[:], (yk if general else ya)[:], dg[:, par], ALU.add).then_inc(S["ys_ready"], 1)

            def tokens_general(i, q, par):
                dve.wait_ge(S["ys_ready"], i)
                dve.wait_ge(S["x1_ready"], i + 1)
                vec.memset(yk[:], 0.0).then_inc(G["zero"], 1)
                def token(t):
                    n = i * L + t
                    hot = cm[:, CONSTS.index("hot"), bass.ds(t, 1) if not isinstance(t, int) else slice(t, t + 1)]
                    wait_past(dve, G["fk_ps"], n)
                    vec.tensor_scalar(oh[:, 0], c_("ones"), hot, None, ALU.mult).then_inc(G["oh"], 1)
                    wait_past(dve, G["p_ps"], n)
                    vec.tensor_scalar(xk[:, 0], x1[:, par], hot, None, ALU.mult).then_inc(G["x1k"], 1)
                    dve.wait_ge(G["fk_ps"], n + 1)
                    vec.tensor_copy(fk[:], bank[3][:, 0:H]).then_inc(G["fk_sb"], 1)
                    dve.wait_ge(G["fk_sb"], n + 1)
                    wait_past(dve, G["st"], n)
                    wait_past(dve, G["y_ps"], n)
                    vec.tensor_tensor(sk[:].rearrange("p (h e) -> p h e", e=P), st[:, q].rearrange("p (h e) -> p h e", e=P),
                                      fk[:].unsqueeze(2).broadcast_to([128, H, P]), ALU.mult).then_inc(G["s1"], 1)
                    dve.wait_ge(G["y_ps"], n + 1)
                    wait_past(dve, G["yk"], n)
                    dve.wait_ge(G["zero"], i + 1)
                    vec.scalar_tensor_tensor(out=yk[:], in0=bank[4][:, 0:DI], scalar=hot, in1=yk[:], op0=ALU.mult,
                                             op1=ALU.add).then_inc(G["yk"], 1)
                    dve.wait_ge(G["p_ps"], n + 1)
                    dve.wait_ge(G["s1"], n + 1)
                    vec.tensor_tensor(st[:, q], bank[5][:, 0:DI], sk[:], ALU.add).then_inc(G["st"], 1)

                steps(dve, L, token, first=1 if isinstance(i, int) and i == 0 else 0)
                dve.wait_ge(G["yk"], (i + 1) * L)

            def stats(i):
                vec.bn_stats(at(ost_all, i), at(o_all, i)).then_inc(S["ost_done"], 1)

            def step(i, q, general, first=False, last=False):
                par, other = q % 2, (q + 1) % 2
                if general:
                    tokens_general(i, q, par)
                if not first:
                    dve.wait_ge(S["o_sb"], i - 1)
                if not last:
                    early(i + 1, other, general)
                if not general:
                    state(i, q)
                outputs(i, par, general)
                if not first:
                    stats(i - 2)
                if not last and not general:
                    mask(i + 1)

            def tiles(general):
                early(0, 0, general)
                if not general:
                    mask(0)
                for q in range(NQ):
                    step(q, q, general, first=(q < 2))
                with dve.Fori(1, NC_ - 1) as c:
                    for q in range(NQ):
                        step(c * NQ + q, q, general)
                for q in range(NQ):
                    step((NC_ - 1) * NQ + q, q, general, last=(q == NQ - 1))
                dve.wait_ge(S["o_sb"], NT)
                stats(NT - 2)
                stats(NT - 1)

            dve.wait_ge(s2, TABLES_AT)
            dve.wait_ge(s_w2, 16 * 6)
            dve.wait_ge(S["st_zero"], 3)
            fl = dve.value_load(flag_i[0:1, 0:1], min_val=0, max_val=1)
            with dve.If(fl > 0):
                tiles(False)
            with dve.Else():
                tiles(True)

            dve.wait_ge(S["ost_done"], NT)
            dve.wait_ge(S["ysq_done"], NT)
            moments(dve, ost_all, tokc, NT, fac_v, 0, 0.0)
            dve.wait_ge(fac_v, MOM)
            vec.scalar_tensor_tensor(out=tokc[:, 1], in0=ysq_all[:, :, 0], scalar=EPS_LN, in1=tokc[:, 5], op0=ALU.mult,
                                     op1=ALU.add).then_inc(fac_v, 1)
            vec.tensor_scalar(tokc[:, 2], csq_all[:, :, 0], EPS_RMS, EPS_LN * EPS_RMS * SCALE2_INV, ALU.add, ALU.mult)\
                .then_inc(fac_v, 1)
            dve.wait_ge(fac_v, MOM + 2)
            vec.tensor_tensor(tokc[:, 6], tokc[:, 1], tokc[:, 2], ALU.add).then_inc(fac_v, 1)
            dve.wait_ge(fac_p, NT // 8)
            vec.scalar_tensor_tensor(out=tokc[:, 3], in0=tokc[:, 0], scalar=-0.5, in1=tokc[:, 7], op0=ALU.mult,
                                     op1=ALU.mult).then_inc(fac_v, 1)
            dve.wait_ge(fac_v, FAC_POW + 1)
            cst = tokc[:, 3, :]
            def chunk(cc):
                for par in range(2):
                    c = cc * 2 + par
                    for q in range(NQ):
                        i = c * NQ + q
                        vec.scalar_tensor_tensor(out=xr[:, par, q], in0=at(o_all, i), scalar=tokc[:, 7, bass.ds(i, 1)],
                                                 in1=at(x_all, i), op0=ALU.mult, op1=ALU.add).then_inc(C["x1"], 1)
                    for q in range(NQ):
                        dve.wait_ge(C["x1"], c * NQ + q + 1)
                        vec.bn_stats(fst[:, q], xr[:, par, q]).then_inc(C["stats"], 1)
                    dve.wait_ge(C["stats"], (c + 1) * NQ)
                    moments(dve, fst, fmo, NQ, C["mom"], c * MOM, EPS_LN)
                    dve.wait_ge(C["pow"], c + 1)
                    wait_past(dve, C["normed"], c * NQ)
                    vec.scalar_tensor_tensor(out=fnb[:], in0=fmo[:, 0], scalar=-0.5, in1=frs[:, 0], op0=ALU.mult,
                                             op1=ALU.mult).then_inc(C["norm_bias"], 1)
                    wait_past(dve, C["delta"], c)
                    vec.tensor_copy(x2T[:, par, :, 0:1], x2T[:, 1 - par, :, L:L + 1]).then_inc(C["carried"], 1)
                    dve.wait_ge(C["delta"], c + 1)
                    prev = x2T[:, par, :, 0:L]
                    for mix_, m, dst, reader in ((C["mix_k"], 1, xkm, C["k_ps"]), (C["mix_r"], 0, xrm, C["r_ps"])):
                        wait_past(dve, reader, c)
                        vec.scalar_tensor_tensor(out=dst[:].rearrange("p (b l) -> p b l", b=B),
                                                 in0=dl[:].rearrange("p (b l) -> p b l", b=B), scalar=mu_sb[:, m:m + 1],
                                                 in1=prev, op0=ALU.mult, op1=ALU.add).then_inc(mix_, 1)
                    dve.wait_ge(C["k_relu"], c + 1)
                    wait_past(dve, C["v_ps"], c)
                    vec.tensor_tensor(ka[:], bank[1][:], kr[:], ALU.mult).then_inc(C["k_act"], 1)
                    dve.wait_ge(C["th"], c + 1)
                    dve.wait_ge(C["v_ps"], c + 1)
                    for q in range(NQ):
                        vec.scalar_tensor_tensor(out=ff[:, q], in0=th[:, q], scalar=1.0, in1=bank[3][:, q * D:q * D + D],
                                                 op0=ALU.add, op1=ALU.mult).then_inc(C["f"], 1)
                    for q in range(NQ):
                        dve.wait_ge(C["f"], c * NQ + q + 1)
                        vec.bn_stats(fst[:, q], ff[:, q]).then_inc(C["stats3"], 1)
                    dve.wait_ge(C["stats3"], (c + 1) * NQ)
                    moments(dve, fst, fmo, NQ, C["mom3"], c * MOM, 4 * EPS_LN)
                    dve.wait_ge(C["pow3"], c + 1)
                    wait_past(dve, C["outv"], c * NQ)
                    vec.scalar_tensor_tensor(out=frs3[:], in0=fmo[:, 0], scalar=-0.5, in1=frs[:, 1], op0=ALU.mult,
                                             op1=ALU.mult).then_inc(C3, 1)
                    for q in range(NQ):
                        vec.scalar_tensor_tensor(out=f2[:, q], in0=ff[:, q], scalar=frs[:, 1, q:q + 1],
                                                 in1=xr[:, par, q], op0=ALU.mult, op1=ALU.add).then_inc(C["res"], 1)
                    dve.wait_ge(C3, c + 1)
                    vec.tensor_tensor(fnb3[:], frs3[:], tokc[:, 3, bass.ds(c * NQ, NQ)], ALU.add).then_inc(C["bias3"], 1)

            steps(dve, NC_ // 2, chunk)


def kernel(L0_attn_x, L0_attn_W_in, L0_attn_A_log, L0_attn_dt_bias, L0_attn_B_norm_bias, L0_attn_C_norm_bias,
           L0_attn_W_out, L0_ffn_W_r, L0_ffn_W_k, L0_ffn_W_v, L0_ffn_mu_r, L0_ffn_mu_k):
    import concourse.bacc as bacc
    from concourse.bass_utils import run_bass_kernel_spmd

    w = np.asarray(L0_attn_W_in)
    z, xr, bcw, rest = w[:, :DI], w[:, DI:DI + DI * R], w[:, DI * (1 + R):DI * (1 + R) + G3 * N], w[:, -NS:]
    bb, cb = np.asarray(L0_attn_B_norm_bias).reshape(-1), np.asarray(L0_attn_C_norm_bias).reshape(-1)
    arrays = {
        "x": np.asarray(L0_attn_x),
        "w_in": np.concatenate([bcw, z, xr, rest], axis=1),
        "a_log": np.asarray(L0_attn_A_log),
        "dt_bias": np.asarray(L0_attn_dt_bias),
        "bc_bias": np.concatenate([bb, bb, cb]),
        "w_out": np.asarray(L0_attn_W_out),
        "w_r": np.asarray(L0_ffn_W_r).T,
        "w_k": np.asarray(L0_ffn_W_k).T,
        "w_v": np.asarray(L0_ffn_W_v).T,
        "mu": np.stack([np.asarray(L0_ffn_mu_r), np.asarray(L0_ffn_mu_k)], axis=1),
        "consts": constants(),
    }
    arrays = {n: np.ascontiguousarray(a) for n, a in arrays.items()}
    nc = bacc.Bacc("TRN2", target_bir_lowering=False, num_devices=1)
    args = [nc.dram_tensor(n, a.shape, mybir.dt.from_np(a.dtype), kind="ExternalInput").ap() for n, a in arrays.items()]
    out = nc.dram_tensor("out", (B, T, D), F32, kind="ExternalOutput").ap()
    build(nc, *args, out)
    r = run_bass_kernel_spmd(nc, [arrays], core_ids=[0])
    return r.results[0]["out"]
```

```python
from contextlib import ExitStack

import numpy as np

import concourse.bass as bass
from concourse import mybir

F32 = mybir.dt.float32
I32 = mybir.dt.int32
ALU = mybir.AluOpType
ACT = mybir.ActivationFunctionType
AX_X = mybir.AxisListType.X

B, T, D = 8, 512, 128
L = 64
NC_ = T // L
NQ = B // 2
NT = NC_ * NQ
H, P, R, N = 32, 8, 2, 64
DI = H * P
G3 = R + 1
O_BC, O_Z, O_X, O_S = 0, G3 * N, G3 * N + DI, G3 * N + DI + DI * R
NS = 3 * H
WCOLS = O_S + NS
AK = 8
MAX_A = 68.0 / (0.5 * L / 2)
EPS_LN, EPS_RMS = 1e-5, 1e-6
SCALE2_INV = float(N * R)
MAGIC = 1.5 * 2.0 ** 23
TWO_PI_HI = 6.28125
TWO_PI_LO = float(2 * np.pi - 6.28125)
PI_IN = 3.1415925

MOM = 6
FLAG_AT = 6
LA_AT, B_AT, PRE_AT, EG_AT, ANG_AT = 5, 8, 17, 20, 28
F_AT, TABLES_AT = 10, 15
P_B, P_CUM, P_F, P_S = 2, 4, 6, 8
FAC_POW = MOM + 3

CONSTS = ["ident", "strict", "tri", "ones", "centre", "late", "early", "shift", "edge", "hot"]


def constants():
    k, m = np.arange(128)[:, None], np.arange(128)[None, :]
    same, kl, ml = k // L == m // L, k % L, m % L
    mid = L // 2 - 1
    mats = {
        "ident": k == m,
        "strict": same & (kl < ml),
        "tri": same & (kl <= ml),
        "ones": same,
        "late": same & (kl > mid),
        "early": same & (kl <= mid),
        "shift": same & (kl == ml + 1),
        "edge": same & (kl == 0) & (ml == L - 1),
        "hot": (kl == m) & (m < L),
    }
    mats = {n: v.astype(np.float32) for n, v in mats.items()}
    mats["centre"] = mats["tri"] - mats["early"]
    return np.concatenate([mats[n] for n in CONSTS], axis=1).astype(np.float32)


def build(nc, x, w_in, a_log, dt_bias, bc_bias, w_out, w_r, w_k, w_v, mu, consts, out, force_general=False):
    ctx = ExitStack()
    with ctx:
        def sb(name, *shape, dt=F32):
            return ctx.enter_context(nc.sbuf_tensor(name, list(shape), dt))

        def sem(name):
            return ctx.enter_context(nc.semaphore(name))

        def at(buf, i):
            if isinstance(i, int):
                return buf[:, i, :]
            return buf[:, bass.ds(i, 1), :].rearrange("p a n -> p (a n)")

        def wait_past(eng, semaphore, value):
            if not isinstance(value, int) or value > 0:
                eng.wait_ge(semaphore, value)

        def steps(eng, n, body, first=1):
            for k in range(first):
                body(k)
            with eng.Fori(first, n) as k:
                body(k)

        x_all = sb("x_all", 128, NT, D)
        xnT_all = sb("xnT_all", 128, NT, 128)
        o_all = sb("o_all", 128, NT, D)
        w_sb = sb("w_sb", 128, WCOLS)
        cm = sb("cm", 128, len(CONSTS), 128)
        wo_sb = sb("wo_sb", 128, 2, D)
        wr_sb = sb("wr_sb", 128, D)
        wk_sb = sb("wk_sb", 128, D)
        wv_sb = sb("wv_sb", 128, D)
        mu_sb = sb("mu_sb", 128, 2)
        one_less_mu = sb("one_less_mu", 128, 2)
        dtb_sb = sb("dtb_sb", 128, H)
        negA = sb("negA", 128, H)
        bcb_sb = sb("bcb_sb", 128, G3 * N)
        flag = sb("flag", 128, 4)
        flag_i = sb("flag_i", 128, 1, dt=I32)
        small = sb("small", 128, NT, NS)
        dt_all = sb("dt_all", 128, NT, H)
        g_all = sb("g_all", 128, NT, H)
        b_all = sb("b_all", 128, NT, H)
        la_all = sb("la_all", 128, NT, H)
        ec_all = sb("ec_all", 128, NT, H)
        eg_all = sb("eg_all", 128, NT, H)
        f_all = sb("f_all", 128, NT, H)
        cs_all = sb("cs_all", 128, NT, 4 * H)
        ost_all = sb("ost_all", 128, NT, 6)
        ysq_all = sb("ysq_all", 128, NT, 1)
        csq_all = sb("csq_all", 128, NT, 1)
        tokc = sb("tokc", 128, 8, NT)
        halfn = sb("halfn", 128, 8)
        epst = sb("epst", 128, 4)
        one = sb("one", 128, 1)

        bank = [ctx.enter_context(nc.psum_tensor(f"bank{n}", [128, 512], F32)) for n in range(8)]

        def c_(name):
            return cm[:, CONSTS.index(name), :]

        s_x = [sem(f"x_loaded{k}") for k in range(4)]
        s_w = sem("w_in_loaded")
        s_w2 = sem("other_weights_loaded")
        s_a = sem("decay_inputs_loaded")
        s_c = sem("consts_loaded")
        s_ones = sem("fills_done")
        prep = sem("prep_vector")

        bn8 = sb("bn8", 128, AK, 6)
        mo8 = sb("mo8", 128, 6, AK)
        rs8 = sb("rs8", 128, AK)
        xn8 = sb("xn8", 128, AK, D)
        xt8 = sb("xt8", 128, AK, 128)
        a_st, a_mo, a_rs, a_xn, a_tr, a_ev, a_mm, a_sm = (sem(n) for n in (
            "a_stats", "a_moments", "a_rstd", "a_normed", "a_transposed", "a_evacuated", "a_projected", "a_small"))
        v2, s2, p2 = sem("tables_vector"), sem("tables_scalar"), sem("tables_tensor")

        mean8 = sem("a_means")
        halfpi = sb("halfpi", 128, 1)
        mdt = sb("mdt", 128, NT)

        def scratch(n):
            return o_all[:].rearrange("p t d -> p (t d)")[:, n * NT * H:(n + 1) * NT * H]\
                .rearrange("p (t h) -> p t h", h=H)

        pre3 = scratch(0)
        turns = scratch(1)
        ang = scratch(2)
        ang_in = scratch(3)

        def flat(buf):
            return buf[:].rearrange("p t h -> p (t h)")

        xt = sb("xt", 128, 2, 128)
        bc = sb("bc", 128, 2, G3 * N)
        rot = sb("rot", 128, G3, 2, 2, H)
        dup = sb("dup", 128, 2, G3, 2, N)
        xs = sb("xs", 128, 2, DI * R)
        zs = sb("zs", 128, 2, DI)
        junk = sb("junk", 128, G3 * N)
        junk_y = sb("junk_y", 128, DI)
        msb = sb("msb", 128, 2, R)
        mse = sb("mse", 128, R)
        rb = sb("rb", 128, 2, R)
        wx = sb("wx", 128, 2, H, R)
        x1 = sb("x1", 128, 2, DI * R)
        prod = sb("prod", 128, R, N)
        cb = sb("cb", 128, R)
        cbr = sb("cbr", 128, 2, R)
        d0 = sb("d0", 128, DI)
        d1 = sb("d1", 128, DI)
        dg = sb("dg", 128, 2, DI)
        bt = sb("bt", 128, G3, 128)
        sg = sb("sg", 128, R, 128)
        st = sb("st", 128, NQ, DI)
        sp = sb("sp", 128, DI)
        ya = sb("ya", 128, DI)
        ys = sb("ys", 128, DI)
        y = sb("y", 128, 2, DI)
        yt = sb("yt", 128, 2, 128)
        oh = sb("oh", 128, 2, 128)
        xk = sb("xk", 128, 2, DI * R)
        fk = sb("fk", 128, H)
        sk = sb("sk", 128, DI)
        yk = sb("yk", 128, DI)

        names = ("xt_copied zbc_ps x_ps bc_ready rotated dup0 dup1 x_silu z_silu sq_done mse_ready rb_ready w_ready "
                 "x1_ready prod_ready cb_ready cbr_ready d0_ready d1_ready dg_ready t_ps t_sb sg_ps sg_ready p_ps "
                 "p_added st_ready y_ps ya_ready ys_ready y_ready ysq_done yt_ps yt_sb o_ps o_sb ost_done st_zero").split()
        S = {n: sem(n) for n in names}
        G = {n: sem("g_" + n) for n in ("oh x1k fk_ps fk_sb s1 y_ps yk p_ps st zero done".split())}

        fst = sb("fst", 128, 2 * NQ, 6)
        fmo = sb("fmo", 128, 6, 2 * NQ)
        frs = sb("frs", 128, 2 * NQ)
        fnb = sb("fnb", 128, 2 * NQ)
        mean_o = sb("mean_o", 128, NQ)
        fnb3 = sb("fnb3", 128, NQ)
        xn2 = sb("xn2", 128, NQ, D)
        curT = sb("curT", 128, 2, B, L)
        prevT = sb("prevT", 128, B, L)
        w_cur = sb("w_cur", 128, 2, D)
        w_prev = sb("w_prev", 128, 2, D)
        kr = sb("kr", 128, B * L)
        ka = sb("ka", 128, B * L)
        th = sb("th", 128, NQ, D)
        wv_half = sb("wv_half", 128, D)
        ff = sb("ff", 128, NQ, D)
        f2 = sb("f2", 128, NQ, D)
        cnames = ("x1 stats mom pow norm_bias normed tr_ps tr_sb carried shifted k_ps k_relu k_act r_ps th v_ps "
                  "f stats3 means res bias3 outv").split()
        C = {n: sem("c_" + n) for n in cnames}
        s_mix = sem("mixing_weights")
        stored = sem("stored")
        fac_v, fac_p = sem("factors_vector"), sem("factors_pool")

        def chunks(eng, body):
            for k in range(2):
                body(k, k % 2)
            with eng.Fori(1, NC_ // 2 - 1) as cc:
                for par in range(2):
                    body(cc * 2 + par, par)
            for k in range(NC_ - 2, NC_ + 2):
                body(k, k % 2)

        def has(k, back=0):
            return not isinstance(k, int) or 0 <= k - back < NC_

        def upto(k):
            return min(k, NC_) if isinstance(k, int) else k

        def norms(k):
            return slice(0 if has(k) else NQ, 2 * NQ if has(k, 2) else NQ)

        def moments(dve, stats, mo, n, chain, base, eps):
            n = n if isinstance(n, slice) else slice(0, n)
            even, odd = stats[:, n, 1], stats[:, n, 4]
            nc.vector.tensor_tensor(mo[:, 0, n], even, odd, ALU.add).then_inc(chain, 1)
            nc.vector.tensor_tensor(mo[:, 1, n], even, odd, ALU.subtract).then_inc(chain, 1)
            nc.vector.tensor_tensor(mo[:, 2, n], stats[:, n, 2], stats[:, n, 5], ALU.add).then_inc(chain, 1)
            dve.wait_ge(chain, base + 2)
            nc.vector.tensor_tensor(mo[:, 3, n], mo[:, 1, n], mo[:, 1, n], ALU.mult).then_inc(chain, 1)
            dve.wait_ge(chain, base + 4)
            nc.vector.scalar_tensor_tensor(out=mo[:, 4, n], in0=mo[:, 3, n], scalar=float(D // 4),
                                           in1=mo[:, 2, n], op0=ALU.mult, op1=ALU.add).then_inc(chain, 1)
            dve.wait_ge(chain, base + 5)
            nc.vector.tensor_scalar(mo[:, 5, n], mo[:, 4, n], 1.0 / D, float(eps), ALU.mult, ALU.add).then_inc(chain, 1)

        block = ctx.enter_context(nc.Block())

        @block.sync
        def _(sp_):
            for k in range(NC_ // 2):
                for h in range(2):
                    for q in range(0, NQ, 1):
                        (sp_ if q % 2 else sp_).dma_start(
                            x_all[64 * h:64 * h + 64, 8 * k + q:8 * k + q + 5:4, :],
                            x[2 * q + h, 2 * k * L:2 * (k + 1) * L, :].rearrange("(c l) d -> l c d", l=L),
                        ).then_inc(s_x[k], 16)
            with sp_.Fori(0, NC_) as c:
                sp_.wait_ge(C["outv"], (c + 1) * NQ)
                for h in range(2):
                    sp_.dma_start(
                        out.rearrange("(q h) (c l) d -> h c l q d", h=2, l=L)[h, bass.ds(c, 1)]
                        .rearrange("a l q d -> (a l) q d"),
                        o_all[64 * h:64 * h + 64, bass.ds(c * NQ, NQ)]).then_inc(stored, 16)
            sp_.wait_ge(stored, 2 * 16 * NC_)

        @block.gpsimd
        def _(pool):
            for dst, src in ((wo_sb[:], w_out.rearrange("(k p) n -> p k n", p=128)), (wr_sb[:], w_r), (wk_sb[:], w_k),
                             (wv_sb[:], w_v), (mu_sb[:], mu), (bcb_sb[:], bc_bias.partition_broadcast(128))):
                pool.dma_start(dst, src).then_inc(s_w2, 16)
            nc.gpsimd.memset(halfn[:], -0.5).then_inc(s_ones, 1)
            nc.gpsimd.memset(epst[:], EPS_RMS).then_inc(s_ones, 1)
            nc.gpsimd.memset(one[:], 1.0).then_inc(s_ones, 1)
            nc.gpsimd.memset(st[:], 0.0).then_inc(S["st_zero"], 1)
            nc.gpsimd.memset(dup[:], 0.0).then_inc(S["st_zero"], 1)
            nc.gpsimd.memset(curT[:, 1], 0.0).then_inc(S["st_zero"], 1)
            pool.wait_ge(s_ones, 3)
            with pool.Fori(0, NT // AK) as k:
                pool.wait_ge(a_mo, (k + 1) * MOM)
                nc.gpsimd.tensor_tensor(rs8[:], mo8[:, 5, :], halfn[:, 0:AK], ALU.pow).then_inc(a_rs, 1)

            def early(n, par):
                pool.wait_ge(S["bc_ready"], n + 1)
                pool.wait_ge(S["cb_ready"], n)
                nc.gpsimd.tensor_tensor(prod[:], bc[:, par, 0:R * N].rearrange("p (r n) -> p r n", r=R),
                                        bc[:, par, R * N:].unsqueeze(1).broadcast_to([128, R, N]),
                                        ALU.mult).then_inc(S["prod_ready"], 1)
                pool.wait_ge(S["sq_done"], n + 1)
                nc.gpsimd.tensor_tensor(mse[:], msb[:, par], epst[:, 0:R], ALU.add).then_inc(S["mse_ready"], 1)
                pool.wait_ge(S["mse_ready"], n + 1)
                nc.gpsimd.tensor_tensor(rb[:, par], mse[:], halfn[:, 0:R], ALU.pow).then_inc(S["rb_ready"], 1)
                pool.wait_ge(S["rb_ready"], n + 1)
                if not isinstance(n, int) or n >= 2:
                    pool.wait_ge(S["x1_ready"], n - 1)
                nc.gpsimd.tensor_tensor(wx[:, par], at(eg_all, n).unsqueeze(2).broadcast_to([128, H, R]),
                                        rb[:, par].unsqueeze(1).broadcast_to([128, H, R]),
                                        ALU.mult).then_inc(S["w_ready"], 1)
                pool.wait_ge(S["cb_ready"], n + 1)
                if not isinstance(n, int) or n >= 2:
                    pool.wait_ge(S["d1_ready"], n - 1)
                nc.gpsimd.tensor_tensor(cbr[:, par], cb[:], rb[:, par], ALU.mult).then_inc(S["cbr_ready"], 1)
                pool.wait_ge(S["d1_ready"], n + 1)
                if not isinstance(n, int) or n >= 2:
                    pool.wait_ge(S["ys_ready"], n - 1)
                nc.gpsimd.tensor_tensor(dg[:, par].rearrange("p (h e) -> p h e", e=P),
                                        d1[:].rearrange("p (h e) -> p h e", e=P),
                                        at(g_all, n).unsqueeze(2).broadcast_to([128, H, P]),
                                        ALU.mult).then_inc(S["dg_ready"], 1)

            def late(i, q, par, general):
                if not general:
                    pool.wait_ge(S["p_added"], i + 1)
                    pool.wait_ge(S["y_ps"], i + 1)
                    nc.gpsimd.tensor_tensor(st[:, q].rearrange("p (h e) -> p h e", e=P),
                                            sp[:].rearrange("p (h e) -> p h e", e=P),
                                            at(f_all, i).unsqueeze(2).broadcast_to([128, H, P]),
                                            ALU.mult).then_inc(S["st_ready"], 1)
                pool.wait_ge(S["ys_ready"], i + 1)
                pool.wait_ge(S["z_silu"], i + 1)
                if not isinstance(i, int) or i >= 2:
                    pool.wait_ge(S["yt_ps"], i - 1)
                    pool.wait_ge(S["ysq_done"], i - 1)
                nc.gpsimd.tensor_tensor(y[:, par], ys[:], zs[:, par], ALU.mult).then_inc(S["y_ready"], 1)

            def tiles(general):
                early(0, 0)
                for q in range(NQ):
                    early(q + 1, (q + 1) % 2)
                    late(q, q, q % 2, general)
                with pool.Fori(1, NC_ - 1) as c:
                    for q in range(NQ):
                        early(c * NQ + q + 1, (q + 1) % 2)
                        late(c * NQ + q, q, q % 2, general)
                for q in range(NQ):
                    if q < NQ - 1:
                        early((NC_ - 1) * NQ + q + 1, (q + 1) % 2)
                    late((NC_ - 1) * NQ + q, q, q % 2, general)

            pool.wait_ge(prep, FLAG_AT)
            pool.wait_ge(v2, EG_AT)
            pool.wait_ge(s2, F_AT)
            fl = pool.value_load(flag_i[0:1, 0:1], min_val=0, max_val=1)
            with pool.If(fl > 0):
                tiles(False)
            with pool.Else():
                tiles(True)

            def factors(c):
                nc.gpsimd.tensor_tensor(tokc[:, 7, c * NQ:c * NQ + NQ], tokc[:, 6, c * NQ:c * NQ + NQ], halfn[:, 0:NQ],
                                        ALU.pow).then_inc(fac_p, 1)

            pool.wait_ge(fac_v, FAC_POW)
            factors(0)
            factors(1)

            def chunk(k, par):
                n = norms(k)
                pool.wait_ge(C["mom"], (k + 1) * MOM)
                wait_past(pool, C["normed"], upto(k) * NQ)
                if has(k, 2):
                    wait_past(pool, C["res"], (k - 2) * NQ)
                nc.gpsimd.tensor_tensor(frs[:, n], fmo[:, 5, n], halfn[:, n], ALU.pow).then_inc(C["pow"], 1)
                if has(k):
                    wait_past(pool, C["r_ps"], k)
                    nc.gpsimd.tensor_tensor(prevT[:, :, 0:1], curT[:, 1 - par, :, L - 1:L],
                                            one[:].unsqueeze(1).broadcast_to([128, B, 1]), ALU.mult).then_inc(C["carried"], 1)
                if isinstance(k, int) and k < 2:
                    for c in range(3 * k + 2, 3 * k + 5):
                        factors(c)

            chunks(pool, chunk)

        @block.scalar
        def _(act):
            act.dma_start(negA[:], a_log.partition_broadcast(128)).then_inc(s_a, 16)
            act.dma_start(dtb_sb[:], dt_bias.partition_broadcast(128)).then_inc(s_a, 16)
            act.dma_start(cm[:], consts.rearrange("p (n m) -> p n m", m=128)).then_inc(s_c, 16)
            act.dma_start(w_sb[:, O_S:], w_in[:, O_S:]).then_inc(s_w, 16)
            act.dma_start(w_sb[:, 0:O_S], w_in[:, 0:O_S]).then_inc(s_w, 16)
            act.wait_ge(s_a, 32)
            nc.scalar.activation(negA[:], negA[:], ACT.Exp).then_inc(s2, 1)
            def first_phase(k):
                for j in range(2):
                    act.wait_ge(a_tr, k * 2 + j + 1)
                    wait_past(act, a_mm, k * 2 + j)
                    nc.scalar.activation(xt8[:, 4 * j:4 * j + 4], bank[j][:], ACT.Copy).then_inc(a_ev, 1)
                for j in range(2):
                    act.wait_ge(a_ev, k * 2 + j + 1)
                    nc.scalar.activation(xnT_all[:, bass.ds(k * AK + 4 * j, 4)], xt8[:, 4 * j:4 * j + 4],
                                         ACT.Copy).then_inc(a_sm, 1)
                    act.wait_ge(a_mm, k * 2 + j + 1)
                    nc.scalar.activation(small[:, bass.ds(k * AK + 4 * j, 4)],
                                         bank[2 + j][:, 0:4 * NS].rearrange("p (t s) -> p t s", t=4),
                                         ACT.Copy).then_inc(a_sm, 1)

            steps(act, NT // AK, first_phase)
            act.wait_ge(v2, 1)
            nc.scalar.activation(dt_all[:], dt_all[:], ACT.Exp).then_inc(s2, 1)
            act.wait_ge(a_sm, 4 * NT // AK)
            nc.scalar.activation(b_all[:], small[:, :, H:2 * H], ACT.Tanh, scale=0.5).then_inc(s2, 1)
            act.wait_ge(v2, 2)
            nc.scalar.activation(dt_all[:], dt_all[:], ACT.Ln).then_inc(s2, 1)
            act.wait_ge(prep, FLAG_AT)
            for j in range(2):
                act.wait_ge(p2, P_CUM)
                nc.scalar.activation(ec_all[:, 16 * j:16 * j + 16].rearrange("p t h -> p (t h)"), bank[j][:],
                                     ACT.Exp, scale=flag[:, 0:1]).then_inc(s2, 1)
                nc.scalar.activation(eg_all[:, 16 * j:16 * j + 16].rearrange("p t h -> p (t h)"), bank[j][:],
                                     ACT.Exp, scale=flag[:, 1:2]).then_inc(s2, 1)
            for j in range(2):
                act.wait_ge(p2, P_F)
                nc.scalar.activation(f_all[:, 16 * j:16 * j + 16].rearrange("p t h -> p (t h)"), bank[2 + j][:],
                                     ACT.Exp).then_inc(s2, 1)
            nc.scalar.activation(b_all[:], la_all[:], ACT.Exp).then_inc(s2, 1)
            act.wait_ge(v2, ANG_AT)
            for slot, src, scale, bias in ((0, turns, -1.0, halfpi[:, 0:1]), (3, turns, -1.0, halfpi[:, 0:1]),
                                           (2, ang_in, 1.0, 0.0), (1, ang_in, -1.0, 0.0)):
                nc.scalar.activation(cs_all[:, :, slot * H:slot * H + H], src[:], ACT.Sin, scale=scale,
                                     bias=bias).then_inc(s2, 1)

            def copy_in(n, par):
                if not isinstance(n, int) or n >= 2:
                    act.wait_ge(S["x_ps"], n - 1)
                nc.scalar.activation(xt[:, par], at(xnT_all, n), ACT.Copy).then_inc(S["xt_copied"], 1)

            def squares(n, par):
                act.wait_ge(S["bc_ready"], n + 1)
                if not isinstance(n, int) or n >= 2:
                    act.wait_ge(S["rb_ready"], n - 1)
                act.wait_ge(S["sq_done"], n)
                for r in range(R):
                    nc.scalar.activation(junk[:, r * N:r * N + N], bank[0][:, r * N:r * N + N], ACT.Square,
                                         scale=float(N) ** -0.5, accum_out=msb[:, par, r:r + 1])
                nc.scalar.activation(junk[:, R * N:], bank[0][:, R * N:G3 * N], ACT.Square, scale=float(N) ** -0.5,
                                     accum_out=at(csq_all, n)).then_inc(S["sq_done"], 1)

            def gates(n, par):
                act.wait_ge(S["x_ps"], n + 1)
                if not isinstance(n, int) or n >= 2:
                    act.wait_ge(S["x1_ready"], n - 1)
                    act.wait_ge(S["d1_ready"], n - 1)
                nc.scalar.activation(xs[:, par], bank[1][:], ACT.Silu).then_inc(S["x_silu"], 1)
                if not isinstance(n, int) or n >= 2:
                    act.wait_ge(S["y_ready"], n - 1)
                nc.scalar.activation(zs[:, par], bank[0][:, O_Z:O_Z + DI], ACT.Silu).then_inc(S["z_silu"], 1)

            def turned(n):
                act.wait_ge(S["t_ps"], n + 1)
                nc.scalar.activation(bt[:].rearrange("p g m -> p (g m)"), bank[2][:, 0:G3 * 128],
                                     ACT.Copy).then_inc(S["t_sb"], 1)

            def own_token(n, par):
                act.wait_ge(S["x_silu"], n + 1)
                act.wait_ge(S["cbr_ready"], n + 1)
                act.wait_ge(S["d1_ready"], n)
                nc.scalar.activation(d0[:].rearrange("p (h e) -> p h e", e=P),
                                     xs[:, par].rearrange("p (h r e) -> p r h e", r=R, e=P)[:, 0],
                                     ACT.Copy, scale=cbr[:, par, 0:1]).then_inc(S["d0_ready"], 1)

            def late_yt(i):
                act.wait_ge(S["yt_ps"], i + 1)
                act.wait_ge(S["o_ps"], i)
                nc.scalar.activation(yt[:].rearrange("p k m -> p (k m)"), bank[6][:, 0:DI], ACT.Copy).then_inc(S["yt_sb"], 1)

            def late_ysq(i, par):
                act.wait_ge(S["ysq_done"], i)
                act.wait_ge(S["y_ready"], i + 1)
                nc.scalar.activation(junk_y[:], y[:, par], ACT.Square, scale=float(DI) ** -0.5,
                                     accum_out=at(ysq_all, i)).then_inc(S["ysq_done"], 1)

            def late_o(i):
                act.wait_ge(S["o_ps"], i + 1)
                nc.scalar.activation(at(o_all, i), bank[7][:, 0:D], ACT.Copy).then_inc(S["o_sb"], 1)

            def step(i, q, ahead=2, behind=True):
                par, other = q % 2, (q + 1) % 2
                if ahead >= 1:
                    squares(i + 1, other)
                if behind:
                    late_yt(i - 1)
                if ahead >= 1:
                    gates(i + 1, other)
                    turned(i + 1)
                    own_token(i + 1, other)
                if behind:
                    late_ysq(i - 1, other)
                if ahead >= 2:
                    copy_in(i + 2, par)
                if behind:
                    late_o(i - 1)

            copy_in(0, 0)
            copy_in(1, 1)
            act.wait_ge(S["st_zero"], 3)
            squares(0, 0)
            gates(0, 0)
            turned(0)
            own_token(0, 0)
            for q in range(NQ):
                step(q, q, behind=q > 0)
            with act.Fori(1, NC_ - 1) as c:
                for q in range(NQ):
                    step(c * NQ + q, q)
            for q in range(NQ):
                step((NC_ - 1) * NQ + q, q, ahead=min(2, NQ - 1 - q))
            late_yt(NT - 1)
            late_ysq(NT - 1, (NT - 1) % 2)
            late_o(NT - 1)

            def chunk(k, par):
                if has(k):
                    act.wait_ge(C["norm_bias"], k + 1)
                    wait_past(act, C["tr_ps"], k)
                    for q in range(NQ):
                        nc.scalar.activation(xn2[:, q], at(x_all, k * NQ + q), ACT.Identity, scale=frs[:, q:q + 1],
                                             bias=fnb[:, q:q + 1]).then_inc(C["normed"], 1)
                    act.wait_ge(C["tr_ps"], k + 1)
                    wait_past(act, C["carried"], k)
                    turned_x = bank[0][:].rearrange("p (b l) -> p b l", b=B)
                    nc.scalar.activation(curT[:, par], turned_x, ACT.Copy).then_inc(C["tr_sb"], 1)
                    wait_past(act, C["r_ps"], k)
                    nc.scalar.activation(prevT[:, :, 1:], turned_x[:, :, 0:L - 1], ACT.Copy).then_inc(C["shifted"], 1)
                if has(k, 2):
                    act.wait_ge(C["bias3"], k - 1)
                    for q in range(NQ):
                        act.wait_ge(C["res"], (k - 2) * NQ + q + 1)
                        nc.scalar.activation(at(o_all, (k - 2) * NQ + q), f2[:, q], ACT.Identity,
                                             bias=fnb3[:, q:q + 1]).then_inc(C["outv"], 1)
                if has(k):
                    act.wait_ge(C["k_ps"], k + 1)
                    wait_past(act, C["k_act"], k)
                    nc.scalar.activation(kr[:], bank[1][:], ACT.Relu).then_inc(C["k_relu"], 1)
                    act.wait_ge(C["k_relu"], k + 1)
                    wait_past(act, C["v_ps"], k)
                    nc.scalar.activation(ka[:], kr[:], ACT.Square).then_inc(C["k_act"], 1)
                    act.wait_ge(C["r_ps"], k + 1)
                    wait_past(act, C["f"], k * NQ)
                    nc.scalar.activation(th[:].rearrange("p q d -> p (q d)"), bank[2][:], ACT.Tanh,
                                         scale=0.5).then_inc(C["th"], 1)

            chunks(act, chunk)

        @block.tensor
        def _(pe):
            pe.wait_ge(s_c, 16)
            pe.wait_ge(s_w, 32)
            def first_phase(k):
                for j in range(2):
                    wait_past(pe, a_ev, k * 2 + j)
                    for t in range(4 * j, 4 * j + 4):
                        pe.wait_ge(a_xn, k * AK + t + 1)
                        mm = nc.tensor.transpose(bank[j][:, (t % 4) * 128:(t % 4) * 128 + 128], xn8[:, t], c_("ident"))
                    mm.then_inc(a_tr, 1)
                for j in range(2):
                    pe.wait_ge(a_ev, k * 2 + j + 1)
                    wait_past(pe, a_sm, (k * 2 + j) * 2)
                    for t in range(4 * j, 4 * j + 4):
                        mm = nc.tensor.matmul(bank[2 + j][:, (t % 4) * NS:(t % 4) * NS + NS], xt8[:, t], w_sb[:, O_S:],
                                              start=True, stop=True)
                    mm.then_inc(a_mm, 1)

            steps(pe, NT // AK, first_phase)
            pe.wait_ge(a_sm, 4 * NT // AK)
            pe.wait_ge(v2, B_AT)
            bf = b_all[:].rearrange("p t h -> p (t h)")
            lf = la_all[:].rearrange("p t h -> p (t h)")
            E = NQ * H
            for j in range(2):
                nc.tensor.matmul(bank[4 + j][:], c_("shift"), bf[:, 512 * j:512 * j + 512], start=True, stop=False,
                                 skip_group_check=True)
                w = 512 if j == 0 else 512 - E
                nc.tensor.matmul(bank[4 + j][:, 0:w], c_("edge"), bf[:, 512 * j + E:512 * j + E + w], start=False,
                                 stop=True, skip_group_check=True).then_inc(p2, 1)
            pe.wait_ge(v2, LA_AT)
            for j in range(2):
                nc.tensor.matmul(bank[j][:], c_("centre"), lf[:, 512 * j:512 * j + 512], start=True,
                                 stop=True).then_inc(p2, 1)
            for j in range(2):
                nc.tensor.matmul(bank[2 + j][:], c_("late"), lf[:, 512 * j:512 * j + 512], start=True, stop=False,
                                 skip_group_check=True)
                w = 512 if j == 0 else 512 - E
                nc.tensor.matmul(bank[2 + j][:, 0:w], c_("early"), lf[:, 512 * j + E:512 * j + E + w], start=False,
                                 stop=True, skip_group_check=True).then_inc(p2, 1)
            pe.wait_ge(v2, PRE_AT)
            mt, pre = flat(dt_all), flat(pre3)
            for j in range(2):
                nc.tensor.matmul(bank[6 + j][:], c_("tri"), mt[:, 512 * j:512 * j + 512], start=True, stop=False)
                nc.tensor.matmul(bank[6 + j][:], c_("ones"), pre[:, 512 * j:512 * j + 512], start=False,
                                 stop=True).then_inc(p2, 1)

            def project(n, par):
                pe.wait_ge(S["xt_copied"], n + 1)
                pe.wait_ge(S["z_silu"], n)
                nc.tensor.matmul(bank[0][:, 0:O_X], xt[:, par], w_sb[:, 0:O_X], start=True, stop=True)\
                    .then_inc(S["zbc_ps"], 1)
                pe.wait_ge(S["x_silu"], n)
                nc.tensor.matmul(bank[1][:], xt[:, par], w_sb[:, O_X:O_S], start=True, stop=True)\
                    .then_inc(S["x_ps"], 1)

            def turn(n, par):
                pe.wait_ge(S["dup1"], n + 1)
                pe.wait_ge(S["t_sb"], n)
                for g in range(G3):
                    mm = nc.tensor.transpose(bank[2][:, g * 128:g * 128 + 128],
                                             dup[:, par, g].rearrange("p a n -> p (a n)"), c_("ident"))
                mm.then_inc(S["t_ps"], 1)

            def score(n):
                pe.wait_ge(S["t_sb"], n + 1)
                pe.wait_ge(S["sg_ready"], n)
                for r in range(R):
                    mm = nc.tensor.matmul(bank[3][:, r * 128:r * 128 + 128], bt[:, r], bt[:, R], start=True, stop=True)
                mm.then_inc(S["sg_ps"], 1)

            def rx(buf, r):
                return buf.rearrange("p (h r e) -> p r h e", r=R, e=P)[:, r]

            def mix(i, q, par, between):
                pe.wait_ge(S["x1_ready"], i + 1)
                pe.wait_ge(S["p_added"], i)
                for r in range(R):
                    mm = nc.tensor.matmul(bank[5][:, 0:DI], dup[:, par, r].rearrange("p a n -> p (a n)"),
                                          rx(x1[:, par], r), start=(r == 0), stop=(r == R - 1))
                mm.then_inc(S["p_ps"], 1)
                if not isinstance(i, int) or i >= NQ:
                    pe.wait_ge(S["st_ready"], i - NQ + 1)
                else:
                    pe.wait_ge(S["st_zero"], 3)
                pe.wait_ge(S["ya_ready"], i)
                nc.tensor.matmul(bank[4][:, 0:DI], bt[:, R], st[:, q], start=True, stop=False)
                between()
                pe.wait_ge(S["sg_ready"], i + 1)
                for r in range(R):
                    mm = nc.tensor.matmul(bank[4][:, 0:DI], sg[:, r], rx(x1[:, par], r), start=False, stop=(r == R - 1))
                mm.then_inc(S["y_ps"], 1)

            def mix_general(i, q, par):
                def token(t):
                    n = i * L + t
                    pe.wait_ge(G["oh"], n + 1)
                    wait_past(pe, G["fk_sb"], n)
                    nc.tensor.matmul(bank[3][:, 0:H], oh[:, 0], at(b_all, i), start=True, stop=True).then_inc(G["fk_ps"], 1)
                    pe.wait_ge(S["t_sb"], i + 1)
                    pe.wait_ge(G["s1"], n + 1)
                    wait_past(pe, G["yk"], n)
                    nc.tensor.matmul(bank[4][:, 0:DI], bt[:, R], sk[:], start=True, stop=True).then_inc(G["y_ps"], 1)
                    pe.wait_ge(G["x1k"], n + 1)
                    wait_past(pe, G["st"], n)
                    for r in range(R):
                        mm = nc.tensor.matmul(bank[5][:, 0:DI], dup[:, par, r].rearrange("p a n -> p (a n)"),
                                              rx(xk[:, 0], r), start=(r == 0), stop=(r == R - 1))
                    mm.then_inc(G["p_ps"], 1)

                steps(pe, L, token, first=1 if isinstance(i, int) and i == 0 else 0)

            def y_turn(i, par):
                pe.wait_ge(S["y_ready"], i + 1)
                pe.wait_ge(S["yt_sb"], i)
                for k in range(2):
                    mm = nc.tensor.transpose(bank[6][:, k * 128:k * 128 + 128], y[:, par, k * 128:k * 128 + 128],
                                             c_("ident"))
                mm.then_inc(S["yt_ps"], 1)

            def y_out(i):
                pe.wait_ge(S["yt_sb"], i + 1)
                pe.wait_ge(S["o_sb"], i)
                for k in range(2):
                    mm = nc.tensor.matmul(bank[7][:, 0:D], yt[:, k], wo_sb[:, k], start=(k == 0), stop=(k == 1))
                mm.then_inc(S["o_ps"], 1)

            def step(i, q, general, first=False, last=False):
                par, other = q % 2, (q + 1) % 2
                if not last:
                    project(i + 1, other)
                if not first:
                    y_turn(i - 1, other)
                if general:
                    mix_general(i, q, par)
                    if not last:
                        turn(i + 1, other)
                else:
                    mix(i, q, par, lambda: None if last else turn(i + 1, other))
                if not first:
                    y_out(i - 1)
                if not last and not general:
                    score(i + 1)

            def tiles(general):
                project(0, 0)
                turn(0, 0)
                if not general:
                    score(0)
                for q in range(NQ):
                    step(q, q, general, first=(q == 0))
                with pe.Fori(1, NC_ - 1) as c:
                    for q in range(NQ):
                        step(c * NQ + q, q, general)
                for q in range(NQ):
                    step((NC_ - 1) * NQ + q, q, general, last=(q == NQ - 1))
                y_turn(NT - 1, (NT - 1) % 2)
                y_out(NT - 1)

            pe.wait_ge(s_w2, 16 * 6)
            pe.wait_ge(prep, FLAG_AT)
            pe.wait_ge(s2, F_AT)
            fl = pe.value_load(flag_i[0:1, 0:1], min_val=0, max_val=1)
            with pe.If(fl > 0):
                tiles(False)
            with pe.Else():
                tiles(True)

            pe.wait_ge(S["o_sb"], NT)
            def chunk(k, par):
                if not has(k):
                    return
                cur = curT[:, par].rearrange("p b l -> p (b l)")
                prev = prevT[:].rearrange("p b l -> p (b l)")
                wait_past(pe, C["shifted"], k)
                for q in range(NQ):
                    pe.wait_ge(C["normed"], k * NQ + q + 1)
                    mm = nc.tensor.transpose(bank[0][:, q * 128:q * 128 + 128], xn2[:, q], c_("ident"))
                mm.then_inc(C["tr_ps"], 1)
                pe.wait_ge(C["tr_sb"], k + 1)
                wait_past(pe, C["k_relu"], k)
                nc.tensor.matmul(bank[1][:], w_cur[:, 0], cur, start=True, stop=False)
                pe.wait_ge(C["carried"], k + 1)
                pe.wait_ge(C["shifted"], k + 1)
                nc.tensor.matmul(bank[1][:], w_prev[:, 0], prev, start=False, stop=True).then_inc(C["k_ps"], 1)
                wait_past(pe, C["th"], k)
                for q in range(NQ):
                    nc.tensor.matmul(bank[2][:, q * D:q * D + D], cur[:, q * 128:q * 128 + 128], w_cur[:, 1], start=True, stop=False)
                    mm = nc.tensor.matmul(bank[2][:, q * D:q * D + D], prev[:, q * 128:q * 128 + 128], w_prev[:, 1],
                                          start=False, stop=True)
                mm.then_inc(C["r_ps"], 1)
                pe.wait_ge(C["k_act"], k + 1)
                wait_past(pe, C["f"], k * NQ)
                for q in range(NQ):
                    mm = nc.tensor.matmul(bank[3][:, q * D:q * D + D], ka[:, q * 128:q * 128 + 128], wv_half[:],
                                          start=True, stop=True)
                mm.then_inc(C["v_ps"], 1)

            pe.wait_ge(s_mix, 6)
            chunks(pe, chunk)

        @block.vector
        def _(dve):
            vec = nc.vector
            dve.wait_ge(s2, 1)
            vec.tensor_reduce(flag[:, 2:3], negA[:], AX_X, ALU.max).then_inc(prep, 1)
            dve.wait_ge(prep, 1)
            vec.tensor_scalar(flag[:, 0:1], flag[:, 2:3], -1.0 if force_general else MAX_A, None, ALU.is_le)\
                .then_inc(prep, 1)
            dve.wait_ge(prep, 2)
            vec.tensor_scalar(flag[:, 1:2], flag[:, 0:1], -1.0, None, ALU.mult).then_inc(prep, 1)
            vec.tensor_copy(flag_i[:], flag[:, 0:1]).then_inc(prep, 1)
            vec.tensor_scalar(negA[:], negA[:], -1.0, None, ALU.mult).then_inc(prep, 1)
            vec.memset(halfpi[:], float(np.pi / 2)).then_inc(prep, 1)

            dve.wait_ge(s_w2, 16 * 6)
            vec.tensor_scalar(one_less_mu[:], mu_sb[:], -1.0, 1.0, ALU.mult, ALU.add).then_inc(s_mix, 1)
            for n, (w_, m) in enumerate(((wk_sb, 1), (wr_sb, 0))):
                vec.tensor_scalar(w_cur[:, n], w_[:], mu_sb[:, m:m + 1], None, ALU.mult).then_inc(s_mix, 1)
            vec.tensor_scalar(wv_half[:], wv_sb[:], 0.5, None, ALU.mult).then_inc(s_mix, 1)
            dve.wait_ge(s_mix, 1)
            for n, (w_, m) in enumerate(((wk_sb, 1), (wr_sb, 0))):
                vec.tensor_scalar(w_prev[:, n], w_[:], one_less_mu[:, m:m + 1], None, ALU.mult).then_inc(s_mix, 1)

            for k4 in range(4):
                dve.wait_ge(s_x[k4], 16 * 8)
            def first_phase(k):
                for t in range(AK):
                    vec.bn_stats(bn8[:, t], at(x_all, k * AK + t)).then_inc(a_st, 1)
                dve.wait_ge(a_st, (k + 1) * AK)
                wait_past(dve, a_rs, k)
                moments(dve, bn8, mo8, AK, a_mo, k * MOM, EPS_LN)
                vec.tensor_scalar(mo8[:, 1, :], mo8[:, 0, :], 0.5, None, ALU.mult).then_inc(mean8, 1)
                dve.wait_ge(mean8, k + 1)
                dve.wait_ge(a_rs, k + 1)
                wait_past(dve, a_tr, k * 2)
                for t in range(AK):
                    vec.tensor_scalar(xn8[:, t], at(x_all, k * AK + t), mo8[:, 1, t:t + 1], rs8[:, t:t + 1],
                                      ALU.subtract, ALU.mult).then_inc(a_xn, 1)

            steps(dve, NT // AK, first_phase)

            chain = [0]

            def link(ins):
                chain[0] += 1
                ins.then_inc(v2, 1)
                return chain[0]

            dve.wait_ge(a_sm, 4 * NT // AK)
            dve.wait_ge(s_a, 32)
            dve.wait_ge(prep, FLAG_AT)
            link(vec.tensor_tensor(dt_all[:], small[:, :, 0:H], dtb_sb[:].unsqueeze(1).broadcast_to([128, NT, H]), ALU.add))
            dve.wait_ge(s2, 2)
            link(vec.tensor_scalar(dt_all[:], dt_all[:], 1e9, 1.0, ALU.min, ALU.add))
            dve.wait_ge(s2, 4)
            link(vec.tensor_scalar(dt_all[:], dt_all[:], 1e-4, 0.5, ALU.max, ALU.min))
            link(vec.tensor_scalar(b_all[:], b_all[:], 0.5, 0.5, ALU.mult, ALU.add))
            dve.wait_ge(v2, 3)
            la = link(vec.tensor_tensor(la_all[:], dt_all[:], negA[:].unsqueeze(1).broadcast_to([128, NT, H]), ALU.mult))
            assert la == LA_AT
            dve.wait_ge(v2, 4)
            link(vec.tensor_tensor(g_all[:], b_all[:], dt_all[:], ALU.mult))
            link(vec.tensor_reduce(mdt[:], dt_all[:], AX_X, ALU.add))
            dve.wait_ge(v2, 6)
            assert link(vec.tensor_tensor(b_all[:], dt_all[:], g_all[:], ALU.subtract)) == B_AT
            dve.wait_ge(v2, B_AT)
            mt3 = dt_all
            link(vec.scalar_tensor_tensor(out=mt3[:], in0=small[:, :, 2 * H:], scalar=1.0 / H,
                                          in1=mdt[:].unsqueeze(2).broadcast_to([128, NT, H]), op0=ALU.mult, op1=ALU.mult))
            link(vec.memset(pre3[:, 0:NQ], 0.0))
            for c in range(1, NC_):
                dve.wait_ge(v2, chain[0])
                n = link(vec.tensor_tensor(pre3[:, NQ * c:NQ * c + NQ], pre3[:, NQ * c - NQ:NQ * c],
                                           mt3[:, NQ * c - NQ:NQ * c], ALU.add))
            assert n == PRE_AT, n
            dve.wait_ge(s2, 10)
            dve.wait_ge(p2, P_B)
            for j in range(2):
                link(vec.tensor_tensor(flat(turns)[:, 512 * j:512 * j + 512], bank[4 + j][:],
                                       flat(g_all)[:, 512 * j:512 * j + 512], ALU.add))
            dve.wait_ge(v2, chain[0])
            assert link(vec.tensor_tensor(eg_all[:], turns[:], eg_all[:], ALU.mult)) == EG_AT
            dve.wait_ge(p2, P_S)
            dve.wait_ge(v2, EG_AT)
            for j in range(2):
                link(vec.tensor_scalar(flat(turns)[:, 512 * j:512 * j + 512], bank[6 + j][:], float(1 / (2 * np.pi)),
                                       MAGIC, ALU.mult, ALU.add))
            dve.wait_ge(v2, chain[0])
            link(vec.tensor_scalar(turns[:], turns[:], MAGIC, None, ALU.subtract))
            dve.wait_ge(v2, chain[0])
            for j in range(2):
                cols = slice(512 * j, 512 * j + 512)
                link(vec.scalar_tensor_tensor(out=flat(ang)[:, cols], in0=flat(turns)[:, cols], scalar=-TWO_PI_HI,
                                              in1=bank[6 + j][:], op0=ALU.mult, op1=ALU.add))
            dve.wait_ge(v2, chain[0])
            link(vec.scalar_tensor_tensor(out=ang[:], in0=turns[:], scalar=-TWO_PI_LO, in1=ang[:], op0=ALU.mult,
                                          op1=ALU.add))
            dve.wait_ge(v2, chain[0])
            link(vec.scalar_tensor_tensor(out=turns[:], in0=ang[:], scalar=-1.0, in1=ang[:], op0=ALU.mult, op1=ALU.max))
            n = link(vec.tensor_scalar(ang_in[:], ang[:], -PI_IN, PI_IN, ALU.max, ALU.min))
            assert n == ANG_AT, n

            def early(n, par, general):
                dve.wait_ge(S["zbc_ps"], n + 1)
                if not isinstance(n, int) or n >= 2:
                    dve.wait_ge(S["prod_ready"], n - 1)
                vec.tensor_tensor(bc[:, par], bank[0][:, 0:G3 * N], bcb_sb[:], ALU.mult).then_inc(S["bc_ready"], 1)
                dve.wait_ge(S["bc_ready"], n + 1)
                vec.tensor_tensor(rot[:], bc[:, par].rearrange("p (g a n) -> p g a n", g=G3, a=2).unsqueeze(3)
                                  .broadcast_to([128, G3, 2, 2, H]),
                                  at(cs_all, n).rearrange("p (a j n) -> p a j n", a=2, j=2).unsqueeze(1)
                                  .broadcast_to([128, G3, 2, 2, H]), ALU.mult).then_inc(S["rotated"], 1)
                dve.wait_ge(S["prod_ready"], n + 1)
                vec.tensor_reduce(cb[:], prod[:], AX_X, ALU.add).then_inc(S["cb_ready"], 1)
                dve.wait_ge(S["rotated"], n + 1)
                if not isinstance(n, int) or n >= 2:
                    if general:
                        dve.wait_ge(G["p_ps"], (n - 1) * L)
                    else:
                        dve.wait_ge(S["y_ps"], n - 1)
                for h in range(2):
                    rows = slice(64 * h, 64 * h + 64)
                    vec.tensor_tensor(dup[rows, par, :, h, :].rearrange("p g (j n) -> p g j n", j=2),
                                      rot[rows, :, 0], rot[rows, :, 1], ALU.add).then_inc(S[f"dup{h}"], 1)
                dve.wait_ge(S["x_silu"], n + 1)
                dve.wait_ge(S["w_ready"], n + 1)
                vec.tensor_tensor(x1[:, par].rearrange("p (a e) -> p a e", e=P),
                                  xs[:, par].rearrange("p (a e) -> p a e", e=P),
                                  wx[:, par].rearrange("p h r -> p (h r)").unsqueeze(2).broadcast_to([128, H * R, P]),
                                  ALU.mult).then_inc(S["x1_ready"], 1)
                dve.wait_ge(S["d0_ready"], n + 1)
                dve.wait_ge(S["dg_ready"], n)
                vec.scalar_tensor_tensor(out=d1[:].rearrange("p (h e) -> p h e", e=P),
                                         in0=xs[:, par].rearrange("p (h r e) -> p r h e", r=R, e=P)[:, 1],
                                         scalar=cbr[:, par, 1:2], in1=d0[:].rearrange("p (h e) -> p h e", e=P),
                                         op0=ALU.mult, op1=ALU.add).then_inc(S["d1_ready"], 1)

            def mask(n):
                dve.wait_ge(S["sg_ps"], n + 1)
                vec.tensor_tensor(sg[:], bank[3][:, 0:R * 128].rearrange("p (r m) -> p r m", r=R),
                                  c_("strict").unsqueeze(1).broadcast_to([128, R, 128]), ALU.mult)\
                    .then_inc(S["sg_ready"], 1)

            def state(i, q):
                dve.wait_ge(S["p_ps"], i + 1)
                dve.wait_ge(S["st_ready"], i)
                vec.tensor_tensor(sp[:], bank[5][:, 0:DI], st[:, q], ALU.add).then_inc(S["p_added"], 1)

            def outputs(i, par, general):
                by_head = lambda a: a.rearrange("p (h e) -> p h e", e=P)
                if not general:
                    dve.wait_ge(S["y_ps"], i + 1)
                    vec.tensor_tensor(by_head(ya[:]), by_head(bank[4][:, 0:DI]),
                                      at(ec_all, i).unsqueeze(2).broadcast_to([128, H, P]), ALU.mult)\
                        .then_inc(S["ya_ready"], 1)
                    dve.wait_ge(S["ya_ready"], i + 1)
                dve.wait_ge(S["dg_ready"], i + 1)
                dve.wait_ge(S["y_ready"], i)
                vec.tensor_tensor(ys[:], (yk if general else ya)[:], dg[:, par], ALU.add).then_inc(S["ys_ready"], 1)

            def tokens_general(i, q, par):
                dve.wait_ge(S["ys_ready"], i)
                dve.wait_ge(S["x1_ready"], i + 1)
                vec.memset(yk[:], 0.0).then_inc(G["zero"], 1)
                def token(t):
                    n = i * L + t
                    hot = cm[:, CONSTS.index("hot"), bass.ds(t, 1) if not isinstance(t, int) else slice(t, t + 1)]
                    wait_past(dve, G["fk_ps"], n)
                    vec.tensor_scalar(oh[:, 0], c_("ones"), hot, None, ALU.mult).then_inc(G["oh"], 1)
                    wait_past(dve, G["p_ps"], n)
                    vec.tensor_scalar(xk[:, 0], x1[:, par], hot, None, ALU.mult).then_inc(G["x1k"], 1)
                    dve.wait_ge(G["fk_ps"], n + 1)
                    vec.tensor_copy(fk[:], bank[3][:, 0:H]).then_inc(G["fk_sb"], 1)
                    dve.wait_ge(G["fk_sb"], n + 1)
                    wait_past(dve, G["st"], n)
                    wait_past(dve, G["y_ps"], n)
                    vec.tensor_tensor(sk[:].rearrange("p (h e) -> p h e", e=P), st[:, q].rearrange("p (h e) -> p h e", e=P),
                                      fk[:].unsqueeze(2).broadcast_to([128, H, P]), ALU.mult).then_inc(G["s1"], 1)
                    dve.wait_ge(G["y_ps"], n + 1)
                    wait_past(dve, G["yk"], n)
                    dve.wait_ge(G["zero"], i + 1)
                    vec.scalar_tensor_tensor(out=yk[:], in0=bank[4][:, 0:DI], scalar=hot, in1=yk[:], op0=ALU.mult,
                                             op1=ALU.add).then_inc(G["yk"], 1)
                    dve.wait_ge(G["p_ps"], n + 1)
                    dve.wait_ge(G["s1"], n + 1)
                    vec.tensor_tensor(st[:, q], bank[5][:, 0:DI], sk[:], ALU.add).then_inc(G["st"], 1)

                steps(dve, L, token, first=1 if isinstance(i, int) and i == 0 else 0)
                dve.wait_ge(G["yk"], (i + 1) * L)

            def stats(i):
                vec.bn_stats(at(ost_all, i), at(o_all, i)).then_inc(S["ost_done"], 1)

            def step(i, q, general, first=False, last=False):
                par, other = q % 2, (q + 1) % 2
                if general:
                    tokens_general(i, q, par)
                if not first:
                    dve.wait_ge(S["o_sb"], i - 1)
                if not last:
                    early(i + 1, other, general)
                if not general:
                    state(i, q)
                outputs(i, par, general)
                if not first:
                    stats(i - 2)
                if not last and not general:
                    mask(i + 1)

            def tiles(general):
                early(0, 0, general)
                if not general:
                    mask(0)
                for q in range(NQ):
                    step(q, q, general, first=(q < 2))
                with dve.Fori(1, NC_ - 1) as c:
                    for q in range(NQ):
                        step(c * NQ + q, q, general)
                for q in range(NQ):
                    step((NC_ - 1) * NQ + q, q, general, last=(q == NQ - 1))
                dve.wait_ge(S["o_sb"], NT)
                stats(NT - 2)
                stats(NT - 1)

            dve.wait_ge(s2, TABLES_AT)
            dve.wait_ge(s_w2, 16 * 6)
            dve.wait_ge(S["st_zero"], 3)
            fl = dve.value_load(flag_i[0:1, 0:1], min_val=0, max_val=1)
            with dve.If(fl > 0):
                tiles(False)
            with dve.Else():
                tiles(True)

            dve.wait_ge(S["ost_done"], NT)
            dve.wait_ge(S["ysq_done"], NT)
            moments(dve, ost_all, tokc, NT, fac_v, 0, 0.0)
            dve.wait_ge(fac_v, MOM)
            vec.scalar_tensor_tensor(out=tokc[:, 1], in0=ysq_all[:, :, 0], scalar=EPS_LN, in1=tokc[:, 5], op0=ALU.mult,
                                     op1=ALU.add).then_inc(fac_v, 1)
            vec.tensor_scalar(tokc[:, 2], csq_all[:, :, 0], EPS_RMS, EPS_LN * EPS_RMS * SCALE2_INV, ALU.add, ALU.mult)\
                .then_inc(fac_v, 1)
            dve.wait_ge(fac_v, MOM + 2)
            vec.tensor_tensor(tokc[:, 6], tokc[:, 1], tokc[:, 2], ALU.add).then_inc(fac_v, 1)

            def residual(k):
                dve.wait_ge(fac_p, k + 1)
                for q in range(NQ):
                    i = k * NQ + q
                    vec.scalar_tensor_tensor(out=at(x_all, i), in0=at(o_all, i), scalar=tokc[:, 7, bass.ds(i, 1)],
                                             in1=at(x_all, i), op0=ALU.mult, op1=ALU.add).then_inc(C["x1"], 1)

            def stats2(k):
                for q in range(NQ):
                    vec.bn_stats(fst[:, q], at(x_all, k * NQ + q)).then_inc(C["stats"], 1)

            residual(0)
            dve.wait_ge(C["x1"], NQ)
            stats2(0)

            def chunk(k, par):
                n, c = norms(k), k - 2
                if has(k):
                    dve.wait_ge(C["stats"], (k + 1) * NQ)
                if has(k, 2):
                    dve.wait_ge(C["stats3"], (c + 1) * NQ)
                wait_past(dve, C["norm_bias"], k)
                moments(dve, fst, fmo, n, C["mom"], k * MOM, EPS_LN)
                if has(k, 2):
                    wait_past(dve, C["bias3"], c)
                    vec.scalar_tensor_tensor(out=mean_o[:], in0=tokc[:, 0, bass.ds(c * NQ, NQ)], scalar=-0.5,
                                             in1=tokc[:, 7, bass.ds(c * NQ, NQ)], op0=ALU.mult, op1=ALU.mult)\
                        .then_inc(C["means"], 1)
                if has(k, -1):
                    residual(k + 1)
                    dve.wait_ge(C["x1"], (k + 2) * NQ)
                dve.wait_ge(C["pow"], k + 1)
                wait_past(dve, C["normed"], upto(k) * NQ)
                if has(k, 2):
                    wait_past(dve, C["bias3"], c)
                vec.scalar_tensor_tensor(out=fnb[:, n], in0=fmo[:, 0, n], scalar=-0.5, in1=frs[:, n], op0=ALU.mult,
                                         op1=ALU.mult).then_inc(C["norm_bias"], 1)
                if has(k, 2):
                    wait_past(dve, C["outv"], c * NQ)
                    for q in range(NQ):
                        vec.scalar_tensor_tensor(out=f2[:, q], in0=ff[:, q], scalar=frs[:, NQ + q:NQ + q + 1],
                                                 in1=at(x_all, c * NQ + q), op0=ALU.mult, op1=ALU.add)\
                            .then_inc(C["res"], 1)
                    dve.wait_ge(C["norm_bias"], k + 1)
                    dve.wait_ge(C["means"], c + 1)
                    vec.tensor_tensor(fnb3[:], fnb[:, NQ:], mean_o[:], ALU.add).then_inc(C["bias3"], 1)
                if has(k, 1):
                    if has(k, 2):
                        dve.wait_ge(C["res"], (c + 1) * NQ)
                    dve.wait_ge(C["th"], k)
                    dve.wait_ge(C["v_ps"], k)
                    for q in range(NQ):
                        vec.scalar_tensor_tensor(out=ff[:, q], in0=th[:, q], scalar=1.0, in1=bank[3][:, q * D:q * D + D],
                                                 op0=ALU.add, op1=ALU.mult).then_inc(C["f"], 1)
                if has(k, -1):
                    stats2(k + 1)
                if has(k, 1):
                    for q in range(NQ):
                        dve.wait_ge(C["f"], (k - 1) * NQ + q + 1)
                        vec.bn_stats(fst[:, NQ + q], ff[:, q]).then_inc(C["stats3"], 1)

            chunks(dve, chunk)


def kernel(L0_attn_x, L0_attn_W_in, L0_attn_A_log, L0_attn_dt_bias, L0_attn_B_norm_bias, L0_attn_C_norm_bias,
           L0_attn_W_out, L0_ffn_W_r, L0_ffn_W_k, L0_ffn_W_v, L0_ffn_mu_r, L0_ffn_mu_k):
    import concourse.bacc as bacc
    from concourse.bass_utils import run_bass_kernel_spmd

    w = np.asarray(L0_attn_W_in)
    z, xr, bcw, rest = w[:, :DI], w[:, DI:DI + DI * R], w[:, DI * (1 + R):DI * (1 + R) + G3 * N], w[:, -NS:]
    bb, cb = np.asarray(L0_attn_B_norm_bias).reshape(-1), np.asarray(L0_attn_C_norm_bias).reshape(-1)
    arrays = {
        "x": np.asarray(L0_attn_x),
        "w_in": np.concatenate([bcw, z, xr, rest], axis=1),
        "a_log": np.asarray(L0_attn_A_log),
        "dt_bias": np.asarray(L0_attn_dt_bias),
        "bc_bias": np.concatenate([bb, bb, cb]),
        "w_out": np.asarray(L0_attn_W_out),
        "w_r": np.asarray(L0_ffn_W_r).T,
        "w_k": np.asarray(L0_ffn_W_k).T,
        "w_v": np.asarray(L0_ffn_W_v).T,
        "mu": np.stack([np.asarray(L0_ffn_mu_r), np.asarray(L0_ffn_mu_k)], axis=1),
        "consts": constants(),
    }
    arrays = {n: np.ascontiguousarray(a) for n, a in arrays.items()}
    nc = bacc.Bacc("TRN2", target_bir_lowering=False, num_devices=1)
    args = [nc.dram_tensor(n, a.shape, mybir.dt.from_np(a.dtype), kind="ExternalInput").ap() for n, a in arrays.items()]
    out = nc.dram_tensor("out", (B, T, D), F32, kind="ExternalOutput").ap()
    build(nc, *args, out)
    r = run_bass_kernel_spmd(nc, [arrays], core_ids=[0])
    return r.results[0]["out"]
```

```python
from contextlib import ExitStack

import numpy as np

import concourse.bass as bass
from concourse import mybir

F32 = mybir.dt.float32
F32R = mybir.dt.float32r
I32 = mybir.dt.int32
ALU = mybir.AluOpType
ACT = mybir.ActivationFunctionType
AX_X = mybir.AxisListType.X

B, T, D = 8, 512, 128
L = 64
NC_ = T // L
NQ = B // 2
NT = NC_ * NQ
H, P, R, N = 32, 8, 2, 64
DI = H * P
G3 = R + 1
O_BC, O_Z, O_X, O_S = 0, G3 * N, G3 * N + DI, G3 * N + DI + DI * R
NS = 3 * H
WCOLS = O_S + NS
AK = 8
MAX_A = 68.0 / (0.5 * L / 2)
EPS_LN, EPS_RMS = 1e-5, 1e-6
SCALE2_INV = float(N * R)
MAGIC = 1.5 * 2.0 ** 23
TWO_PI_HI = 6.28125
TWO_PI_LO = float(2 * np.pi - 6.28125)
PI_IN = 3.1415925

MOM = 6
FLAG_AT = 6
S_A, S_LN, S_CUM, F_AT, TABLES_AT = 1, 3, 7, 12, 21
MIN_AT, SIG_AT, CLIP_AT, LA_AT, DTSUM_AT, MT_AT, PRE_AT = 2, 3, 5, 7, 8, 9, 17
ANG_AT, EG_AT = (23, 30), 27
G_AT, B_AT, WSUM_AT = 2, 5, 6
P_CUM, P_LATE, P_EARLY, P_ANG = (1, 2), (3, 6), (4, 7), (5, 8)
FAC_POW = MOM + 3

CONSTS = ["ident", "strict", "tri", "ones", "centre", "late", "early", "shift", "edge", "hot"]


def constants():
    k, m = np.arange(128)[:, None], np.arange(128)[None, :]
    same, kl, ml = k // L == m // L, k % L, m % L
    mid = L // 2 - 1
    mats = {
        "ident": k == m,
        "strict": same & (kl < ml),
        "tri": same & (kl <= ml),
        "ones": same,
        "late": same & (kl > mid),
        "early": same & (kl <= mid),
        "shift": same & (kl == ml + 1),
        "edge": same & (kl == 0) & (ml == L - 1),
        "hot": (kl == m) & (m < L),
    }
    mats = {n: v.astype(np.float32) for n, v in mats.items()}
    mats["centre"] = mats["tri"] - mats["early"]
    return np.concatenate([mats[n] for n in CONSTS], axis=1).astype(np.float32)


def build(nc, x, w_in, a_log, dt_bias, bc_bias, w_out, w_r, w_k, w_v, mu, consts, out, force_general=False):
    ctx = ExitStack()
    with ctx:
        def sb(name, *shape, dt=F32):
            return ctx.enter_context(nc.sbuf_tensor(name, list(shape), dt))

        def sem(name):
            return ctx.enter_context(nc.semaphore(name))

        def at(buf, i):
            if isinstance(i, int):
                return buf[:, i, :]
            return buf[:, bass.ds(i, 1), :].rearrange("p a n -> p (a n)")

        def wait_past(eng, semaphore, value):
            if not isinstance(value, int) or value > 0:
                eng.wait_ge(semaphore, value)

        def steps(eng, n, body, first=1):
            for k in range(first):
                body(k)
            with eng.Fori(first, n) as k:
                body(k)

        x_all = sb("x_all", 128, NT, D)
        xnT_all = sb("xnT_all", 128, NT, 128)
        o_all = sb("o_all", 128, NT, D)
        w_sb = sb("w_sb", 128, WCOLS)
        cm = sb("cm", 128, len(CONSTS), 128)
        wo_sb = sb("wo_sb", 128, 2, D)
        wr_sb = sb("wr_sb", 128, D)
        wk_sb = sb("wk_sb", 128, D)
        wv_sb = sb("wv_sb", 128, D)
        mu_sb = sb("mu_sb", 128, 2)
        one_less_mu = sb("one_less_mu", 128, 2)
        dtb_sb = sb("dtb_sb", 128, H)
        negA = sb("negA", 128, H)
        bcb_sb = sb("bcb_sb", 128, G3 * N)
        flag = sb("flag", 128, 4)
        flag_i = sb("flag_i", 128, 1, dt=I32)
        th_all = sb("th_all", 128, NT, H)
        dt_all = sb("dt_all", 128, NT, H)
        g_all = sb("g_all", 128, NT, H)
        b_all = sb("b_all", 128, NT, H)
        bnext = sb("bnext", 128, NT, H)
        la_all = sb("la_all", 128, NT, H)
        ec_all = sb("ec_all", 128, NT, H)
        eg_all = sb("eg_all", 128, NT, H)
        f_all = sb("f_all", 128, NT, H)
        r_all = sb("r_all", 128, NT, H)
        cs_all = sb("cs_all", 128, NT, 4 * H)
        ost_all = sb("ost_all", 128, NT, 6)
        ysq_all = sb("ysq_all", 128, NT, 1)
        csq_all = sb("csq_all", 128, NT, 1)
        tokc = sb("tokc", 128, 8, NT)
        halfn = sb("halfn", 128, 8)
        epst = sb("epst", 128, 4)
        one = sb("one", 128, 1)

        bank = [ctx.enter_context(nc.psum_tensor(f"bank{n}", [128, 512], F32)) for n in range(8)]

        def c_(name):
            return cm[:, CONSTS.index(name), :]

        s_x = [sem(f"x_loaded{k}") for k in range(4)]
        s_w, s_wp = sem("w_scalars_loaded"), sem("w_in_loaded")
        s_w2 = sem("other_weights_loaded")
        s_a = sem("decay_inputs_loaded")
        s_c, s_c2 = sem("identity_loaded"), sem("consts_loaded")
        s_ones = sem("fills_done")
        s_bn = sem("next_b_shifted")
        prep = sem("prep_vector")

        bn8 = sb("bn8", 128, 2, AK, 6)
        mo8 = sb("mo8", 128, 2, 6, AK)
        mean8 = sb("mean8", 128, 2, AK)
        rs8 = sb("rs8", 128, 2, AK)
        xn8 = sb("xn8", 128, AK, D)
        xt8 = sb("xt8", 128, AK, 128)
        a_st, a_mo, a_me, a_rs, a_xn, a_tr, a_ev, a_mm, a_sm, a_kept, a_dt, a_exp = (sem(n) for n in (
            "a_stats", "a_moments", "a_means", "a_rstd", "a_normed", "a_transposed", "a_evacuated", "a_projected",
            "a_lam_theta", "a_kept", "a_dt", "a_exp"))
        v2, s2, p2, g2 = (sem("tables_" + n) for n in ("vector", "scalar", "tensor", "pool"))
        s_warm = sem("exp_table_loaded")
        halfpi = sb("halfpi", 128, 2)
        mdt = sb("mdt", 128, NT)

        def scratch(n):
            return o_all[:].rearrange("p t d -> p (t d)")[:, n * NT * H:(n + 1) * NT * H]\
                .rearrange("p (t h) -> p t h", h=H)

        pre3 = scratch(0)
        turns = scratch(1)
        ang = scratch(2)
        ang_in = scratch(3)

        def carries(i):
            return not isinstance(i, int) or i < NT - NQ

        def flat(buf):
            return buf[:].rearrange("p t h -> p (t h)")

        x_hi = sb("x_hi", 128, 2, 128, dt=F32R)
        x_lo = sb("x_lo", 128, 2, 128, dt=F32R)
        w_hi = sb("w_hi", 128, O_S, dt=F32R)
        w_lo = sb("w_lo", 128, O_S, dt=F32R)
        s_split = sem("w_split")
        bc = sb("bc", 128, 2, G3 * N)
        rot = sb("rot", 128, G3, 2, 2, H)
        dup = sb("dup", 128, 2, G3, 2, N)
        xs = sb("xs", 128, 2, DI * R)
        zs = sb("zs", 128, 2, DI)
        junk = sb("junk", 128, G3 * N)
        junk_y = sb("junk_y", 128, DI)
        msb = sb("msb", 128, 2, R)
        mse = sb("mse", 128, R)
        rb = sb("rb", 128, 2, R)
        wx = sb("wx", 128, 2, H, R)
        x1 = sb("x1", 128, 2, DI * R)
        prod = sb("prod", 128, R, N)
        cb = sb("cb", 128, R)
        cbr = sb("cbr", 128, 2, R)
        d0 = sb("d0", 128, DI)
        d1 = sb("d1", 128, DI)
        dg = sb("dg", 128, 2, DI)
        bt = sb("bt", 128, G3, 128)
        sg = sb("sg", 128, R, 128)
        st = sb("st", 128, NQ, DI)
        sp = sb("sp", 128, DI)
        ya = sb("ya", 128, DI)
        ys = sb("ys", 128, DI)
        y = sb("y", 128, 2, DI)
        yt = sb("yt", 128, 2, 128)
        oh = sb("oh", 128, 2, 128)
        xk = sb("xk", 128, 2, DI * R)
        fk = sb("fk", 128, H)
        sk = sb("sk", 128, DI)
        yk = sb("yk", 128, DI)

        names = ("x_hi x_lo zbc_ps x_ps bc_ready rotated dup0 dup1 x_silu z_silu sq_done mse_ready rb_ready w_ready "
                 "x1_ready prod_ready cb_ready cbr_ready d0_ready d1_ready dg_ready t_ps t_sb sg_ps sg_ready p_ps "
                 "p_added st_ready st_scaled y_ps ya_ready ys_ready y_ready ysq_done yt_ps yt_sb o_ps o_sb ost_done st_zero").split()
        S = {n: sem(n) for n in names}
        G = {n: sem("g_" + n) for n in ("oh x1k fk_ps fk_sb s1 y_ps yk p_ps st zero done".split())}

        fst = sb("fst", 128, 2 * NQ, 6)
        fmo = sb("fmo", 128, 6, 2 * NQ)
        frs = sb("frs", 128, 2 * NQ)
        fnb = sb("fnb", 128, 2 * NQ)
        mean_o = sb("mean_o", 128, NQ)
        fnb3 = sb("fnb3", 128, NQ)
        xn2 = sb("xn2", 128, NQ, D)
        curT = sb("curT", 128, 2, B, L)
        prevT = sb("prevT", 128, B, L)
        w_cur = sb("w_cur", 128, 2, D)
        w_prev = sb("w_prev", 128, 2, D)
        kr = sb("kr", 128, B * L)
        ka = sb("ka", 128, B * L)
        th = sb("th", 128, NQ, D)
        wv_half = sb("wv_half", 128, D)
        ff = sb("ff", 128, NQ, D)
        f2 = sb("f2", 128, NQ, D)
        cnames = ("scaled_o x1_first x1 stats mom pow norm_bias pow3 norm_bias3 normed tr_ps tr_sb carried shifted k_ps k_relu k_act r_ps th v_ps "
                  "f stats3 means res bias3 outv").split()
        C = {n: sem("c_" + n) for n in cnames}
        s_mix = sem("mixing_weights")
        stored = sem("stored")
        fac_v, fac_p = sem("factors_vector"), sem("factors_pool")

        def chunks(eng, body):
            for k in range(2):
                body(k, k % 2)
            with eng.Fori(1, NC_ // 2 - 1) as cc:
                for par in range(2):
                    body(cc * 2 + par, par)
            for k in range(NC_ - 2, NC_ + 2):
                body(k, k % 2)

        def has(k, back=0):
            return not isinstance(k, int) or 0 <= k - back < NC_

        def norms(k):
            return slice(0 if has(k, -1) else NQ, 2 * NQ if has(k, 2) else NQ)

        def moments(dve, stats, mo, n, chain, base, eps):
            n = n if isinstance(n, slice) else slice(0, n)
            even, odd = stats[:, n, 1], stats[:, n, 4]
            nc.vector.tensor_tensor(mo[:, 0, n], even, odd, ALU.add).then_inc(chain, 1)
            nc.vector.tensor_tensor(mo[:, 1, n], even, odd, ALU.subtract).then_inc(chain, 1)
            nc.vector.tensor_tensor(mo[:, 2, n], stats[:, n, 2], stats[:, n, 5], ALU.add).then_inc(chain, 1)
            dve.wait_ge(chain, base + 2)
            nc.vector.tensor_tensor(mo[:, 3, n], mo[:, 1, n], mo[:, 1, n], ALU.mult).then_inc(chain, 1)
            dve.wait_ge(chain, base + 4)
            nc.vector.scalar_tensor_tensor(out=mo[:, 4, n], in0=mo[:, 3, n], scalar=float(D // 4),
                                           in1=mo[:, 2, n], op0=ALU.mult, op1=ALU.add).then_inc(chain, 1)
            dve.wait_ge(chain, base + 5)
            nc.vector.tensor_scalar(mo[:, 5, n], mo[:, 4, n], 1.0 / D, float(eps), ALU.mult, ALU.add).then_inc(chain, 1)

        block = ctx.enter_context(nc.Block())

        @block.sync
        def _(sp_):
            for c in range(NC_):
                for h in range(2):
                    sp_.dma_start(x_all[64 * h:64 * h + 64, NQ * c:NQ * c + NQ, :],
                                  x.rearrange("(q h) (c l) d -> h c l q d", h=2, l=L)[h, c]).then_inc(s_x[c // 2], 16)
            sp_.dma_start(cm[:, 1:], consts[:, 128:].rearrange("p (n m) -> p n m", m=128)).then_inc(s_c2, 16)
            sp_.dma_start(w_sb[:, 0:O_S], w_in[:, 0:O_S]).then_inc(s_wp, 16)
            for dst, src in ((wo_sb[:], w_out.rearrange("(k p) n -> p k n", p=128)), (wr_sb[:], w_r), (wk_sb[:], w_k),
                             (wv_sb[:], w_v), (mu_sb[:], mu), (bcb_sb[:], bc_bias.partition_broadcast(128))):
                sp_.dma_start(dst, src).then_inc(s_w2, 16)
            sp_.wait_ge(g2, B_AT)
            for h in range(2):
                sp_.dma_start(bnext[64 * h:64 * h + L - 1], b_all[64 * h + 1:64 * h + L]).then_inc(s_bn, 16)
                sp_.dma_start(bnext[64 * h + L - 1:64 * h + L, 0:NT - NQ], b_all[64 * h:64 * h + 1, NQ:]).then_inc(s_bn, 16)
            with sp_.Fori(0, NC_) as c:
                sp_.wait_ge(C["outv"], (c + 1) * NQ)
                for h in range(2):
                    sp_.dma_start(
                        out.rearrange("(q h) (c l) d -> h c l q d", h=2, l=L)[h, bass.ds(c, 1)]
                        .rearrange("a l q d -> (a l) q d"),
                        o_all[64 * h:64 * h + 64, bass.ds(c * NQ, NQ)]).then_inc(stored, 16)
            sp_.wait_ge(stored, 2 * 16 * NC_)

        @block.gpsimd
        def _(pool):
            pool.dma_start(cm[:, 0], consts[:, 0:128]).then_inc(s_c, 16)
            pool.dma_start(w_sb[:, O_S:], w_in[:, O_S:]).then_inc(s_w, 16)
            pool.dma_start(negA[:], a_log.partition_broadcast(128)).then_inc(s_a, 16)
            pool.dma_start(dtb_sb[:], dt_bias.partition_broadcast(128)).then_inc(s_a, 16)
            nc.gpsimd.memset(halfn[:], -0.5).then_inc(s_ones, 1)
            nc.gpsimd.memset(epst[:], EPS_RMS).then_inc(s_ones, 1)
            nc.gpsimd.memset(one[:], 1.0).then_inc(s_ones, 1)
            nc.gpsimd.memset(st[:], 0.0).then_inc(S["st_zero"], 1)
            nc.gpsimd.memset(dup[:], 0.0).then_inc(S["st_zero"], 1)
            nc.gpsimd.memset(curT[:, 1], 0.0).then_inc(S["st_zero"], 1)
            pool.wait_ge(s_ones, 3)
            for k in range(NT // AK):
                pool.wait_ge(a_mo, (k + 1) * MOM)
                if k >= 2:
                    pool.wait_ge(a_xn, (k - 1) * AK)
                nc.gpsimd.tensor_tensor(rs8[:, k % 2], mo8[:, k % 2, 5, :], halfn[:, 0:AK], ALU.pow).then_inc(a_rs, 1)
            pool.wait_ge(s_wp, 16)
            nc.gpsimd.tensor_copy(w_hi[:], w_sb[:, 0:O_S]).then_inc(s_split, 1)
            pool.wait_ge(s_split, 1)
            nc.gpsimd.tensor_tensor(w_lo[:], w_sb[:, 0:O_S], w_hi[:].bitcast(F32), ALU.subtract).then_inc(s_split, 1)
            def lower_part(n, par):
                pool.wait_ge(S["x_hi"], n + 1)
                if not isinstance(n, int) or n >= 2:
                    pool.wait_ge(S["x_ps"], n - 1)
                    pool.wait_ge(S["zbc_ps"], n - 1)
                nc.gpsimd.tensor_tensor(x_lo[:, par], at(xnT_all, n), x_hi[:, par].bitcast(F32),
                                        ALU.subtract).then_inc(S["x_lo"], 1)

            lower_part(0, 0)
            lower_part(1, 1)
            for j in range(2):
                t = slice(16 * j, 16 * j + 16)
                pool.wait_ge(v2, CLIP_AT - 1 + j)
                nc.gpsimd.tensor_tensor(g_all[:, t], b_all[:, t], dt_all[:, t], ALU.mult).then_inc(g2, 1)
            nc.gpsimd.memset(bnext[:, NT - NQ:], 0.0).then_inc(g2, 1)
            for j in range(2):
                t = slice(16 * j, 16 * j + 16)
                pool.wait_ge(g2, 1 + j)
                nc.gpsimd.tensor_tensor(b_all[:, t], dt_all[:, t], g_all[:, t], ALU.subtract).then_inc(g2, 1)
            pool.wait_ge(s_bn, 4 * 16)
            nc.gpsimd.tensor_tensor(bnext[:], bnext[:], g_all[:], ALU.add).then_inc(g2, 1)

            def early(n, par):
                pool.wait_ge(S["bc_ready"], n + 1)
                pool.wait_ge(S["cb_ready"], n)
                nc.gpsimd.tensor_tensor(prod[:], bc[:, par, 0:R * N].rearrange("p (r n) -> p r n", r=R),
                                        bc[:, par, R * N:].unsqueeze(1).broadcast_to([128, R, N]),
                                        ALU.mult).then_inc(S["prod_ready"], 1)
                pool.wait_ge(S["sq_done"], n + 1)
                nc.gpsimd.tensor_tensor(mse[:], msb[:, par], epst[:, 0:R], ALU.add).then_inc(S["mse_ready"], 1)
                pool.wait_ge(S["mse_ready"], n + 1)
                nc.gpsimd.tensor_tensor(rb[:, par], mse[:], halfn[:, 0:R], ALU.pow).then_inc(S["rb_ready"], 1)
                pool.wait_ge(S["rb_ready"], n + 1)
                if not isinstance(n, int) or n >= 2:
                    pool.wait_ge(S["x1_ready"], n - 1)
                if isinstance(n, int) and n == 0:
                    pool.wait_ge(v2, EG_AT)
                nc.gpsimd.tensor_tensor(wx[:, par], at(eg_all, n).unsqueeze(2).broadcast_to([128, H, R]),
                                        rb[:, par].unsqueeze(1).broadcast_to([128, H, R]),
                                        ALU.mult).then_inc(S["w_ready"], 1)
                pool.wait_ge(S["cb_ready"], n + 1)
                if not isinstance(n, int) or n >= 2:
                    pool.wait_ge(S["d1_ready"], n - 1)
                nc.gpsimd.tensor_tensor(cbr[:, par], cb[:], rb[:, par], ALU.mult).then_inc(S["cbr_ready"], 1)

            def own_weight(n, par):
                pool.wait_ge(S["d1_ready"], n + 1)
                if not isinstance(n, int) or n >= 2:
                    pool.wait_ge(S["ys_ready"], n - 1)
                nc.gpsimd.tensor_tensor(dg[:, par].rearrange("p (h e) -> p h e", e=P),
                                        d1[:].rearrange("p (h e) -> p h e", e=P),
                                        at(g_all, n).unsqueeze(2).broadcast_to([128, H, P]),
                                        ALU.mult).then_inc(S["dg_ready"], 1)

            def state(i, q):
                pool.wait_ge(S["p_added"], i + 1)
                pool.wait_ge(S["y_ps"], i + 1)
                nc.gpsimd.tensor_tensor(st[:, q].rearrange("p (h e) -> p h e", e=P),
                                        sp[:].rearrange("p (h e) -> p h e", e=P),
                                        at(f_all, i).unsqueeze(2).broadcast_to([128, H, P]),
                                        ALU.mult).then_inc(S["st_ready"], 1)

            def gated(i, par):
                pool.wait_ge(S["ys_ready"], i + 1)
                pool.wait_ge(S["z_silu"], i + 1)
                if not isinstance(i, int) or i >= 2:
                    pool.wait_ge(S["yt_ps"], i - 1)
                    pool.wait_ge(S["ysq_done"], i - 1)
                nc.gpsimd.tensor_tensor(y[:, par], ys[:], zs[:, par], ALU.mult).then_inc(S["y_ready"], 1)

            def factors(c):
                cols = slice(c * 2 * NQ, (c + 1) * 2 * NQ)
                nc.gpsimd.tensor_tensor(tokc[:, 7, cols], tokc[:, 6, cols], halfn[:, 0:2 * NQ],
                                        ALU.pow).then_inc(fac_p, 1)

            def step(i, q, general, ahead=3, chunk=None):
                par, other = q % 2, (q + 1) % 2
                last = ahead < 1
                if not last:
                    early(i + 1, other)
                if ahead >= 3:
                    lower_part(i + 3, other)
                if not general and carries(i):
                    state(i, q)
                if chunk is not None and chunk < NC_ // 2 - 1:
                    pool.wait_ge(fac_v, FAC_POW)
                    factors(chunk)
                if not last:
                    own_weight(i + 1, other)
                if last:
                    pool.wait_ge(C["mom"], MOM)
                    rstd2(0)
                gated(i, par)

            def rstd2(k):
                wait_past(pool, C["normed"], k * NQ)
                nc.gpsimd.tensor_tensor(frs[:, 0:NQ], fmo[:, 5, 0:NQ], halfn[:, 0:NQ], ALU.pow).then_inc(C["pow"], 1)

            def tiles(general):
                early(0, 0)
                lower_part(2, 0)
                own_weight(0, 0)
                for q in range(NQ):
                    step(q, q, general)
                with pool.Fori(1, NC_ - 1) as c:
                    for q in range(NQ):
                        step(c * NQ + q, q, general)
                for q in range(NQ):
                    step((NC_ - 1) * NQ + q, q, general, ahead=min(3, NQ - 1 - q), chunk=q)

            pool.wait_ge(prep, FLAG_AT)
            pool.wait_ge(s2, F_AT)
            fl = pool.value_load(flag_i[0:1, 0:1], min_val=0, max_val=1)
            with pool.If(fl > 0):
                tiles(False)
            with pool.Else():
                tiles(True)

            def residual(c):
                rows = bass.ds(c * NQ, NQ)
                pool.wait_ge(fac_p, c // 2 + 1 if isinstance(c, int) else NC_ // 2)
                nc.gpsimd.tensor_tensor(o_all[:, rows], o_all[:, rows],
                                        tokc[:, 7, rows].unsqueeze(2).broadcast_to([128, NQ, D]), ALU.mult)\
                    .then_inc(C["scaled_o"], 1)
                pool.wait_ge(C["scaled_o"], c - 1)
                nc.gpsimd.tensor_tensor(x_all[:, rows], o_all[:, rows], x_all[:, rows], ALU.add).then_inc(C["x1"], 1)

            def carry(k, par):
                wait_past(pool, C["r_ps"], k)
                nc.gpsimd.tensor_tensor(prevT[:, :, 0:1], curT[:, 1 - par, :, L - 1:L],
                                        one[:].unsqueeze(1).broadcast_to([128, B, 1]), ALU.mult).then_inc(C["carried"], 1)

            carry(0, 0)

            def chunk(k, par):
                if has(k, -2):
                    residual(k + 2)
                pool.wait_ge(C["mom"], (k + 2) * MOM)
                if has(k, 2):
                    wait_past(pool, C["res"], (k - 2) * NQ)
                    nc.gpsimd.tensor_tensor(frs[:, NQ:], fmo[:, 5, NQ:], halfn[:, 0:NQ], ALU.pow).then_inc(C["pow3"], 1)
                if has(k, -1):
                    rstd2(k + 1)
                if has(k) and not (isinstance(k, int) and k == 0):
                    carry(k, par)
                if isinstance(k, int) and k == 1:
                    pool.wait_ge(fac_v, 2 * FAC_POW)
                    factors(NC_ // 2 - 1)

            chunks(pool, chunk)

        @block.scalar
        def _(act):
            act.wait_ge(s_a, 32)
            nc.scalar.activation(negA[:], negA[:], ACT.Exp).then_inc(s2, 1)
            def copy_in(n, par):
                if not isinstance(n, int) or n >= 2:
                    act.wait_ge(S["x_ps"], n - 1)
                    act.wait_ge(S["zbc_ps"], n - 1)
                    act.wait_ge(S["x_lo"], n - 1)
                nc.scalar.activation(x_hi[:, par], at(xnT_all, n), ACT.Copy).then_inc(S["x_hi"], 1)

            def lam_theta(k, j):
                act.wait_ge(a_mm, k * 2 + j + 1)
                ps = bank[2 + j][:, 0:4 * NS].rearrange("p (t s) -> p t s", t=4)
                t = bass.ds(k * AK + 4 * j, 4)
                nc.scalar.activation(b_all[:, t], ps[:, :, H:2 * H], ACT.Tanh, scale=0.5).then_inc(a_sm, 1)
                nc.scalar.activation(th_all[:, t], ps[:, :, 2 * H:], ACT.Copy).then_inc(a_sm, 1)

            def exp_dt(k):
                act.wait_ge(a_dt, (k + 1) * 2)
                dt = dt_all[:, bass.ds(k * AK, AK)]
                nc.scalar.activation(dt, dt, ACT.Exp).then_inc(a_exp, 1)

            def first_phase(k):
                for j in range(2):
                    act.wait_ge(a_tr, k * 2 + j + 1)
                    wait_past(act, a_mm, k * 2 + j - 1)
                    wait_past(act, a_kept, k * 2 + j - 1)
                    nc.scalar.activation(xt8[:, 4 * j:4 * j + 4], bank[j][:], ACT.Copy).then_inc(a_ev, 1)
                def keep(j):
                    act.wait_ge(a_ev, k * 2 + j + 1)
                    nc.scalar.activation(xnT_all[:, bass.ds(k * AK + 4 * j, 4)], xt8[:, 4 * j:4 * j + 4],
                                         ACT.Copy).then_inc(a_kept, 1)

                keep(0)
                keep(1)
                if not (isinstance(k, int) and k == 0):
                    exp_dt(k - 1)
                lam_theta(k, 0)
                lam_theta(k, 1)

            steps(act, NT // AK, first_phase)
            copy_in(0, 0)
            copy_in(1, 1)
            exp_dt(NT // AK - 1)
            for j in range(2):
                act.wait_ge(v2, MIN_AT - 1 + j)
                dt = dt_all[:, 16 * j:16 * j + 16]
                nc.scalar.activation(dt, dt, ACT.Ln).then_inc(s2, 1)
            act.wait_ge(prep, FLAG_AT)
            nc.scalar.activation(halfpi[:, 1:2], halfpi[:, 0:1], ACT.Exp).then_inc(s_warm, 1)
            for j in range(2):
                act.wait_ge(p2, P_CUM[j])
                nc.scalar.activation(ec_all[:, 16 * j:16 * j + 16].rearrange("p t h -> p (t h)"), bank[4 + j][:],
                                     ACT.Exp, scale=flag[:, 0:1]).then_inc(s2, 1)
                nc.scalar.activation(eg_all[:, 16 * j:16 * j + 16].rearrange("p t h -> p (t h)"), bank[4 + j][:],
                                     ACT.Exp, scale=flag[:, 1:2]).then_inc(s2, 1)
            act.wait_ge(g2, B_AT)
            act.wait_ge(v2, DTSUM_AT)
            nc.scalar.activation(dt_all[:], la_all[:], ACT.Exp).then_inc(s2, 1)
            for j in range(2):
                w = 512 if j == 0 else 512 - NQ * H
                act.wait_ge(p2, P_LATE[j])
                nc.scalar.activation(flat(f_all)[:, 512 * j:512 * j + 512], bank[2 + j][:], ACT.Exp).then_inc(s2, 1)
                act.wait_ge(p2, P_EARLY[j])
                nc.scalar.activation(flat(r_all)[:, 512 * j:512 * j + w], bank[4 + j][:, 0:w],
                                     ACT.Exp).then_inc(s2, 1)
            act.wait_ge(s_warm, 1)
            nc.scalar.activation(halfpi[:, 1:2], halfpi[:, 0:1], ACT.Silu).then_inc(s2, 1)

            def cos_sin(j, slots=range(4)):
                t = slice(16 * j, 16 * j + 16)
                act.wait_ge(v2, ANG_AT[j])
                for slot in slots:
                    src, scale, bias = ((turns, -1.0, halfpi[:, 0:1]), (ang_in, -1.0, 0.0), (ang_in, 1.0, 0.0),
                                        (turns, -1.0, halfpi[:, 0:1]))[slot]
                    nc.scalar.activation(cs_all[:, t, slot * H:slot * H + H], src[:, t], ACT.Sin, scale=scale,
                                         bias=bias).then_inc(s2, 1)

            cos_sin(0)
            def squares(n, par):
                act.wait_ge(S["bc_ready"], n + 1)
                if not isinstance(n, int) or n >= 2:
                    act.wait_ge(S["rb_ready"], n - 1)
                act.wait_ge(S["sq_done"], n)
                for r in range(R):
                    nc.scalar.activation(junk[:, r * N:r * N + N], bank[0][:, r * N:r * N + N], ACT.Square,
                                         scale=float(N) ** -0.5, accum_out=msb[:, par, r:r + 1])
                nc.scalar.activation(junk[:, R * N:], bank[0][:, R * N:G3 * N], ACT.Square, scale=float(N) ** -0.5,
                                     accum_out=at(csq_all, n)).then_inc(S["sq_done"], 1)

            def x_gate(n, par):
                act.wait_ge(S["x_ps"], n + 1)
                if not isinstance(n, int) or n >= 2:
                    act.wait_ge(S["x1_ready"], n - 1)
                    act.wait_ge(S["d1_ready"], n - 1)
                nc.scalar.activation(xs[:, par], bank[1][:], ACT.Silu).then_inc(S["x_silu"], 1)

            def z_gate(n, par):
                act.wait_ge(S["zbc_ps"], n + 1)
                if not isinstance(n, int) or n >= 2:
                    act.wait_ge(S["y_ready"], n - 1)
                nc.scalar.activation(zs[:, par], bank[0][:, O_Z:O_Z + DI], ACT.Silu).then_inc(S["z_silu"], 1)

            def turned(n):
                act.wait_ge(S["t_ps"], n + 1)
                nc.scalar.activation(bt[:].rearrange("p g m -> p (g m)"), bank[2][:, 0:G3 * 128],
                                     ACT.Copy).then_inc(S["t_sb"], 1)

            def own_token(n, par):
                act.wait_ge(S["x_silu"], n + 1)
                act.wait_ge(S["cbr_ready"], n + 1)
                act.wait_ge(S["d1_ready"], n)
                nc.scalar.activation(d0[:].rearrange("p (h e) -> p h e", e=P),
                                     xs[:, par].rearrange("p (h r e) -> p r h e", r=R, e=P)[:, 0],
                                     ACT.Copy, scale=cbr[:, par, 0:1]).then_inc(S["d0_ready"], 1)

            def late_yt(i):
                act.wait_ge(S["yt_ps"], i + 1)
                act.wait_ge(S["o_ps"], i)
                nc.scalar.activation(yt[:].rearrange("p k m -> p (k m)"), bank[6][:, 0:DI], ACT.Copy).then_inc(S["yt_sb"], 1)

            def late_ysq(i, par):
                act.wait_ge(S["ysq_done"], i)
                act.wait_ge(S["y_ready"], i + 1)
                nc.scalar.activation(junk_y[:], y[:, par], ACT.Square, scale=float(DI) ** -0.5,
                                     accum_out=at(ysq_all, i)).then_inc(S["ysq_done"], 1)

            def late_o(i):
                act.wait_ge(S["o_ps"], i + 1)
                nc.scalar.activation(at(o_all, i), bank[7][:, 0:D], ACT.Copy).then_inc(S["o_sb"], 1)

            def step(i, q, ahead=3, behind=True):
                par, other = q % 2, (q + 1) % 2
                if ahead >= 1:
                    x_gate(i + 1, other)
                    squares(i + 1, other)
                    z_gate(i + 1, other)
                if ahead >= 3:
                    copy_in(i + 3, other)
                if behind:
                    late_yt(i - 1)
                if ahead >= 1:
                    turned(i + 1)
                    own_token(i + 1, other)
                if behind:
                    late_ysq(i - 1, other)
                    late_o(i - 1)

            act.wait_ge(S["st_zero"], 3)
            x_gate(0, 0)
            squares(0, 0)
            z_gate(0, 0)
            copy_in(2, 0)
            turned(0)
            own_token(0, 0)
            for q in range(NQ):
                step(q, q, behind=q > 0)
                cos_sin(1, [q])
            with act.Fori(1, NC_ - 1) as c:
                for q in range(NQ):
                    step(c * NQ + q, q)
            for q in range(NQ):
                step((NC_ - 1) * NQ + q, q, ahead=min(3, NQ - 1 - q))
            def normed(k, q):
                if q == 0:
                    act.wait_ge(C["norm_bias"], k + 1)
                    wait_past(act, C["tr_ps"], k)
                nc.scalar.activation(xn2[:, q], at(x_all, k * NQ + q), ACT.Identity, scale=frs[:, q:q + 1],
                                     bias=fnb[:, q:q + 1]).then_inc(C["normed"], 1)

            for q in range(NQ // 2):
                normed(0, q)
            late_yt(NT - 1)
            for q in range(NQ // 2, NQ):
                normed(0, q)
            late_ysq(NT - 1, (NT - 1) % 2)
            late_o(NT - 1)

            def chunk(k, par):
                if has(k, 1):
                    act.wait_ge(C["r_ps"], k)
                    wait_past(act, C["f"], (k - 1) * NQ)
                    nc.scalar.activation(th[:].rearrange("p q d -> p (q d)"), bank[2][:], ACT.Tanh,
                                         scale=0.5).then_inc(C["th"], 1)
                if has(k):
                    act.wait_ge(C["tr_ps"], k + 1)
                    wait_past(act, C["carried"], k)
                    turned_x = bank[0][:].rearrange("p (b l) -> p b l", b=B)
                    nc.scalar.activation(curT[:, par], turned_x, ACT.Copy).then_inc(C["tr_sb"], 1)
                    wait_past(act, C["r_ps"], k)
                    nc.scalar.activation(prevT[:, :, 1:], turned_x[:, :, 0:L - 1], ACT.Copy).then_inc(C["shifted"], 1)
                if has(k, 2):
                    act.wait_ge(C["bias3"], k - 1)
                    for q in range(NQ):
                        nc.scalar.activation(at(o_all, (k - 2) * NQ + q), f2[:, q], ACT.Identity,
                                             bias=fnb3[:, q:q + 1]).then_inc(C["outv"], 1)
                if has(k, -1):
                    for q in range(NQ // 2):
                        normed(k + 1, q)
                if has(k):
                    act.wait_ge(C["k_ps"], k + 1)
                    wait_past(act, C["k_act"], k)
                    nc.scalar.activation(kr[:], bank[1][:], ACT.Relu).then_inc(C["k_relu"], 1)
                if has(k, -1):
                    for q in range(NQ // 2, NQ):
                        normed(k + 1, q)
                if has(k):
                    act.wait_ge(C["k_relu"], k + 1)
                    wait_past(act, C["v_ps"], k)
                    nc.scalar.activation(ka[:], kr[:], ACT.Square).then_inc(C["k_act"], 1)

            chunks(act, chunk)

        @block.tensor
        def _(pe):
            pe.wait_ge(s_c, 16)
            pe.wait_ge(s_w, 16)
            def first_phase(k):
                for j in range(2):
                    wait_past(pe, a_ev, k * 2 + j - 1)
                    for t in range(4 * j, 4 * j + 4):
                        pe.wait_ge(a_xn, k * AK + t + 1)
                        mm = nc.tensor.transpose(bank[j][:, (t % 4) * 128:(t % 4) * 128 + 128], xn8[:, t], c_("ident"))
                    mm.then_inc(a_tr, 1)
                for j in range(2):
                    pe.wait_ge(a_ev, k * 2 + j + 1)
                    wait_past(pe, a_sm, (k * 2 + j - 1) * 2)
                    wait_past(pe, a_dt, k * 2 + j - 1)
                    for t in range(4 * j, 4 * j + 4):
                        mm = nc.tensor.matmul(bank[2 + j][:, (t % 4) * NS:(t % 4) * NS + NS], xt8[:, t], w_sb[:, O_S:],
                                              start=True, stop=True)
                    mm.then_inc(a_mm, 1)

            steps(pe, NT // AK, first_phase)
            parts = ((x_hi, w_hi), (x_hi, w_lo), (x_lo, w_hi))

            def project_bc(n, par):
                pe.wait_ge(S["x_hi"], n + 1)
                pe.wait_ge(S["x_lo"], n + 1)
                pe.wait_ge(S["z_silu"], n)
                for k, (a, b) in enumerate(parts):
                    mm = nc.tensor.matmul(bank[0][:, 0:O_X], a[:, par], b[:, 0:O_X], start=(k == 0), stop=(k == 2))
                mm.then_inc(S["zbc_ps"], 1)

            def project_x(n, par):
                pe.wait_ge(S["x_hi"], n + 1)
                pe.wait_ge(S["x_lo"], n + 1)
                pe.wait_ge(S["x_silu"], n)
                for k, (a, b) in enumerate(parts):
                    mm = nc.tensor.matmul(bank[1][:], a[:, par], b[:, O_X:O_S], start=(k == 0), stop=(k == 2))
                mm.then_inc(S["x_ps"], 1)

            pe.wait_ge(s_split, 2)
            pe.wait_ge(a_ev, 2 * NT // AK)
            project_x(0, 0)
            project_bc(0, 0)
            pe.wait_ge(s_c2, 16)
            lf = la_all[:].rearrange("p t h -> p (t h)")
            E = NQ * H
            for j in range(2):
                pe.wait_ge(v2, LA_AT - 1 + j)
                nc.tensor.matmul(bank[4 + j][:], c_("centre"), lf[:, 512 * j:512 * j + 512], start=True,
                                 stop=True).then_inc(p2, 1)
            pe.wait_ge(a_sm, 4 * NT // AK)
            pe.wait_ge(a_dt, 2 * NT // AK)
            mt, pre = flat(th_all), flat(pre3)

            def decay_after(j):
                nc.tensor.matmul(bank[2 + j][:], c_("late"), lf[:, 512 * j:512 * j + 512], start=True,
                                 stop=True).then_inc(p2, 1)

            def decay_next(j):
                w = 512 if j == 0 else 512 - E
                pe.wait_ge(s2, S_CUM - 2 + 2 * j)
                nc.tensor.matmul(bank[4 + j][:, 0:w], c_("early"), lf[:, 512 * j + E:512 * j + E + w], start=True,
                                 stop=True).then_inc(p2, 1)

            def angle_sums(j):
                pe.wait_ge(v2, MT_AT)
                nc.tensor.matmul(bank[6 + j][:], c_("tri"), mt[:, 512 * j:512 * j + 512], start=True, stop=False)
                pe.wait_ge(v2, PRE_AT - NC_ // 2 * (1 - j))
                nc.tensor.matmul(bank[6 + j][:], c_("ones"), pre[:, 512 * j:512 * j + 512], start=False,
                                 stop=True).then_inc(p2, 1)

            for j in range(2):
                decay_after(j)
                decay_next(j)
                angle_sums(j)
            def turn(n, par):
                pe.wait_ge(S["dup1"], n + 1)
                pe.wait_ge(S["t_sb"], n)
                for g in range(G3):
                    mm = nc.tensor.transpose(bank[2][:, g * 128:g * 128 + 128],
                                             dup[:, par, g].rearrange("p a n -> p (a n)"), c_("ident"))
                mm.then_inc(S["t_ps"], 1)

            def score(n):
                pe.wait_ge(S["t_sb"], n + 1)
                pe.wait_ge(S["sg_ready"], n)
                for r in range(R):
                    mm = nc.tensor.matmul(bank[3][:, r * 128:r * 128 + 128], bt[:, r], bt[:, R], start=True, stop=True)
                mm.then_inc(S["sg_ps"], 1)

            def rx(buf, r):
                return buf.rearrange("p (h r e) -> p r h e", r=R, e=P)[:, r]

            def mix(i, q, par):
                pe.wait_ge(S["x1_ready"], i + 1)
                if carries(i):
                    pe.wait_ge(S["p_added"], i)
                    for r in range(R):
                        mm = nc.tensor.matmul(bank[5][:, 0:DI], dup[:, par, r].rearrange("p a n -> p (a n)"),
                                              rx(x1[:, par], r), start=(r == 0), stop=(r == R - 1))
                    mm.then_inc(S["p_ps"], 1)
                if not isinstance(i, int) or i >= NQ:
                    pe.wait_ge(S["st_scaled"], i - NQ + 1)
                else:
                    pe.wait_ge(S["st_zero"], 3)
                pe.wait_ge(S["ya_ready"], i)
                nc.tensor.matmul(bank[4][:, 0:DI], bt[:, R], st[:, q], start=True, stop=False)
                pe.wait_ge(S["sg_ready"], i + 1)
                for r in range(R):
                    mm = nc.tensor.matmul(bank[4][:, 0:DI], sg[:, r], rx(x1[:, par], r), start=False, stop=(r == R - 1))
                mm.then_inc(S["y_ps"], 1)

            def mix_general(i, q, par):
                def token(t):
                    n = i * L + t
                    pe.wait_ge(G["oh"], n + 1)
                    wait_past(pe, G["fk_sb"], n)
                    nc.tensor.matmul(bank[3][:, 0:H], oh[:, 0], at(dt_all, i), start=True, stop=True).then_inc(G["fk_ps"], 1)
                    pe.wait_ge(S["t_sb"], i + 1)
                    pe.wait_ge(G["s1"], n + 1)
                    wait_past(pe, G["yk"], n)
                    nc.tensor.matmul(bank[4][:, 0:DI], bt[:, R], sk[:], start=True, stop=True).then_inc(G["y_ps"], 1)
                    pe.wait_ge(G["x1k"], n + 1)
                    wait_past(pe, G["st"], n)
                    for r in range(R):
                        mm = nc.tensor.matmul(bank[5][:, 0:DI], dup[:, par, r].rearrange("p a n -> p (a n)"),
                                              rx(xk[:, 0], r), start=(r == 0), stop=(r == R - 1))
                    mm.then_inc(G["p_ps"], 1)

                steps(pe, L, token, first=1 if isinstance(i, int) and i == 0 else 0)

            def y_turn(i, par):
                pe.wait_ge(S["y_ready"], i + 1)
                pe.wait_ge(S["yt_sb"], i)
                for k in range(2):
                    mm = nc.tensor.transpose(bank[6][:, k * 128:k * 128 + 128], y[:, par, k * 128:k * 128 + 128],
                                             c_("ident"))
                mm.then_inc(S["yt_ps"], 1)

            def y_out(i):
                pe.wait_ge(S["yt_sb"], i + 1)
                pe.wait_ge(S["o_sb"], i)
                for k in range(2):
                    mm = nc.tensor.matmul(bank[7][:, 0:D], yt[:, k], wo_sb[:, k], start=(k == 0), stop=(k == 1))
                mm.then_inc(S["o_ps"], 1)

            def step(i, q, general, first=False, ahead=2):
                par, other = q % 2, (q + 1) % 2
                last = ahead < 1
                if not last:
                    project_bc(i + 1, other)
                if general:
                    mix_general(i, q, par)
                else:
                    mix(i, q, par)
                if not first:
                    y_turn(i - 1, other)
                if not last:
                    turn(i + 1, other)
                if ahead >= 2:
                    project_x(i + 2, par)
                if not first:
                    y_out(i - 1)
                if not last and not general:
                    score(i + 1)

            def tiles(general):
                turn(0, 0)
                project_x(1, 1)
                if not general:
                    score(0)
                for q in range(NQ):
                    step(q, q, general, first=(q == 0))
                with pe.Fori(1, NC_ - 1) as c:
                    for q in range(NQ):
                        step(c * NQ + q, q, general)
                for q in range(NQ):
                    step((NC_ - 1) * NQ + q, q, general, ahead=min(2, NQ - 1 - q))
                y_turn(NT - 1, (NT - 1) % 2)
                y_out(NT - 1)

            pe.wait_ge(s_w2, 16 * 6)
            pe.wait_ge(s_split, 2)
            pe.wait_ge(prep, FLAG_AT)
            pe.wait_ge(s2, F_AT)
            fl = pe.value_load(flag_i[0:1, 0:1], min_val=0, max_val=1)
            with pe.If(fl > 0):
                tiles(False)
            with pe.Else():
                tiles(True)

            def chunk(k, par):
                if has(k):
                    wait_past(pe, C["shifted"], k)
                    for q in range(NQ):
                        pe.wait_ge(C["normed"], k * NQ + q + 1)
                        mm = nc.tensor.transpose(bank[0][:, q * 128:q * 128 + 128], xn2[:, q], c_("ident"))
                    mm.then_inc(C["tr_ps"], 1)
                if has(k, 1):
                    pe.wait_ge(C["k_act"], k)
                    wait_past(pe, C["f"], (k - 1) * NQ)
                    for q in range(NQ):
                        mm = nc.tensor.matmul(bank[3][:, q * D:q * D + D], ka[:, q * 128:q * 128 + 128], wv_half[:],
                                              start=True, stop=True)
                    mm.then_inc(C["v_ps"], 1)
                if not has(k):
                    return
                cur = curT[:, par].rearrange("p b l -> p (b l)")
                prev = prevT[:].rearrange("p b l -> p (b l)")
                pe.wait_ge(C["tr_sb"], k + 1)
                wait_past(pe, C["k_act"], k)
                nc.tensor.matmul(bank[1][:], w_cur[:, 0], cur, start=True, stop=False)
                pe.wait_ge(C["carried"], k + 1)
                pe.wait_ge(C["shifted"], k + 1)
                nc.tensor.matmul(bank[1][:], w_prev[:, 0], prev, start=False, stop=True).then_inc(C["k_ps"], 1)
                wait_past(pe, C["th"], k)
                for q in range(NQ):
                    nc.tensor.matmul(bank[2][:, q * D:q * D + D], cur[:, q * 128:q * 128 + 128], w_cur[:, 1],
                                     start=True, stop=False)
                    mm = nc.tensor.matmul(bank[2][:, q * D:q * D + D], prev[:, q * 128:q * 128 + 128], w_prev[:, 1],
                                          start=False, stop=True)
                mm.then_inc(C["r_ps"], 1)

            pe.wait_ge(s_mix, 6)
            chunks(pe, chunk)

        @block.vector
        def _(dve):
            vec = nc.vector
            def first_stats(k):
                dve.wait_ge(s_x[k], 64)
                for t in range(AK):
                    vec.bn_stats(bn8[:, k % 2, t], x_all[:, k * AK + t]).then_inc(a_st, 1)
                dve.wait_ge(a_st, (k + 1) * AK)
                moments(dve, bn8[:, k % 2], mo8[:, k % 2], AK, a_mo, k * MOM, EPS_LN)
                vec.tensor_scalar(mean8[:, k % 2], mo8[:, k % 2, 0, :], 0.5, None, ALU.mult).then_inc(a_me, 1)

            def biased_dt(k):
                for j in range(2):
                    t = slice(k * AK + 4 * j, k * AK + 4 * j + 4)
                    dve.wait_ge(a_sm, 2 * (k * 2 + j + 1))
                    vec.tensor_tensor(dt_all[:, t], bank[2 + j][:, 0:4 * NS].rearrange("p (t s) -> p t s", t=4)[:, :, 0:H],
                                      dtb_sb[:].unsqueeze(1).broadcast_to([128, 4, H]), ALU.add).then_inc(a_dt, 1)

            first_stats(0)
            dve.wait_ge(s_a, 32)
            for k in range(NT // AK):
                if k + 1 < NT // AK:
                    first_stats(k + 1)
                dve.wait_ge(a_me, k + 1)
                dve.wait_ge(a_rs, k + 1)
                if k >= 1:
                    dve.wait_ge(a_tr, k * 2)
                for t in range(AK):
                    vec.tensor_scalar(xn8[:, t], x_all[:, k * AK + t], mean8[:, k % 2, t:t + 1], rs8[:, k % 2, t:t + 1],
                                      ALU.subtract, ALU.mult).then_inc(a_xn, 1)
                if k >= 1:
                    biased_dt(k - 1)

            dve.wait_ge(s2, S_A)
            vec.tensor_reduce(flag[:, 2:3], negA[:], AX_X, ALU.max).then_inc(prep, 1)
            dve.wait_ge(prep, 1)
            vec.tensor_scalar(flag[:, 0:1], flag[:, 2:3], -1.0 if force_general else MAX_A, None, ALU.is_le)\
                .then_inc(prep, 1)
            dve.wait_ge(prep, 2)
            vec.tensor_scalar(flag[:, 1:2], flag[:, 0:1], -1.0, None, ALU.mult).then_inc(prep, 1)
            vec.tensor_copy(flag_i[:], flag[:, 0:1]).then_inc(prep, 1)
            vec.tensor_scalar(negA[:], negA[:], -1.0, None, ALU.mult).then_inc(prep, 1)
            vec.memset(halfpi[:, 0:1], float(np.pi / 2)).then_inc(prep, 1)

            dve.wait_ge(s_w2, 16 * 6)
            vec.tensor_scalar(one_less_mu[:], mu_sb[:], -1.0, 1.0, ALU.mult, ALU.add).then_inc(s_mix, 1)
            for n, (w_, m) in enumerate(((wk_sb, 1), (wr_sb, 0))):
                vec.tensor_scalar(w_cur[:, n], w_[:], mu_sb[:, m:m + 1], None, ALU.mult).then_inc(s_mix, 1)
            vec.tensor_scalar(wv_half[:], wv_sb[:], 0.5, None, ALU.mult).then_inc(s_mix, 1)
            dve.wait_ge(s_mix, 1)
            for n, (w_, m) in enumerate(((wk_sb, 1), (wr_sb, 0))):
                vec.tensor_scalar(w_prev[:, n], w_[:], one_less_mu[:, m:m + 1], None, ALU.mult).then_inc(s_mix, 1)

            chain = [0]

            def link(ins, value=None):
                chain[0] += 1
                ins.then_inc(v2, 1)
                assert value in (None, chain[0]), (value, chain[0])
                return chain[0]

            tiles_of = lambda j: slice(16 * j, 16 * j + 16)
            for j in range(2):
                if j == 1:
                    biased_dt(NT // AK - 1)
                dve.wait_ge(a_exp, 2 * j + 2)
                dt = dt_all[:, tiles_of(j)]
                link(vec.tensor_scalar(dt, dt, 1e9, 1.0, ALU.min, ALU.add), MIN_AT - 1 + j)
            dve.wait_ge(a_sm, 4 * NT // AK)
            link(vec.tensor_scalar(b_all[:], b_all[:], 0.5, 0.5, ALU.mult, ALU.add), SIG_AT)
            dve.wait_ge(v2, SIG_AT)
            for j in range(2):
                dve.wait_ge(s2, S_LN - 1 + j)
                dt = dt_all[:, tiles_of(j)]
                link(vec.tensor_scalar(dt, dt, 1e-4, 0.5, ALU.max, ALU.min), CLIP_AT - 1 + j)
            for j in range(2):
                dve.wait_ge(v2, CLIP_AT - 1 + j)
                link(vec.tensor_tensor(la_all[:, tiles_of(j)], dt_all[:, tiles_of(j)],
                                       negA[:].unsqueeze(1).broadcast_to([128, 16, H]), ALU.mult), LA_AT - 1 + j)
            link(vec.tensor_reduce(mdt[:], dt_all[:], AX_X, ALU.add))
            dve.wait_ge(v2, LA_AT + 1)
            link(vec.scalar_tensor_tensor(out=th_all[:], in0=th_all[:], scalar=1.0 / H,
                                          in1=mdt[:].unsqueeze(2).broadcast_to([128, NT, H]), op0=ALU.mult,
                                          op1=ALU.mult), MT_AT)
            link(vec.memset(pre3[:, 0:NQ], 0.0))
            for c in range(1, NC_):
                dve.wait_ge(v2, chain[0])
                n = link(vec.tensor_tensor(pre3[:, NQ * c:NQ * c + NQ], pre3[:, NQ * c - NQ:NQ * c],
                                           th_all[:, NQ * c - NQ:NQ * c], ALU.add))
            assert n == PRE_AT, n
            def whole_turns(j):
                cols = cols_of(j)
                tf, af = flat(turns)[:, cols], flat(ang)[:, cols]
                dve.wait_ge(p2, P_ANG[j])
                link(vec.tensor_scalar(tf, bank[6 + j][:], float(1 / (2 * np.pi)), MAGIC, ALU.mult, ALU.add))
                dve.wait_ge(v2, chain[0])
                link(vec.tensor_scalar(tf, tf, MAGIC, None, ALU.subtract))
                dve.wait_ge(v2, chain[0])
                link(vec.scalar_tensor_tensor(out=af, in0=tf, scalar=-TWO_PI_HI, in1=bank[6 + j][:], op0=ALU.mult,
                                              op1=ALU.add))

            def low_turns(j):
                tf, af = flat(turns)[:, cols_of(j)], flat(ang)[:, cols_of(j)]
                dve.wait_ge(v2, ANG_AT[j] - 3)
                vec.scalar_tensor_tensor(out=af, in0=tf, scalar=-TWO_PI_LO, in1=af, op0=ALU.mult, op1=ALU.add)\
                    .then_inc(v2, 1)

            def sine_angles(j):
                dve.wait_ge(v2, ANG_AT[j] - 2)
                vec.tensor_scalar(flat(ang_in)[:, cols_of(j)], flat(ang)[:, cols_of(j)], -PI_IN, PI_IN, ALU.max,
                                  ALU.min).then_inc(v2, 1)

            def cosine_angles(j):
                af = flat(ang)[:, cols_of(j)]
                vec.scalar_tensor_tensor(out=flat(turns)[:, cols_of(j)], in0=af, scalar=-1.0, in1=af, op0=ALU.mult,
                                         op1=ALU.max).then_inc(v2, 1)

            cols_of = lambda j: slice(512 * j, 512 * j + 512)
            whole_turns(0)
            low_turns(0)
            sine_angles(0)
            cosine_angles(0)
            chain[0] = ANG_AT[0]

            def token_weights():
                dve.wait_ge(s2, S_CUM)
                dve.wait_ge(g2, WSUM_AT)
                vec.tensor_tensor(eg_all[:], bnext[:], eg_all[:], ALU.mult).then_inc(v2, 1)

            def biased(n, par):
                dve.wait_ge(S["zbc_ps"], n + 1)
                if not isinstance(n, int) or n >= 2:
                    dve.wait_ge(S["prod_ready"], n - 1)
                vec.tensor_tensor(bc[:, par], bank[0][:, 0:G3 * N], bcb_sb[:], ALU.mult).then_inc(S["bc_ready"], 1)

            def rotations(n, par, general):
                dve.wait_ge(S["bc_ready"], n + 1)
                vec.tensor_tensor(rot[:], bc[:, par].rearrange("p (g a n) -> p g a n", g=G3, a=2).unsqueeze(3)
                                  .broadcast_to([128, G3, 2, 2, H]),
                                  at(cs_all, n).rearrange("p (a j n) -> p a j n", a=2, j=2).unsqueeze(1)
                                  .broadcast_to([128, G3, 2, 2, H]), ALU.mult).then_inc(S["rotated"], 1)
                dve.wait_ge(S["prod_ready"], n + 1)
                vec.tensor_reduce(cb[:], prod[:], AX_X, ALU.add).then_inc(S["cb_ready"], 1)
                dve.wait_ge(S["rotated"], n + 1)
                if not isinstance(n, int) or n >= 2:
                    if general:
                        dve.wait_ge(G["p_ps"], (n - 1) * L)
                    else:
                        dve.wait_ge(S["y_ps"], n - 1)
                for h in range(2):
                    rows = slice(64 * h, 64 * h + 64)
                    vec.tensor_tensor(dup[rows, par, :, h, :].rearrange("p g (j n) -> p g j n", j=2),
                                      rot[rows, :, 0], rot[rows, :, 1], ALU.add).then_inc(S[f"dup{h}"], 1)

            def weighted_x(n, par):
                dve.wait_ge(S["x_silu"], n + 1)
                dve.wait_ge(S["w_ready"], n + 1)
                vec.tensor_tensor(x1[:, par].rearrange("p (a e) -> p a e", e=P),
                                  xs[:, par].rearrange("p (a e) -> p a e", e=P),
                                  wx[:, par].rearrange("p h r -> p (h r)").unsqueeze(2).broadcast_to([128, H * R, P]),
                                  ALU.mult).then_inc(S["x1_ready"], 1)

            def own_token(n, par):
                dve.wait_ge(S["d0_ready"], n + 1)
                dve.wait_ge(S["dg_ready"], n)
                vec.scalar_tensor_tensor(out=d1[:].rearrange("p (h e) -> p h e", e=P),
                                         in0=xs[:, par].rearrange("p (h r e) -> p r h e", r=R, e=P)[:, 1],
                                         scalar=cbr[:, par, 1:2], in1=d0[:].rearrange("p (h e) -> p h e", e=P),
                                         op0=ALU.mult, op1=ALU.add).then_inc(S["d1_ready"], 1)

            def mask(n):
                dve.wait_ge(S["sg_ps"], n + 1)
                vec.tensor_tensor(sg[:], bank[3][:, 0:R * 128].rearrange("p (r m) -> p r m", r=R),
                                  c_("strict").unsqueeze(1).broadcast_to([128, R, 128]), ALU.mult)\
                    .then_inc(S["sg_ready"], 1)

            def state(i, q):
                dve.wait_ge(S["p_ps"], i + 1)
                dve.wait_ge(S["st_ready"], i)
                if not isinstance(i, int) or i >= NQ:
                    dve.wait_ge(S["st_scaled"], i - NQ + 1)
                vec.tensor_tensor(sp[:], bank[5][:, 0:DI], st[:, q], ALU.add).then_inc(S["p_added"], 1)

            def rescale(i, q):
                dve.wait_ge(S["st_ready"], i + 1)
                vec.tensor_tensor(st[:, q].rearrange("p (h e) -> p h e", e=P), st[:, q].rearrange("p (h e) -> p h e", e=P),
                                  at(r_all, i).unsqueeze(2).broadcast_to([128, H, P]), ALU.mult)\
                    .then_inc(S["st_scaled"], 1)

            def scaled_y(i):
                dve.wait_ge(S["y_ps"], i + 1)
                vec.tensor_tensor(ya[:].rearrange("p (h e) -> p h e", e=P),
                                  bank[4][:, 0:DI].rearrange("p (h e) -> p h e", e=P),
                                  at(ec_all, i).unsqueeze(2).broadcast_to([128, H, P]), ALU.mult)\
                    .then_inc(S["ya_ready"], 1)

            def summed_y(i, par, general):
                if not general:
                    dve.wait_ge(S["ya_ready"], i + 1)
                dve.wait_ge(S["dg_ready"], i + 1)
                dve.wait_ge(S["y_ready"], i)
                vec.tensor_tensor(ys[:], (yk if general else ya)[:], dg[:, par], ALU.add).then_inc(S["ys_ready"], 1)

            def tokens_general(i, q, par):
                dve.wait_ge(S["ys_ready"], i)
                dve.wait_ge(S["x1_ready"], i + 1)
                vec.memset(yk[:], 0.0).then_inc(G["zero"], 1)
                def token(t):
                    n = i * L + t
                    hot = cm[:, CONSTS.index("hot"), bass.ds(t, 1) if not isinstance(t, int) else slice(t, t + 1)]
                    wait_past(dve, G["fk_ps"], n)
                    vec.tensor_scalar(oh[:, 0], c_("ones"), hot, None, ALU.mult).then_inc(G["oh"], 1)
                    wait_past(dve, G["p_ps"], n)
                    vec.tensor_scalar(xk[:, 0], x1[:, par], hot, None, ALU.mult).then_inc(G["x1k"], 1)
                    dve.wait_ge(G["fk_ps"], n + 1)
                    vec.tensor_copy(fk[:], bank[3][:, 0:H]).then_inc(G["fk_sb"], 1)
                    dve.wait_ge(G["fk_sb"], n + 1)
                    wait_past(dve, G["st"], n)
                    wait_past(dve, G["y_ps"], n)
                    vec.tensor_tensor(sk[:].rearrange("p (h e) -> p h e", e=P), st[:, q].rearrange("p (h e) -> p h e", e=P),
                                      fk[:].unsqueeze(2).broadcast_to([128, H, P]), ALU.mult).then_inc(G["s1"], 1)
                    dve.wait_ge(G["y_ps"], n + 1)
                    wait_past(dve, G["yk"], n)
                    dve.wait_ge(G["zero"], i + 1)
                    vec.scalar_tensor_tensor(out=yk[:], in0=bank[4][:, 0:DI], scalar=hot, in1=yk[:], op0=ALU.mult,
                                             op1=ALU.add).then_inc(G["yk"], 1)
                    dve.wait_ge(G["p_ps"], n + 1)
                    dve.wait_ge(G["s1"], n + 1)
                    vec.tensor_tensor(st[:, q], bank[5][:, 0:DI], sk[:], ALU.add).then_inc(G["st"], 1)

                steps(dve, L, token, first=1 if isinstance(i, int) and i == 0 else 0)
                dve.wait_ge(G["yk"], (i + 1) * L)

            def stats(i):
                vec.bn_stats(at(ost_all, i), at(o_all, i)).then_inc(S["ost_done"], 1)

            def factor_terms(t, base):
                moments(dve, ost_all, tokc, t, fac_v, base, 0.0)
                dve.wait_ge(fac_v, base + MOM)
                vec.scalar_tensor_tensor(out=tokc[:, 1, t], in0=ysq_all[:, t, 0], scalar=EPS_LN, in1=tokc[:, 5, t],
                                         op0=ALU.mult, op1=ALU.add).then_inc(fac_v, 1)
                vec.tensor_scalar(tokc[:, 2, t], csq_all[:, t, 0], EPS_RMS, EPS_LN * EPS_RMS * SCALE2_INV, ALU.add,
                                  ALU.mult).then_inc(fac_v, 1)
                dve.wait_ge(fac_v, base + MOM + 2)
                vec.tensor_tensor(tokc[:, 6, t], tokc[:, 1, t], tokc[:, 2, t], ALU.add).then_inc(fac_v, 1)

            def residual(k):
                dve.wait_ge(fac_p, k // 2 + 1)
                for q in range(NQ):
                    i = k * NQ + q
                    mm = vec.scalar_tensor_tensor(out=x_all[:, i], in0=o_all[:, i], scalar=tokc[:, 7, i:i + 1],
                                                  in1=x_all[:, i], op0=ALU.mult, op1=ALU.add)
                mm.then_inc(C["x1_first"], 1)

            def stats2(k):
                for q in range(NQ):
                    vec.bn_stats(fst[:, q], at(x_all, k * NQ + q)).then_inc(C["stats"], 1)

            def moments2(k):
                wait_past(dve, C["norm_bias"], min(k + 1, NC_) if isinstance(k, int) else k + 1)
                wait_past(dve, C["norm_bias3"], k - 2)
                if has(k, -1):
                    dve.wait_ge(C["stats"], (k + 2) * NQ)
                if has(k, 2):
                    dve.wait_ge(C["stats3"], (k - 1) * NQ)
                moments(dve, fst, fmo, norms(k), C["mom"], (k + 1) * MOM, EPS_LN)

            def norm_bias(k):
                dve.wait_ge(C["pow"], k + 1)
                wait_past(dve, C["normed"], k * NQ)
                vec.scalar_tensor_tensor(out=fnb[:, 0:NQ], in0=fmo[:, 0, 0:NQ], scalar=-0.5, in1=frs[:, 0:NQ],
                                         op0=ALU.mult, op1=ALU.mult).then_inc(C["norm_bias"], 1)

            def step(i, q, general, first=False, last=False):
                par, other = q % 2, (q + 1) % 2
                if general:
                    tokens_general(i, q, par)
                if not first:
                    dve.wait_ge(S["o_sb"], i - 1)
                if not last:
                    biased(i + 1, other)
                if not first:
                    stats(i - 2)
                if not last:
                    rotations(i + 1, other, general)
                if not general and carries(i):
                    state(i, q)
                if not general and (not isinstance(i, int) or 0 < i <= NT - NQ):
                    rescale(i - 1, (q - 1) % NQ)
                if isinstance(i, int) and i == NT - NQ:
                    dve.wait_ge(S["ost_done"], NT - 2 * NQ)
                    dve.wait_ge(S["ysq_done"], NT - 2 * NQ)
                    factor_terms(slice(0, NT - 2 * NQ), 0)
                if isinstance(i, int) and i == NT - 3:
                    residual(0)
                if isinstance(i, int) and i == NT - 2:
                    dve.wait_ge(C["x1_first"], 1)
                    stats2(0)
                if last:
                    dve.wait_ge(C["stats"], NQ)
                    moments(dve, fst, fmo, NQ, C["mom"], 0, EPS_LN)
                if not last:
                    weighted_x(i + 1, other)
                if not general:
                    scaled_y(i)
                if not last:
                    own_token(i + 1, other)
                summed_y(i, par, general)
                if not last and not general:
                    mask(i + 1)
                if last:
                    norm_bias(0)
                    residual(1)
                    dve.wait_ge(C["x1_first"], 2)
                    stats2(1)

            biased(0, 0)
            whole_turns(1)

            def tiles(general):
                dve.wait_ge(s2, TABLES_AT - 4)
                rotations(0, 0, general)
                token_weights()
                weighted_x(0, 0)
                low_turns(1)
                own_token(0, 0)
                sine_angles(1)
                if not general:
                    mask(0)
                cosine_angles(1)
                for q in range(NQ):
                    step(q, q, general, first=(q < 2))
                dve.wait_ge(s2, TABLES_AT)
                with dve.Fori(1, NC_ - 1) as c:
                    for q in range(NQ):
                        step(c * NQ + q, q, general)
                for q in range(NQ):
                    step((NC_ - 1) * NQ + q, q, general, last=(q == NQ - 1))

            dve.wait_ge(s_w2, 16 * 6)
            dve.wait_ge(S["st_zero"], 3)
            fl = dve.value_load(flag_i[0:1, 0:1], min_val=0, max_val=1)
            with dve.If(fl > 0):
                tiles(False)
            with dve.Else():
                tiles(True)

            def chunk(k, par):
                c = k - 2
                moments2(k)
                if isinstance(k, int) and k == 1:
                    dve.wait_ge(S["o_sb"], NT)
                    stats(NT - 2)
                    stats(NT - 1)
                    dve.wait_ge(S["ost_done"], NT)
                    dve.wait_ge(S["ysq_done"], NT)
                    factor_terms(slice(NT - 2 * NQ, NT), FAC_POW)
                if has(k, -2):
                    dve.wait_ge(C["x1"], k + 1)
                    stats2(k + 2)
                if has(k, 2):
                    vec.scalar_tensor_tensor(out=mean_o[:], in0=tokc[:, 0, bass.ds(c * NQ, NQ)], scalar=-0.5,
                                             in1=tokc[:, 7, bass.ds(c * NQ, NQ)], op0=ALU.mult, op1=ALU.mult)\
                        .then_inc(C["means"], 1)
                if has(k, 2):
                    dve.wait_ge(C["pow3"], c + 1)
                    wait_past(dve, C["bias3"], c)
                    vec.scalar_tensor_tensor(out=fnb[:, NQ:], in0=fmo[:, 0, NQ:], scalar=-0.5, in1=frs[:, NQ:],
                                             op0=ALU.mult, op1=ALU.mult).then_inc(C["norm_bias3"], 1)
                    wait_past(dve, C["outv"], c * NQ)
                    for q in range(NQ):
                        vec.scalar_tensor_tensor(out=f2[:, q], in0=ff[:, q], scalar=frs[:, NQ + q:NQ + q + 1],
                                                 in1=at(x_all, c * NQ + q), op0=ALU.mult, op1=ALU.add)\
                            .then_inc(C["res"], 1)
                    dve.wait_ge(C["norm_bias3"], c + 1)
                    dve.wait_ge(C["means"], c + 1)
                    vec.tensor_tensor(fnb3[:], fnb[:, NQ:], mean_o[:], ALU.add).then_inc(C["bias3"], 1)
                if has(k, -1):
                    norm_bias(k + 1)
                if has(k, 1):
                    dve.wait_ge(C["th"], k)
                    dve.wait_ge(C["v_ps"], k)
                    if has(k, 2):
                        dve.wait_ge(C["res"], (c + 1) * NQ)
                    for q in range(NQ):
                        vec.scalar_tensor_tensor(out=ff[:, q], in0=th[:, q], scalar=1.0, in1=bank[3][:, q * D:q * D + D],
                                                 op0=ALU.add, op1=ALU.mult).then_inc(C["f"], 1)
                    for q in range(NQ):
                        dve.wait_ge(C["f"], (k - 1) * NQ + q + 1)
                        vec.bn_stats(fst[:, NQ + q], ff[:, q]).then_inc(C["stats3"], 1)

            chunks(dve, chunk)


def kernel(L0_attn_x, L0_attn_W_in, L0_attn_A_log, L0_attn_dt_bias, L0_attn_B_norm_bias, L0_attn_C_norm_bias,
           L0_attn_W_out, L0_ffn_W_r, L0_ffn_W_k, L0_ffn_W_v, L0_ffn_mu_r, L0_ffn_mu_k):
    import concourse.bacc as bacc
    from concourse.bass_utils import run_bass_kernel_spmd

    w = np.asarray(L0_attn_W_in)
    z, xr, bcw, rest = w[:, :DI], w[:, DI:DI + DI * R], w[:, DI * (1 + R):DI * (1 + R) + G3 * N], w[:, -NS:]
    bb, cb = np.asarray(L0_attn_B_norm_bias).reshape(-1), np.asarray(L0_attn_C_norm_bias).reshape(-1)
    arrays = {
        "x": np.asarray(L0_attn_x),
        "w_in": np.concatenate([bcw, z, xr, rest], axis=1),
        "a_log": np.asarray(L0_attn_A_log),
        "dt_bias": np.asarray(L0_attn_dt_bias),
        "bc_bias": np.concatenate([bb, bb, cb]),
        "w_out": np.asarray(L0_attn_W_out),
        "w_r": np.asarray(L0_ffn_W_r).T,
        "w_k": np.asarray(L0_ffn_W_k).T,
        "w_v": np.asarray(L0_ffn_W_v).T,
        "mu": np.stack([np.asarray(L0_ffn_mu_r), np.asarray(L0_ffn_mu_k)], axis=1),
        "consts": constants(),
    }
    arrays = {n: np.ascontiguousarray(a) for n, a in arrays.items()}
    nc = bacc.Bacc("TRN2", target_bir_lowering=False, num_devices=1)
    args = [nc.dram_tensor(n, a.shape, mybir.dt.from_np(a.dtype), kind="ExternalInput").ap() for n, a in arrays.items()]
    out = nc.dram_tensor("out", (B, T, D), F32, kind="ExternalOutput").ap()
    build(nc, *args, out)
    r = run_bass_kernel_spmd(nc, [arrays], core_ids=[0])
    return r.results[0]["out"]
```
